# Optimizing a Trainium2 kernel written in Bass

```python
import numpy as np
import jax
import jax.numpy as jnp

def _softmax(x, axis=-1):
    return jax.nn.softmax(x, axis=axis)

def _gelu(x):
    return jax.nn.gelu(x, approximate=True)

def _silu(x):
    return jax.nn.silu(x)

def _sigmoid(x):
    return jax.nn.sigmoid(x)

def _layernorm(x, axis=-1, eps=1e-05):
    m = jnp.mean(x, axis=axis, keepdims=True)
    v = jnp.var(x, axis=axis, keepdims=True)
    return (x - m) / jnp.sqrt(v + eps)

def _scatter_add(tgt, idx, src, axis=0):
    return tgt.at[idx].add(src)

def _segment_sum(src, seg, n):
    return jax.ops.segment_sum(src, seg, n)
kernel_name = 'mk_gnn_ffn_d2_gnn_r16_f55009'

def setup_inputs(seed: int=0):
    np.random.seed(seed)
    _w = jnp.asarray

    def _rec_inputs():
        import jax
        import jax.numpy as jnp
        _gk = jax.random.key(seed)
        x = -0.0002117 + 1 * jax.random.normal(jax.random.fold_in(_gk, 1), (3125, 256), jnp.float32)
        src = jax.random.randint(jax.random.fold_in(_gk, 2), (100000,), 0, 3125, jnp.int32)
        dst = jax.random.randint(jax.random.fold_in(_gk, 3), (100000,), 0, 3125, jnp.int32)
        _o = jnp.argsort(dst, stable=True)
        src = src[_o]
        dst = dst[_o]
        edge_attr_32 = 0.000398968 + 1.00027 * jax.random.normal(jax.random.fold_in(_gk, 11), (100000, 32), jnp.float32)
        edge_type_3 = jax.random.randint(jax.random.fold_in(_gk, 13), (100000,), 0, 3, jnp.int32)
        return (x, src, dst, edge_attr_32, edge_type_3)
    x, src, dst, edge_attr_32, edge_type_3 = _rec_inputs()

    def _L0_gnn_setup():
        import jax, jax.numpy as jnp
        import numpy as np
        N_NODES = 6250
        N_EDGES = 200000
        D_IN = 256
        D_OUT = 256
        LEAKY_SLOPE = 0.01
        key = jax.random.key(seed)
        ks = jax.random.split(key, 8)
        s_in = 1.0 / np.sqrt(D_IN)
        s_out = 1.0 / np.sqrt(D_OUT)
        return {'features': jax.random.normal(ks[0], (N_NODES, D_IN), dtype=jnp.float32), 'indices': jax.random.randint(ks[1], (2, N_EDGES), 0, N_NODES, dtype=jnp.int64), 'W_layer': jax.random.uniform(ks[2], (D_OUT, D_IN), jnp.float32, -s_in, s_in), 'b_layer': jax.random.uniform(ks[3], (D_OUT,), jnp.float32, -s_in, s_in), 'w_a1': jax.random.uniform(ks[4], (1, D_OUT), jnp.float32, -s_out, s_out), 'b_a1': jax.random.uniform(ks[5], (1,), jnp.float32, -s_out, s_out), 'w_a2': jax.random.uniform(ks[6], (1, D_OUT), jnp.float32, -s_out, s_out), 'b_a2': jax.random.uniform(ks[7], (1,), jnp.float32, -s_out, s_out)}
    _L0_gnn_all = _L0_gnn_setup()
    _L0_gnn_in = {k: v for k, v in _L0_gnn_all.items() if k in ('W_layer', 'b_layer', 'w_a1', 'b_a1', 'w_a2', 'b_a2')}
    del _L0_gnn_all

    def _L0_ffn_setup():
        import jax, jax.numpy as jnp
        import numpy as np
        B, S, D = (8, 256, 256)
        H = 4 * D
        CAPACITY = 0.5
        key = jax.random.key(seed)
        ks = jax.random.split(key, 6)
        x = jax.random.normal(ks[0], (B, S, D), dtype=jnp.float32)
        attention_mask = jnp.zeros((B, 1, 1, S), dtype=jnp.float32)
        wr = jax.random.normal(ks[1], (D, 1), dtype=jnp.float32) * 0.02
        br = jnp.zeros((1,), dtype=jnp.float32)
        w1 = jax.random.normal(ks[2], (D, H), dtype=jnp.float32) * 0.02
        b1 = jnp.zeros((H,), dtype=jnp.float32)
        w2 = jax.random.normal(ks[3], (H, D), dtype=jnp.float32) * 0.02
        b2 = jnp.zeros((D,), dtype=jnp.float32)
        return {'x': x, 'attention_mask': attention_mask, 'wr': wr, 'br': br, 'w1': w1, 'b1': b1, 'w2': w2, 'b2': b2}
    _L0_ffn_all = _L0_ffn_setup()
    _L0_ffn_in = {k: v for k, v in _L0_ffn_all.items() if k in ('attention_mask', 'wr', 'br', 'w1', 'b1', 'w2', 'b2')}
    del _L0_ffn_all

    def _L1_gnn_setup():
        import jax, jax.numpy as jnp
        import numpy as np
        N_NODES = 625
        N_EDGES = 10000
        D = 256
        NUM_REL = 3
        NUM_DISTS = 32
        N_LAYERS = 3

        def _gcn_forward(x, edge_index, edge_type, edge_attr, weights, roots, biases, edge_w, edge_b):
            n = x.shape[0]
            src, dst = (edge_index[0], edge_index[1])
            ew = edge_attr @ edge_w + edge_b
            rel_masks = [(edge_type == i).astype(x.dtype) for i in range(NUM_REL)]
            inv_cnt = [1.0 / jnp.maximum(jax.ops.segment_sum(m, dst, num_segments=n), 1.0) for m in rel_masks]
            for l in range(N_LAYERS):
                residual = x
                msg = jax.nn.relu(x[src] * ew)
                out = jnp.zeros((n, D), dtype=x.dtype)
                for i in range(NUM_REL):
                    h = jax.ops.segment_sum(msg * rel_masks[i][:, None], dst, num_segments=n)
                    h = h * inv_cnt[i][:, None]
                    out = out + h @ weights[l, i]
                out = out + x @ roots[l] + biases[l]
                x = residual + jax.nn.relu(out)
            return x
        key = jax.random.key(seed)
        ks = jax.random.split(key, 12)
        s = 1.0 / np.sqrt(D)
        inp = {'x': jax.random.normal(ks[0], (N_NODES, D), dtype=jnp.float32), 'edge_index': jax.random.randint(ks[1], (2, N_EDGES), 0, N_NODES, dtype=jnp.int32), 'edge_type': jax.random.randint(ks[2], (N_EDGES,), 0, NUM_REL, dtype=jnp.int32), 'edge_attr': jax.random.normal(ks[3], (N_EDGES, NUM_DISTS), dtype=jnp.float32), 'weights': jax.random.normal(ks[4], (N_LAYERS, NUM_REL, D, D), dtype=jnp.float32) * s, 'roots': jax.random.normal(ks[5], (N_LAYERS, D, D), dtype=jnp.float32) * s, 'biases': jax.random.normal(ks[6], (N_LAYERS, D), dtype=jnp.float32) * 0.01, 'edge_w': jax.random.normal(ks[7], (NUM_DISTS, D), dtype=jnp.float32) * (1.0 / np.sqrt(NUM_DISTS)), 'edge_b': jax.random.normal(ks[8], (D,), dtype=jnp.float32) * 0.01}
        return inp
    _L1_gnn_all = _L1_gnn_setup()
    _L1_gnn_in = {k: v for k, v in _L1_gnn_all.items() if k in ('weights', 'roots', 'biases', 'edge_w', 'edge_b')}
    del _L1_gnn_all

    def _L1_ffn_setup():
        import math
        import jax, jax.numpy as jnp
        import numpy as np
        CAPACITY_FACTOR = 1.25
        TOP_K = 2
        LN_EPS = 1e-05

        def _layer_norm(x, gamma, beta):
            mu = jnp.mean(x, axis=-1, keepdims=True)
            var = jnp.var(x, axis=-1, keepdims=True)
            return (x - mu) * jax.lax.rsqrt(var + LN_EPS) * gamma + beta
        key = jax.random.key(seed)
        ks = jax.random.split(key, 4)
        B, S, D, F, E = (8, 256, 256, 512, 8)
        x = jax.random.normal(ks[0], (B, S, D), dtype=jnp.float32)
        Wr = jax.random.normal(ks[1], (D, E), dtype=jnp.float32) / np.sqrt(D)
        br = jnp.zeros((E,), jnp.float32)
        W1 = jax.random.normal(ks[2], (E, D, F), dtype=jnp.float32) / np.sqrt(D)
        b1 = jnp.zeros((E, F), jnp.float32)
        W2 = jax.random.normal(ks[3], (E, F, D), dtype=jnp.float32) / np.sqrt(F)
        b2 = jnp.zeros((E, D), jnp.float32)
        gamma = jnp.ones((D,), jnp.float32)
        beta = jnp.zeros((D,), jnp.float32)
        return {'x': x, 'Wr': Wr, 'br': br, 'W1': W1, 'b1': b1, 'W2': W2, 'b2': b2, 'gamma': gamma, 'beta': beta}
    _L1_ffn_all = _L1_ffn_setup()
    _L1_ffn_in = {k: v for k, v in _L1_ffn_all.items() if k in ('Wr', 'br', 'W1', 'b1', 'W2', 'b2', 'gamma', 'beta')}
    del _L1_ffn_all
    return {'x': x, 'src': src, 'dst': dst, 'edge_attr_32': edge_attr_32, 'edge_type_3': edge_type_3, 'L0_gnn_W_layer': _L0_gnn_in['W_layer'], 'L0_gnn_b_layer': _L0_gnn_in['b_layer'], 'L0_gnn_w_a1': _L0_gnn_in['w_a1'], 'L0_gnn_b_a1': _L0_gnn_in['b_a1'], 'L0_gnn_w_a2': _L0_gnn_in['w_a2'], 'L0_gnn_b_a2': _L0_gnn_in['b_a2'], 'L0_ffn_attention_mask': _L0_ffn_in['attention_mask'], 'L0_ffn_wr': _L0_ffn_in['wr'], 'L0_ffn_br': _L0_ffn_in['br'], 'L0_ffn_w1': _L0_ffn_in['w1'], 'L0_ffn_b1': _L0_ffn_in['b1'], 'L0_ffn_w2': _L0_ffn_in['w2'], 'L0_ffn_b2': _L0_ffn_in['b2'], 'L1_gnn_weights': _L1_gnn_in['weights'], 'L1_gnn_roots': _L1_gnn_in['roots'], 'L1_gnn_biases': _L1_gnn_in['biases'], 'L1_gnn_edge_w': _L1_gnn_in['edge_w'], 'L1_gnn_edge_b': _L1_gnn_in['edge_b'], 'L1_ffn_Wr': _L1_ffn_in['Wr'], 'L1_ffn_br': _L1_ffn_in['br'], 'L1_ffn_W1': _L1_ffn_in['W1'], 'L1_ffn_b1': _L1_ffn_in['b1'], 'L1_ffn_W2': _L1_ffn_in['W2'], 'L1_ffn_b2': _L1_ffn_in['b2'], 'L1_ffn_gamma': _L1_ffn_in['gamma'], 'L1_ffn_beta': _L1_ffn_in['beta']}

def reference(x, src, dst, edge_attr_32, edge_type_3, L0_gnn_W_layer, L0_gnn_b_layer, L0_gnn_w_a1, L0_gnn_b_a1, L0_gnn_w_a2, L0_gnn_b_a2, L0_ffn_attention_mask, L0_ffn_wr, L0_ffn_br, L0_ffn_w1, L0_ffn_b1, L0_ffn_w2, L0_ffn_b2, L1_gnn_weights, L1_gnn_roots, L1_gnn_biases, L1_gnn_edge_w, L1_gnn_edge_b, L1_ffn_Wr, L1_ffn_br, L1_ffn_W1, L1_ffn_b1, L1_ffn_W2, L1_ffn_b2, L1_ffn_gamma, L1_ffn_beta):
    import jax
    import jax.numpy as jnp

    def _L0_gnn_ref(features, indices, W_layer, b_layer, w_a1, b_a1, w_a2, b_a2):
        import jax, jax.numpy as jnp
        import numpy as np
        N_NODES = 6250
        N_EDGES = 200000
        D_IN = 256
        D_OUT = 256
        LEAKY_SLOPE = 0.01
        n = features.shape[0]
        h = features @ W_layer.T + b_layer
        a1 = (h @ w_a1.T + b_a1)[:, 0]
        a2 = (h @ w_a2.T + b_a2)[:, 0]
        row = indices[0]
        col = indices[1]
        v = jax.nn.leaky_relu(a1[row] + a2[col], negative_slope=LEAKY_SLOPE)
        m = jax.ops.segment_max(v, row, num_segments=n)
        ev = jnp.exp(v - m[row])
        s = jax.ops.segment_sum(ev, row, num_segments=n)
        att = ev / s[row]
        out = jax.ops.segment_sum(att[:, None] * h[col], row, num_segments=n)
        return out

    def _L0_ffn_ref(x, attention_mask, wr, br, w1, b1, w2, b2):
        import jax, jax.numpy as jnp
        import numpy as np
        B, S, D = (8, 256, 256)
        H = 4 * D
        CAPACITY = 0.5
        b, s, d = x.shape
        weights = (jnp.einsum('bsd,do->bso', x, wr) + br)[..., 0]
        k = max(1, int(CAPACITY * s))
        kk = k - 1 if k > 1 else 1
        _, idx = jax.lax.top_k(weights, k)
        sel_idx = idx[:, :kk]
        sel = jnp.take_along_axis(x, sel_idx[:, :, None], axis=1)
        h = jax.nn.gelu(jnp.einsum('bkd,dh->bkh', sel, w1) + b1)
        y = jnp.einsum('bkh,hd->bkd', h, w2) + b2
        w_sel = jnp.take_along_axis(weights, sel_idx, axis=1)
        y = y * w_sel[..., None]
        batch_idx = jnp.arange(b)[:, None]
        processed = jnp.zeros_like(x).at[batch_idx, sel_idx].set(y)
        return processed + x

    def _L1_gnn_ref(x, edge_index, edge_type, edge_attr, weights, roots, biases, edge_w, edge_b):
        import jax, jax.numpy as jnp
        import numpy as np
        N_NODES = 625
        N_EDGES = 10000
        D = 256
        NUM_REL = 3
        NUM_DISTS = 32
        N_LAYERS = 3

        def _gcn_forward(x, edge_index, edge_type, edge_attr, weights, roots, biases, edge_w, edge_b):
            n = x.shape[0]
            src, dst = (edge_index[0], edge_index[1])
            ew = edge_attr @ edge_w + edge_b
            rel_masks = [(edge_type == i).astype(x.dtype) for i in range(NUM_REL)]
            inv_cnt = [1.0 / jnp.maximum(jax.ops.segment_sum(m, dst, num_segments=n), 1.0) for m in rel_masks]
            for l in range(N_LAYERS):
                residual = x
                msg = jax.nn.relu(x[src] * ew)
                out = jnp.zeros((n, D), dtype=x.dtype)
                for i in range(NUM_REL):
                    h = jax.ops.segment_sum(msg * rel_masks[i][:, None], dst, num_segments=n)
                    h = h * inv_cnt[i][:, None]
                    out = out + h @ weights[l, i]
                out = out + x @ roots[l] + biases[l]
                x = residual + jax.nn.relu(out)
            return x
        return _gcn_forward(x, edge_index, edge_type, edge_attr, weights, roots, biases, edge_w, edge_b)

    def _L1_ffn_ref(x, Wr, br, W1, b1, W2, b2, gamma, beta):
        import math
        import jax, jax.numpy as jnp
        import numpy as np
        CAPACITY_FACTOR = 1.25
        TOP_K = 2
        LN_EPS = 1e-05

        def _layer_norm(x, gamma, beta):
            mu = jnp.mean(x, axis=-1, keepdims=True)
            var = jnp.var(x, axis=-1, keepdims=True)
            return (x - mu) * jax.lax.rsqrt(var + LN_EPS) * gamma + beta
        B, S, D = x.shape
        E = Wr.shape[1]
        N = B * S
        K = TOP_K
        logits = jnp.mean(x, axis=1) @ Wr + br
        routing_weights = jax.nn.softmax(logits, axis=-1)
        capacity = float(math.ceil(N * CAPACITY_FACTOR / E))
        expected_loads = routing_weights.sum(axis=0) * (N / B)
        scale = jnp.where(expected_loads > capacity, capacity / expected_loads, 1.0)
        routing_weights = jax.nn.softmax(routing_weights * scale, axis=-1)
        rw_tok = jnp.broadcast_to(routing_weights[:, None, :], (B, S, E)).reshape(N, E)
        top_w, top_i = jax.lax.top_k(rw_tok, K)
        top_w = jax.nn.softmax(top_w, axis=-1)
        xf = x.reshape(N, D)
        h = jax.nn.gelu(jnp.einsum('nd,edf->enf', xf, W1) + b1[:, None, :], approximate=False)
        y = jnp.einsum('enf,efd->end', h, W2) + b2[:, None, :]
        w_dense = jnp.zeros((N, E), x.dtype).at[jnp.arange(N)[:, None], top_i].add(top_w)
        out = jnp.einsum('ne,end->nd', w_dense, y).reshape(B, S, D)
        out = _layer_norm(out + x, gamma, beta)
        return out
    edge_index = jnp.stack([src, dst])
    x = x + _L0_gnn_ref(_layernorm(x, axis=-1), edge_index, L0_gnn_W_layer, L0_gnn_b_layer, L0_gnn_w_a1, L0_gnn_b_a1, L0_gnn_w_a2, L0_gnn_b_a2)
    x = x + _L0_ffn_ref(_layernorm(x, axis=-1)[None], L0_ffn_attention_mask, L0_ffn_wr, L0_ffn_br, L0_ffn_w1, L0_ffn_b1, L0_ffn_w2, L0_ffn_b2)[0]
    x = x + _L1_gnn_ref(_layernorm(x, axis=-1), edge_index, edge_type_3, edge_attr_32, L1_gnn_weights, L1_gnn_roots, L1_gnn_biases, L1_gnn_edge_w, L1_gnn_edge_b)
    x = x + _L1_ffn_ref(_layernorm(x, axis=-1)[None], L1_ffn_Wr, L1_ffn_br, L1_ffn_W1, L1_ffn_b1, L1_ffn_W2, L1_ffn_b2, L1_ffn_gamma, L1_ffn_beta)[0]
    return x

_drawn_inputs = setup_inputs


def setup_inputs(seed=0):
    import zlib

    import numpy as np

    out = dict(_drawn_inputs(seed))
    spreads = {'L0_ffn_b1': (0.0, 0.8),
     'L0_ffn_b2': (0.0, 0.762),
     'L1_ffn_br': (0.0, 0.1),
     'L1_ffn_b1': (0.0, 0.8),
     'L1_ffn_b2': (0.0, 0.656),
     'L1_ffn_gamma': (1.0, 0.2),
     'L1_ffn_beta': (0.0, 0.411)}
    factors = {'L0_gnn_w_a1': 16.032,
     'L0_ffn_wr': 4.121,
     'L0_ffn_w1': 4.863,
     'L0_ffn_w2': 4.581,
     'L1_gnn_biases': 8.0,
     'L1_gnn_edge_b': 26.048}
    for name, (base, spread) in spreads.items():
        noise = np.random.default_rng([zlib.crc32(name.encode()), seed]).standard_normal(out[name].shape)
        drawn = base * np.exp(spread * noise) if base else spread * noise
        out[name] = jnp.asarray(drawn.astype(out[name].dtype))
    for name, factor in factors.items():
        out[name] = (out[name] * factor).astype(out[name].dtype)
    return out
```

```python
import math
from contextlib import ExitStack

import concourse.bass as bass
from concourse import mybir

FP32 = mybir.dt.float32
BF16 = mybir.dt.bfloat16
INT32 = mybir.dt.int32
ALU = mybir.AluOpType
ACT = mybir.ActivationFunctionType
X_AXIS = mybir.AxisListType.X
ds = bass.ds

P = 128
N = 3125
D = 256
NT = -(-N // P)
NP_ = NT * P
LAST = N - (NT - 1) * P
E = 100000
EP, EC = 125, 800
R = 3
F_ATTR = 32
LAYERS = 3
EPS = 1e-5
TOPK = max(1, int(0.5 * N)) - 1
NE, FE = 8, 512
HID = 1024
BKT_A, BKT_B = NT, R * NT


def slots_tiles(buckets):
    return -(-((E + buckets * (P - 1)) // P) // 8) * 8


TA, TB = slots_tiles(BKT_A), slots_tiles(BKT_B)
QB = TB // 4
RW = 64
W_SRC, W_SEG = 50, 51
KA = 3 * F_ATTR + 3
HC = D + 2
AC = D + 1


def build(nc, t, out):
    ctx = ExitStack()
    with ctx:
        def sb(name, shape, dt=FP32):
            return ctx.enter_context(nc.sbuf_tensor(name, shape, dt))[:]

        sems = {}

        def S(name):
            if name not in sems:
                sems[name] = ctx.enter_context(nc.semaphore(name))
            return sems[name]

        def dram(name, shape, dt=FP32):
            return nc.dram_tensor(name, shape, dt, kind="Internal").ap()

        def due(value):
            return not isinstance(value, int) or value > 0

        class Steps:

            def __init__(self, eng, name):
                self.eng, self.name, self.n = eng, name, 0

            def did(self, ins):
                ins.then_inc(S(self.name), 1)
                self.n += 1

            def settle(self):
                self.eng.wait_ge(S(self.name), self.n)

            def run(self, ins):
                self.did(ins)
                self.settle()

        def looped(eng, n, body):
            body(0)
            with eng.Fori(1, n - 1) as i:
                body(i)
            body(n - 1)

        x_sb = sb("x_sb", [P, NT, D])
        xn_mem = sb("xn_mem", [P, NT * D])
        xn = xn_mem.rearrange("p (t d) -> p t d", d=D)
        xt_mem = sb("xt_mem", [P, NT * HC])
        acc_mem = sb("acc_mem", [P, (BKT_B + 1) * AC])
        acc = acc_mem.rearrange("p (w c) -> p w c", c=AC)
        sort_mem = sb("sort_mem", [P, 7 * EC])
        keyA, keyB = (sort_mem[:EP, k * EC // 2:(k + 1) * EC // 2].bitcast(BF16) for k in range(2))
        itemA, itemB = (sort_mem[:EP, (1 + 2 * k) * EC:(3 + 2 * k) * EC].rearrange("p (e c) -> p e c", c=2) for k in range(2))
        addrA, addrB = (sort_mem[:EP, (5 + k) * EC:(6 + k) * EC].bitcast(INT32) for k in range(2))
        winpA, winpB = sb("winpA", [1, TA // 2], INT32), sb("winpB", [1, TB // 2], INT32)
        z_mem = sb("z_mem", [P, 5500])

        def z(lo, n, dt=FP32):
            assert lo + n <= 5500
            v = z_mem[:, lo:lo + n]
            return v if dt == FP32 else v.bitcast(dt)

        iota = sb("iota", [P, P])
        iota_col = sb("iota_col", [P, 1])
        iota_b = sb("iota_b", [P, P], BF16)
        ident = sb("ident", [P, P])
        ident_b = sb("ident_b", [P, P], BF16)
        tri_b = sb("tri_b", [P, P], BF16)
        tri = sb("tri", [P, P])
        ones = sb("ones", [P, P])
        ones_b = sb("ones_b", [P, 1], BF16)
        vecs = sb("vecs", [P, 4, D])
        small = sb("small", [P, 512])

        raw = [acc_mem[:EP, k * EC:(k + 1) * EC].bitcast(INT32) for k in range(5)]
        src_i, dst_i, rel_i, hi_i, lo_i = raw
        o = 5 * EC
        cnt = acc_mem[:, o:o + EC]; o += EC
        cum = acc_mem[:, o:o + EC]; o += EC
        zeros = acc_mem[:, o:o + EC]; o += EC
        base_sb = acc_mem[:, o:o + 8 * BKT_B]; o += 8 * BKT_B
        slotf = acc_mem[:EP, o:o + EC]; o += EC
        iotaT = acc_mem[:, o:o + TB]; o += TB
        winge = acc_mem[:, o:o + TB]; o += TB
        winbc = acc_mem[:, o:o + TB]; o += TB
        fill = acc_mem[:, o:o + 512]; o += 512
        GC = {0: 10, 1: 5}
        kring = [acc_mem[:EP, o + k * 192:o + (k + 1) * 192].bitcast(BF16) for k in range(4)]; o += 4 * 192
        baser = [acc_mem[0:1, o + k * 768:o + k * 768 + 768] for k in range(2)]; o += 2 * 768
        prod = [acc_mem[:EP, o + k * 384:o + (k + 1) * 384] for k in range(2)]; o += 2 * 384
        slotg = acc_mem[:EP, o:o + 40]; o += 40
        assert o <= (BKT_B + 1) * AC, o

        bank = [ctx.enter_context(nc.psum_tensor(f"bank{k}", [P, 512], FP32))[:] for k in range(8)]

        o = 0
        recA = xn_mem[:, o:o + 2 * TA].rearrange("p (t c) -> p t c", c=2); o += 2 * TA
        vmax = xn_mem[:, o:o + TA]; o += TA
        winA = xn_mem[:, o:o + TA]; o += TA
        tbl = xn_mem[:, o:o + 3 * TA].bitcast(BF16).rearrange("p (t c s) -> p t c s", c=2, s=3); o += 3 * TA
        assert o <= NT * D
        htab = xt_mem[:, 0:NT * HC].rearrange("p (t c) -> p t c", c=HC)

        stA_i = z(0, 8, INT32)[:EP].rearrange("p (h k) -> p h k", h=2)
        stA = z(8, 16)[:EP].rearrange("p (h k c) -> p h k c", h=2, c=2)

        wl = z(32, 2 * D).rearrange("p (k d) -> p k d", k=2)
        xtr = z(544, 2 * D).rearrange("p (h c) -> p h c", h=2)
        dots = z(1056, 5 * D).rearrange("p (t d) -> p t d", d=D)
        hrow = z(32, 8 * HC).rearrange("p (h k c) -> p h k c", h=2, k=4)
        vsel = z(2112, 1024).rearrange("p (h k s) -> p h k s", h=2, k=4)
        oneb = z(3136, 512, BF16).rearrange("p (h k s) -> p h k s", h=2, k=4)
        onet = z(3648, 512, BF16).rearrange("p (h k s) -> p h k s", h=2, k=4)
        gidx = z(4160, 8, INT32).rearrange("p (h k) -> p h k", h=2)
        gseg = z(4168, 8).rearrange("p (h k) -> p h k", h=2)
        amv = z(4176, 64).rearrange("p (h n) -> p h n", h=2)
        attr_in = z(4240, 256)[:EP].rearrange("p (h k f) -> p h k f", h=2, k=4)
        attr_r = z(4496, 128)[:EP].rearrange("p (k f) -> p k f", k=4)
        stB = z(4624, 8 * RW)[:EP].rearrange("p (h k w) -> p h k w", h=2, k=4)
        stB_i = z(5136, 8, INT32)[:EP].rearrange("p (h k) -> p h k", h=2)
        stBb = z(4624, 8 * RW, BF16)[:EP].rearrange("p (h k w) -> p h k w", h=2, k=4)
        stBi = z(4624, 8 * RW, INT32)[:EP].rearrange("p (h k w) -> p h k w", h=2, k=4)
        o = (BKT_A + 1) * AC
        ta1 = acc_mem[:, o:o + TA]; o += TA
        tm = acc_mem[:, o:o + TA]; o += TA
        tx = acc_mem[:, o:o + TA]; o += TA
        ty = acc_mem[:, o:o + TA]; o += TA
        a1 = small[:, 330:355]
        a2 = small[:, 355:380]
        mx = small[:, 380:405]
        mrow = small[:, 405:430]
        gmin = small[:, 430:432]
        ssum = small[:, 432:457]
        stats = small[:, 64:214].rearrange("p (t c) -> p t c", c=6)
        mv = small[:, 214:264].rearrange("p (t c) -> p t c", c=2)
        sd = small[:, 264:289]
        rs = small[:, 289:314]

        w_row = acc_mem[:, 0:NP_]
        o = NP_
        w1_sb = acc_mem[:, o:o + 2 * HID].rearrange("p (k f) -> p k f", k=2); o += 2 * HID
        w2_sb = acc_mem[:, o:o + 8 * D].rearrange("p (j d) -> p j d", d=D); o += 8 * D
        hid_sb = acc_mem[:, o:o + 2 * 8 * 512].rearrange("p (h j n) -> p h j n", h=2, j=8); o += 2 * 8 * 512
        seen = acc_mem[:, o:o + NP_ // 2].bitcast(BF16); o += NP_ // 2
        ycol = acc_mem[:, o:o + 2 * D].rearrange("p (h d) -> p h d", h=2); o += 2 * D
        assert o <= (BKT_B + 1) * AC
        xt = xt_mem[:, 0:2 * NP_].rearrange("p (k n) -> p k n", k=2)
        tok_w = small[:, 330:355]
        n_gt = small[:, 355:430].rearrange("p (c t) -> p c t", c=3)
        coef = small[:, 432:457]
        real = small[:, 457:458]
        b1_sb = small[:, 460:468]
        br_sb = small[:, 468:469]
        low = z(0, P)
        w_turn = z(P, P)
        lw = xt_mem[:, 0:LAYERS * 8 * D].rearrange("p (l m d) -> p l m d", l=LAYERS, m=8)
        rec = z(0, 8 * RW).rearrange("p (h k w) -> p h k w", h=2, k=4)
        recb = z(0, 8 * RW, BF16).rearrange("p (h k w) -> p h k w", h=2, k=4)
        reci = z(0, 8 * RW, INT32).rearrange("p (h k w) -> p h k w", h=2, k=4)
        at = z(512, 512, BF16).rearrange("p (h n) -> p h n", h=2)
        oneh = z(1024, 1024).rearrange("p (h k s) -> p h k s", h=2, k=4)
        msg = z(2048, 8 * AC).rearrange("p (h k c) -> p h k c", h=2, k=4)
        we = z(4104, 3 * 128, BF16).rearrange("p (m d) -> p m d", m=3)
        we_f = z(4488, D)
        we_r = z(4744, D)
        xg = sort_mem[:, 0:8 * D].rearrange("p (h k d) -> p h k d", h=2, k=4)
        turned = sort_mem[:, 0:8 * D].rearrange("p (h n) -> p h n", h=2)
        flat = sort_mem[:, 8 * D:16 * D].rearrange("p (h m d) -> p h m d", h=2, m=4)
        inv = small[:, 320:395]
        gate = small[:, 0:64]
        wr_sb = small[:, 470:486].rearrange("p (k e) -> p k e", k=2)

        recA_d = dram("recA_d", [P * TA, 2])
        recB_d = dram("recB_d", [P * TB, RW])
        h_d = dram("h_d", [NP_, HC])
        pay_d = dram("pay_d", [P, TA * HC])
        x_d = dram("x_d", [NP_, D])
        tok_d = dram("tok_d", [1, NP_])
        baseA_d, baseB_d = dram("baseA_d", [EC, BKT_A]), dram("baseB_d", [EC, BKT_B])
        SORT = [dict(nb=BKT_A, T=TA, key=keyA, base_d=baseA_d, addr=addrA, winp=winpA, n=0),
                dict(nb=BKT_B, T=TB, key=keyB, base_d=baseB_d, addr=addrB, winp=winpB, n=1)]
        for s, cols in zip(SORT, (10, 5)):
            s["cols"] = cols
            s["bodies"] = EC // (4 * cols)

        block = ctx.enter_context(nc.Block())

        @block.sync
        def _(sp):
            for dst, name in ((src_i, "src"), (dst_i, "dst"), (rel_i, "edge_type_3")):
                sp.dma_start(dst, t[name].rearrange("(p c) -> p c", c=EC)).then_inc(S("ids_loaded"), 16)
            x_rows = t["x"][0:(NT - 1) * P, :].rearrange("(t p) d -> p t d", p=P)
            sp.wait_ge(S("x_zeroed"), 1)
            sp.dma_start(x_sb[:, 0:NT - 1, :], x_rows).then_inc(S("x_loaded"), 16)
            sp.dma_start(x_sb[0:LAST, NT - 1, :], t["x"][(NT - 1) * P:N, :]).then_inc(S("x_loaded"), 16)
            sp.dma_start(wl, t["W_layer_t"].rearrange("(k p) d -> p k d", p=P)).then_inc(S("att_w_loaded"), 16)
            for k, name in enumerate(("L0_gnn_b_layer", "L0_gnn_w_a1", "L0_gnn_w_a2")):
                sp.dma_start(vecs[:, k, :], t[name].rearrange("(a d) -> a d", a=1).broadcast_to([P, D]))\
                    .then_inc(S("att_w_loaded"), 16)
            for k, name in enumerate(("L0_gnn_b_a1", "L0_gnn_b_a2")):
                sp.dma_start(small[:, 320 + k:321 + k], t[name].rearrange("(a d) -> a d", a=1).broadcast_to([P, 1]))\
                    .then_inc(S("att_w_loaded"), 16)
            sp.wait_ge(S("fill_ready"), 1)
            sp.dma_start(recA_d.rearrange("(p t) c -> p t c", p=P),
                         xn_mem[:, 0:2 * TA].rearrange("p (t c) -> p t c", c=2)).then_inc(S("filled0"), 16)
            fb = fill.rearrange("p (a c) -> p a c", a=1).broadcast_to([P, TB // 8, 512])
            sp.dma_start(recB_d.rearrange("(p q t) c -> p q (t c)", p=P, t=8), fb).then_inc(S("filled1"), 16)

            def rank_io(s):
                nb, cols, n_ = s["nb"], s["cols"], s["n"]
                sp.wait_ge(S("base_ready"), n_ * 1 + 1)
                sp.dma_start(s["base_d"].rearrange("(k j) b -> j k b", j=100),
                             base_sb[:100, :8 * nb].rearrange("j (k b) -> j k b", b=nb)).then_inc(S("base_stored"), 16)
                sp.wait_ge(S("base_stored"), n_ * 16 + 16)
                rows = s["base_d"].rearrange("(a j) b -> a (j b)", j=2 * cols)

                def body(i):
                    for h in range(2):
                        if due(i * 4 + 2 * h - 2):
                            sp.wait_ge(S("rank_summed"), n_ * 80 + i * 4 + 2 * h - 2)
                        sp.dma_start(baser[h][:, :2 * cols * nb], rows[ds(2 * i + h, 1), :]).then_inc(S(f"row{h}"), 16)
                looped(sp, s["bodies"], body)
            rank_io(SORT[0])
            rank_io(SORT[1])
            sp.wait_ge(S("htab_ready"), 1)
            sp.dma_start(h_d.rearrange("(t p) c -> p t c", p=P), htab).then_inc(S("h_stored"), 16)
            for h in range(2):
                sp.wait_ge(S(f"scattered{h}"), EC // 8 * 64)
            sp.dma_start(recA, recA_d.rearrange("(p t) c -> p t c", p=P)).then_inc(S("recA_loaded"), 16)

            def keep(i):
                for h in range(2):
                    sp.wait_ge(S(f"gathered{h}"), i * 64 + 64)
                    sp.dma_start(pay_d[:, ds((2 * i + h) * 4 * HC, 4 * HC)],
                                 hrow[:, h, :, :].rearrange("p k c -> p (k c)")).then_inc(S(f"kept{h}"), 16)
            looped(sp, TA // 8, keep)
            for h in range(2):
                sp.wait_ge(S(f"kept{h}"), TA // 8 * 16)
            sp.wait_ge(S("v_ready"), TA // 4)
            attr = t["edge_attr_32"].rearrange("(p e) f -> p (e f)", e=EC)

            def feed(i):
                for h in range(2):
                    Q = 2 * i + h
                    if not (isinstance(i, int) and i == TA // 8 - 1):
                        if due(Q - 1):
                            sp.wait_ge(S("attr_split"), Q - 1)
                        sp.dma_start(attr_in[:, h, :, :].rearrange("p k f -> p (k f)"),
                                     attr[:, ds(Q * 4 * F_ATTR, 4 * F_ATTR)]).then_inc(S(f"attr_loaded{h}"), 16)
                    if due((Q - 1) * 4):
                        sp.wait_ge(S("att_summed"), (Q - 1) * 4)
                    sp.dma_start(hrow[:, h, :, :].rearrange("p k c -> p (k c)"),
                                 pay_d[:, ds(Q * 4 * HC, 4 * HC)]).then_inc(S(f"pay_loaded{h}"), 16)
            looped(sp, TA // 8, feed)
            sp.wait_ge(S("x1_ready"), 1)
            sp.dma_start(w1_sb, t["L0_ffn_w1"].rearrange("(k p) f -> p k f", p=P)).then_inc(S("mod_w_loaded"), 16)
            sp.dma_start(w2_sb, t["L0_ffn_w2"].rearrange("(j p) d -> p j d", p=P)).then_inc(S("mod_w_loaded"), 16)
            sp.dma_start(b1_sb, t["b1_mod"]).then_inc(S("mod_w_loaded"), 16)
            sp.dma_start(vecs[:, 0, :], t["wr_mod"].rearrange("(a d) -> a d", a=1).broadcast_to([P, D]))\
                .then_inc(S("mod_v_loaded"), 16)
            sp.dma_start(vecs[:, 1, :], t["L0_ffn_b2"].rearrange("(a d) -> a d", a=1).broadcast_to([P, D]))\
                .then_inc(S("mod_v_loaded"), 16)
            sp.dma_start(br_sb, t["L0_ffn_br"].rearrange("(a d) -> a d", a=1).broadcast_to([P, 1]))\
                .then_inc(S("mod_v_loaded"), 16)
            sp.wait_ge(S("router_turned"), 1)
            sp.dma_start(tok_d.rearrange("a (t p) -> (a t) p", p=P), w_turn[:NT, :]).then_inc(S("router_stored"), 16)
            sp.wait_ge(S("router_stored"), 16)
            sp.dma_start(w_row, tok_d.broadcast_to([P, NP_])).then_inc(S("router_row"), 16)
            sp.wait_ge(S("x2_ready"), 1)
            for h in range(2):
                sp.wait_ge(S(f"scattered{h}"), EC * 8 + EC // 8 * 64)
            for l in range(LAYERS):
                for r in range(R):
                    sp.dma_start(lw[:, l, 2 * r:2 * r + 2, :], t["L1_gnn_weights"][l, r].rearrange("(k p) d -> p k d", p=P))\
                        .then_inc(S("layer_w_loaded"), 16)
                sp.dma_start(lw[:, l, 6:8, :], t["L1_gnn_roots"][l].rearrange("(k p) d -> p k d", p=P))\
                    .then_inc(S("layer_w_loaded"), 16)
            sp.dma_start(vecs[0:1, 0:LAYERS, :], t["L1_gnn_biases"].rearrange("(a l) d -> a l d", a=1))\
                .then_inc(S("layer_w_loaded"), 16)
            for k in range(3):
                sp.dma_start(we_f[32 * k:32 * k + 32, :], t["L1_gnn_edge_w"]).then_inc(S("edge_w_loaded"), 16)
            sp.dma_start(we_f[96:99, :], t["L1_gnn_edge_b"].rearrange("(a d) -> a d", a=1).broadcast_to([3, D]))\
                .then_inc(S("edge_w_loaded"), 16)
            recs = recB_d.rearrange("(p t) w -> p (t w)", p=P)
            for l in range(LAYERS):
                sp.wait_ge(S("state_ready"), l + 1)
                sp.dma_start(x_d.rearrange("(t p) d -> p t d", p=P), xn).then_inc(S("state_stored"), 16)
                if l == 0:
                    sp.wait_ge(S("edge_w_ready"), 1)

                def feed(i):
                    for h in range(2):
                        Q = 2 * i + h
                        if due(Q - 1):
                            sp.wait_ge(S("rec_turned"), l * QB + Q - 1)
                        sp.sem_inc(S("passed"), 1)
                        if due(i * 64):
                            sp.wait_ge(S(f"sources{h}"), l * TB * 8 + i * 64)
                        if due(Q - 1):
                            sp.wait_ge(S("seg_ready"), l * QB + Q - 1)
                        sp.dma_start(rec[:, h, :, :].rearrange("p k w -> p (k w)"),
                                     recs[:, ds(Q * 4 * RW, 4 * RW)]).then_inc(S(f"rec_loaded{h}"), 16)
                looped(sp, TB // 8, feed)
            sp.wait_ge(S("x3_ready"), 1)
            sp.dma_start(wr_sb, t["L1_ffn_Wr"].rearrange("(k p) e -> p k e", p=P)).then_inc(S("gate_w_loaded"), 16)
            sp.dma_start(gate[0:1, 0:8], t["L1_ffn_br"].rearrange("(a e) -> a e", a=1)).then_inc(S("gate_w_loaded"), 16)
            for k, name in ((2, "L1_ffn_gamma"), (3, "L1_ffn_beta")):
                sp.dma_start(vecs[:, k, :], t[name].rearrange("(a d) -> a d", a=1).broadcast_to([P, D]))\
                    .then_inc(S("norm_w_loaded"), 16)
            sp.wait_ge(S("chosen"), 1)
            for c in range(2):
                e = sp.value_load(gate[0:1, 62 + c:63 + c].bitcast(INT32), min_val=0, max_val=NE - 1)
                sp.dma_start(w1_sb[:, :, c * FE:(c + 1) * FE],
                             t["L1_ffn_W1"][ds(e, 1), :, :].rearrange("e (k p) f -> p (e k) f", p=P)).then_inc(S("moe_w_loaded"), 16)
                sp.dma_start(w2_sb[:, 4 * c:4 * c + 4, :],
                             t["L1_ffn_W2"][ds(e, 1), :, :].rearrange("e (j p) d -> p (e j) d", p=P)).then_inc(S("moe_w_loaded"), 16)
                sp.dma_start(b1_sb[:, 4 * c:4 * c + 4],
                             t["b1_moe"][ds(e, 1), :, :].rearrange("e p j -> p (e j)")).then_inc(S("moe_w_loaded"), 16)
                sp.dma_start(vecs[:, c, :], t["L1_ffn_b2"][ds(e, 1), :].broadcast_to([P, D])).then_inc(S("moe_w_loaded"), 16)
            sp.wait_ge(S("out_ready"), 1)
            sp.dma_start(out[0:(NT - 1) * P, :].rearrange("(t p) d -> p t d", p=P), x_sb[:, 0:NT - 1, :]).then_inc(S("out_stored"), 16)
            sp.dma_start(out[(NT - 1) * P:N, :], x_sb[0:LAST, NT - 1, :]).then_inc(S("out_stored"), 16)
            sp.wait_ge(S("out_stored"), 32)
            sp.wait_ge(S("x_loaded"), 32)
            sp.wait_ge(S("layer_w_loaded"), 16 * 13)

        @block.gpsimd
        def _(pool):
            g = nc.gpsimd
            g.memset(x_sb[:, NT - 1, :], 0.0).then_inc(S("x_zeroed"), 1)
            g.memset(fill, 0.0).then_inc(S("p_const"), 1)
            g.memset(xn_mem[:, 0:2 * TA], 0.0).then_inc(S("p_const"), 1)
            g.iota(iota, pattern=[[1, P]], base=0, channel_multiplier=0,
                   allow_small_or_imprecise_dtypes=True).then_inc(S("p_const"), 1)
            g.iota(iota_b, pattern=[[1, P]], base=0, channel_multiplier=0,
                   allow_small_or_imprecise_dtypes=True).then_inc(S("p_const"), 1)
            g.iota(iota_col, pattern=[[1, 1]], base=0, channel_multiplier=1,
                   allow_small_or_imprecise_dtypes=True).then_inc(S("p_const"), 1)
            g.iota(iotaT, pattern=[[1, TB]], base=0, channel_multiplier=0,
                   allow_small_or_imprecise_dtypes=True).then_inc(S("p_const"), 1)
            g.memset(ones, 1.0).then_inc(S("p_const"), 1)
            g.memset(ones_b, 1.0).then_inc(S("p_const"), 1)
            g.memset(zeros, 0.0).then_inc(S("p_const"), 1)
            pool.wait_ge(S("p_const"), 9)
            g.memset(fill.rearrange("p (t c) -> p t c", c=RW)[:, :, W_SEG:W_SEG + 1], -1.0).then_inc(S("p_const"), 1)
            g.memset(xn_mem[:, 0:2 * TA].rearrange("p (t c) -> p t c", c=2)[:, :, 1:2], -1.0).then_inc(S("p_const"), 1)
            pool.wait_ge(S("p_const"), 11)
            pool.sem_inc(S("fill_ready"), 1)

            def scatter(s, item_words, rec_d, stage):
                n_ = s["n"]
                pool.wait_ge(S(f"filled{n_}"), 16)

                def body(i):
                    for h in range(2):
                        pool.wait_ge(S("staged"), n_ * (EC // 4) + 2 * i + h + 1)
                        pool.sem_inc(S("passed_pool"), 1)
                        for k in range(4):
                            idx, item = stage(h, k)
                            pool.indirect_dma_start(
                                out=rec_d, out_offset=bass.IndirectOffsetOnAxis(ap=idx, axis=0),
                                in_=item, in_offset=None).then_inc(S(f"scattered{h}"), 16)
                looped(pool, EC // 8, body)
            scatter(SORT[0], 2, recA_d, lambda h, k: (stA_i[:, h, k:k + 1], stA[:, h, k, :]))
            pool.wait_ge(S("gmin_part"), 1)
            g.partition_all_reduce(gmin[:, 1:2], gmin[:, 0:1], P, bass.bass_isa.ReduceOp.max).then_inc(S("gmin_all"), 1)

            def gather_h(i):
                for h in range(2):
                    if due(i * 16):
                        pool.wait_ge(S(f"kept{h}"), i * 16)
                    if due(2 * i + h - 1):
                        pool.wait_ge(S("v_ready"), 2 * i + h - 1)
                    pool.wait_ge(S("gidx_staged"), 2 * i + h + 1)
                    pool.sem_inc(S("passed_pool"), 1)
                    for k in range(4):
                        pool.indirect_dma_start(
                            out=hrow[:, h, k, :], out_offset=None, in_=h_d,
                            in_offset=bass.IndirectOffsetOnAxis(ap=gidx[:, h, k:k + 1], axis=0))\
                            .then_inc(S(f"gathered{h}"), 16)
            pool.wait_ge(S("h_stored"), 16)
            pool.wait_ge(S("dots_done"), 1)
            looped(pool, TA // 8, gather_h)
            scatter(SORT[1], RW, recB_d, lambda h, k: (stB_i[:, h, k:k + 1], stB[:, h, k, :]))
            for l in range(LAYERS):
                pool.wait_ge(S("state_stored"), l * 16 + 16)
                if l:
                    pool.wait_ge(S("flat_ready"), (l - 1) * NT + NT)
                    g.memset(acc_mem[:, 0:38 * AC], 0.0).then_inc(S("acc_half"), 1)

                def gather_x(i):
                    for h in range(2):
                        Q = 2 * i + h
                        pool.wait_ge(S(f"rec_loaded{h}"), l * TB * 2 + i * 16 + 16)
                        if due(2 * Q - 2):
                            pool.wait_ge(S("multiplied"), l * 2 * QB + 2 * Q - 2)
                        pool.sem_inc(S("passed_pool"), 1)
                        for k in range(4):
                            pool.indirect_dma_start(
                                out=xg[:, h, k, :], out_offset=None, in_=x_d,
                                in_offset=bass.IndirectOffsetOnAxis(ap=reci[:, h, k, W_SRC:W_SRC + 1], axis=0))\
                                .then_inc(S(f"sources{h}"), 16)
                looped(pool, TB // 8, gather_x)

        @block.scalar
        def _(act):
            a = nc.scalar

            def stage_A(i, h):
                Q = 2 * i + h
                if due(i * 64):
                    act.wait_ge(S(f"scattered{h}"), i * 64)
                act.sem_inc(S("passed"), 1)
                act.wait_ge(S("addr_ready"), 1)
                a.activation(stA_i[:, h, :], addrA[:, ds(Q * 4, 4)], ACT.Copy).then_inc(S("act_stepA"), 1)
                a.activation(stA[:, h, :, :], itemA[:, ds(Q * 4, 4), :], ACT.Copy).then_inc(S("act_stepA"), 1)
                act.wait_ge(S("act_stepA"), Q * 2 + 2)
                act.sem_inc(S("passed"), 1)
                act.sem_inc(S("staged"), 1)

            def sqrt_of_var(n):
                if due(n):
                    act.wait_ge(S("var_ready"), n)
                a.activation(sd, sd, ACT.Sqrt).then_inc(S("std_ready"), 1)

            sqrt_of_var(1)

            for tt in range(NT):
                if due(tt - 1):
                    act.wait_ge(S("h_made"), tt - 1)
                act.wait_ge(S("xn_turned"), tt + 1)
                a.activation(xtr[:, tt % 2, :], bank[4 + 3 * (tt % 2)][:, :D], ACT.Copy).then_inc(S("xn_turn_copied"), 1)
            looped(act, EC // 8, lambda i: [stage_A(i, h) for h in range(2)])

            def stage_gather(i):
                for h in range(2):
                    Q = 2 * i + h
                    if due(Q - 1):
                        act.wait_ge(S("v_ready"), Q - 1)
                    if due(i * 64):
                        act.wait_ge(S(f"gathered{h}"), i * 64)
                    act.sem_inc(S("passed"), 1)
                    a.activation(gidx[:, h, :], recA[:, ds(Q * 4, 4), 0], ACT.Copy).then_inc(S("act_stepG"), 1)
                    a.activation(gseg[:, h, :], recA[:, ds(Q * 4, 4), 1], ACT.Copy).then_inc(S("act_stepG"), 1)
                    act.wait_ge(S("act_stepG"), Q * 2 + 2)
                    act.sem_inc(S("passed"), 1)
                    act.sem_inc(S("gidx_staged"), 1)
            act.wait_ge(S("recA_loaded"), 16)
            looped(act, TA // 8, stage_gather)

            def attend(i):
                for h in range(2):
                    Q = 2 * i + h
                    act.wait_ge(S("oneh_turned"), Q + 1)
                    if due(Q - 1):
                        act.wait_ge(S("am_ready"), Q - 1)
                    a.activation(onet[:, h, :, :].rearrange("p k s -> p (k s)"), bank[h][:, 0:256].bitcast(BF16), ACT.Copy)\
                        .then_inc(S("onet_ready"), 1)
                    if not (isinstance(i, int) and i == TA // 8 - 1):
                        if due(i * 64):
                            act.wait_ge(S(f"scattered{h}"), EC * 8 + i * 64)
                        act.wait_ge(S(f"attr_loaded{h}"), i * 16 + 16)
                        a.activation(stBb[:, h, :, 0:32], attr_in[:, h, :, :], ACT.Copy).then_inc(S("attr_hi"), 1)
                        a.activation(stB_i[:, h, :], addrB[:, ds(Q * 4, 4)], ACT.Copy).then_inc(S("act_stepB"), 1)
                        a.activation(stBi[:, h, :, W_SRC], itemB[:, ds(Q * 4, 4), 0].bitcast(INT32), ACT.Copy)\
                            .then_inc(S("act_stepB"), 1)
                        a.activation(stB[:, h, :, W_SEG], itemB[:, ds(Q * 4, 4), 1], ACT.Copy).then_inc(S("act_stepB"), 1)
                    act.wait_ge(S("logit_ready"), Q + 1)
                    a.activation(amv[:, h, 16:20], amv[:, h, 12:16], ACT.Exp).then_inc(S("weight_ready"), 1)
                    if not (isinstance(i, int) and i == TA // 8 - 1):
                        act.wait_ge(S("attr_rest"), Q + 1)
                        a.activation(stBb[:, h, :, 32:64], attr_r, ACT.Copy).then_inc(S("act_stepB"), 1)
                        act.wait_ge(S("act_stepB"), Q * 4 + 4)
                        act.sem_inc(S("passed"), 1)
                        act.wait_ge(S("attr_split"), Q + 1)
                        act.sem_inc(S("passed"), 1)
                        act.sem_inc(S("staged"), 1)
            act.wait_ge(S("stB_ready"), 1)
            act.wait_ge(S("addr_ready"), 1 + 1)
            looped(act, TA // 8, attend)

            def turn_all(n):
                for tt in range(NT):
                    act.wait_ge(S("xn_all"), n * NT + tt + 1)
                    a.activation(xt[:, :, tt * P:(tt + 1) * P], bank[tt % 2][:, :D].rearrange("p (k n) -> p k n", k=2), ACT.Copy)\
                        .then_inc(S("xt_copied"), 1)

            def hidden(n, func):
                def chunk(c, h, m):
                    for j in range(8):
                        if due((c - 1) * 4):
                            act.wait_ge(S("tok_done"), n * NT + (c - 1) * 4)
                        act.wait_ge(S("up_done"), n * 56 + c * 8 + j + 1)
                        a.activation(hid_sb[:, h, j, :m], bank[j % 4][:, :m], func, bias=b1_sb[:, j:j + 1])\
                            .then_inc(S("hid_ready"), 1)
                for h in range(2):
                    chunk(h, h, 512)
                with act.Fori(1, 3) as i:
                    for h in range(2):
                        chunk(2 * i + h, h, 512)
                chunk(6, 0, NP_ - 6 * 512)
            sqrt_of_var(2)
            turn_all(0)
            act.wait_ge(S("mod_w_loaded"), 48)
            hidden(0, ACT.Gelu_apprx_tanh)
            sqrt_of_var(3)
            for l in range(LAYERS):
                def relu_msg(i):
                    def copy_attr(Q, h):
                        act.wait_ge(S("rec_turned"), l * QB + Q + 1)
                        if due(2 * Q - 2):
                            act.wait_ge(S("projected"), l * 2 * QB + 2 * Q - 2)
                        a.activation(at[:KA, h, :], bank[h][:KA, 0:256].bitcast(BF16), ACT.Copy).then_inc(S("attr_ready"), 1)
                    for h in range(2):
                        Q = 2 * i + h
                        if isinstance(i, int) and Q == 0:
                            copy_attr(0, 0)
                        if not (isinstance(i, int) and Q == TB // 4 - 1):
                            copy_attr(Q + 1, 1 - h)
                        for j in range(2):
                            act.wait_ge(S("multiplied"), l * 2 * QB + 2 * Q + j + 1)
                            mm = msg[:, h, 2 * j:2 * j + 2, :D]
                            a.activation(mm, mm, ACT.Relu).then_inc(S("msg_ready"), 1)
                looped(act, TB // 8, relu_msg)

                act.wait_ge(S("inv_ready"), l + 1)
                act.wait_ge(S("flushed_b"), l * TB + TB)
                a_flat = lambda tt, h: [
                    a.activation(flat[:, h, r, :], acc_mem[:, ds((tt + r * NT) * AC, D)], ACT.Copy,
                                 scale=inv[:, ds(tt + r * NT, 1)]) for r in range(R)
                ] + [a.activation(flat[:, h, 3, :], xn_mem[:, ds(tt * D, D)], ACT.Copy)]

                def flatten(tt, h):
                    if due(2 * tt - 2):
                        act.wait_ge(S("flat_turned"), l * 2 * NT + 2 * tt - 2)
                    act.sem_inc(S("passed"), 1)
                    if due(tt - 1):
                        act.wait_ge(S("updated"), l * NT + tt - 1)
                    act.sem_inc(S("passed"), 1)
                    a_flat(tt, h)[-1].then_inc(S("flat_ready"), 1)
                for h in range(2):
                    flatten(h, h)
                with act.Fori(1, NT // 2) as i:
                    for h in range(2):
                        flatten(2 * i + h, h)
                flatten(NT - 1, 0)
            sqrt_of_var(4)
            for n in range(3):
                act.wait_ge(S("gate_exp"), n + 1)
                gx = gate[0:1, (8, 24, 40)[n]:(16, 32, 41)[n]]
                a.activation(gx, gx, ACT.Exp).then_inc(S("gate_exp_done"), 1)
            turn_all(1)
            act.wait_ge(S("moe_w_loaded"), 128)
            hidden(1, ACT.Gelu)
            sqrt_of_var(5)

        @block.tensor
        def _(pe):
            m = nc.tensor
            pe.wait_ge(S("const_ready"), 1)

            def rank(s):
                nb, cols, n_ = s["nb"], s["cols"], s["n"]
                for half in range(2):
                    n = s["bodies"] // 2

                    def body(i):
                        for k in range(4):
                            q = (i + half * n) * 4 + k
                            pe.wait_ge(S("onehot"), n_ * 80 + q + 1)
                            if half == 0 and isinstance(i, int) and i == 0 and k == 0 and n_ == 1:
                                pe.wait_ge(S("counts_read"), 1)
                            for c in range(cols):
                                last = m.matmul(bank[half][:nb, ds((i * 4 + k) * cols + c, 1)],
                                                kring[k][:, c * nb:(c + 1) * nb], ones_b[:EP], start=True, stop=True)
                            last.then_inc(S("counted"), 1)
                    looped(pe, n, body)
                pe.wait_ge(S("tiles_ready"), n_ * 1 + 1)
                m.matmul(bank[2][:nb, 0:1], tri[:nb, :nb], small[:nb, 1:2], start=True, stop=True).then_inc(S("tilesum"), 1)
                pe.wait_ge(S("basecol_ready"), n_ * 1 + 1)
                for k in range(8):
                    last = m.transpose(bank[3][:100, k * nb:(k + 1) * nb] if k * nb + nb <= 512 else
                                       bank[4][:100, (k * nb - 450):(k * nb - 450) + nb],
                                       cum[:nb, k * 100:(k + 1) * 100], ident[:nb, :nb])
                last.then_inc(S("base_turned"), 1)
                pe.wait_ge(S("winge_ready"), n_ * 1 + 1)
                for lo in (0, 512):
                    n = min(512, s["T"] - lo)
                    last = m.matmul(bank[5 + lo // 512][:, :n], ones[:nb, :], winge[:nb, lo:lo + n], start=True, stop=True)
                last.then_inc(S("win_summed"), 1)

                def body(i):
                    for k in range(4):
                        q = i * 4 + k
                        h = k // 2
                        pe.wait_ge(S(f"row{h}"), n_ * 320 + i * 16 + 16)
                        pe.wait_ge(S("onehot2"), n_ * 80 + q + 1)
                        if due(q - 1):
                            pe.wait_ge(S("rank_summed"), n_ * 80 + q - 1)
                        ps = bank[k % 2][:EP, :cols * nb]
                        m.matmul(ps, tri_b[:EP, :EP], kring[k][:, :cols * nb], start=True, stop=False)
                        m.matmul(ps, ones[0:1, :EP], baser[h][:, (k % 2) * cols * nb:(k % 2 + 1) * cols * nb],
                                 start=False, stop=True).then_inc(S("ranked"), 1)
                looped(pe, s["bodies"], body)
            rank(SORT[0])

            pe.wait_ge(S("xn_ready"), 1)
            pe.wait_ge(S("att_w_loaded"), 96)

            for tt in range(NT):
                if due(tt - 1):
                    pe.wait_ge(S("h_read"), tt - 1)
                if due(tt - 1):
                    pe.wait_ge(S("xn_turn_copied"), tt - 1)
                for k in range(2):
                    last = m.transpose(bank[4 + 3 * (tt % 2)][:, k * P:(k + 1) * P], xn[:, tt, k * P:(k + 1) * P], ident)
                last.then_inc(S("xn_turned"), 1)
                pe.wait_ge(S("xn_turn_copied"), tt + 1)
                for k in range(2):
                    last = m.matmul(bank[2 + tt % 2][:, :D], xtr[:, tt % 2, k * P:(k + 1) * P], wl[:, k, :],
                                    start=(k == 0), stop=(k == 1))
                last.then_inc(S("h_made"), 1)
            rank(SORT[1])

            def turn_v(i):
                for h in range(2):
                    pe.wait_ge(S("v_ready"), 2 * i + h + 1)
                    if due(2 * i + h - 1):
                        pe.wait_ge(S("v_maxed"), 2 * i + h - 1)
                    for k in range(4):
                        last = m.transpose(bank[h][:, k * P:(k + 1) * P], vsel[:, h, k, :], ident)
                    last.then_inc(S("v_turned"), 1)
            looped(pe, TA // 8, turn_v)

            def attend(i):
                def turn(Q, h):
                    if due(Q - 1):
                        pe.wait_ge(S("onet_ready"), Q - 1)
                    pe.wait_ge(S("oneh_ready"), Q + 1)
                    ps = bank[h][:, 0:256].bitcast(BF16)
                    for k in range(4):
                        last = m.transpose(ps[:, k * P:(k + 1) * P], oneb[:, h, k, :], ident_b)
                    last.then_inc(S("oneh_turned"), 1)
                for h in range(2):
                    Q = 2 * i + h
                    if isinstance(i, int) and i == 0 and h == 0:
                        turn(0, 0)
                    if not (isinstance(i, int) and Q == TA // 4 - 1):
                        turn(Q + 1, 1 - h)
                    pe.wait_ge(S("onet_ready"), Q + 1)
                    if due(Q - 1):
                        pe.wait_ge(S("am_read"), Q - 1)
                    for k in range(4):
                        last = m.matmul(bank[2][:, h * 32 + k * 6:h * 32 + k * 6 + 6], onet[:, h, k, :],
                                        tbl[:, ds(Q * 4 + k, 1), :, :].rearrange("p t c s -> p (t c s)"), start=True, stop=True)
                    last.then_inc(S("am_ready"), 1)
                    pe.wait_ge(S(f"pay_loaded{h}"), i * 16 + 16)
                    for k in range(4):
                        if due(Q * 4 + k - 3):
                            pe.wait_ge(S("flushed"), Q * 4 + k - 3)
                        pe.wait_ge(S("ov_ready"), Q * 4 + k + 1)
                        m.matmul(bank[3 + k][:, :AC], vsel[:, h, k, :], hrow[:, h, k, :AC], start=True, stop=True)\
                            .then_inc(S("att_summed"), 1)
            pe.wait_ge(S("tbl_ready"), 1)
            looped(pe, TA // 8, attend)

            def turn_all(n, ready):
                pe.wait_ge(S(ready), 1)
                for tt in range(NT):
                    if due(tt - 1):
                        pe.wait_ge(S("xt_copied"), n * NT + tt - 1)
                    for k in range(2):
                        last = m.transpose(bank[tt % 2][:, k * P:(k + 1) * P], xn[:, tt, k * P:(k + 1) * P], ident)
                    last.then_inc(S("xn_all"), 1)

            def two_products(n):
                def up(c, m_):
                    for j in range(8):
                        if due(c * 8 + j - 3):
                            pe.wait_ge(S("hid_ready"), n * 56 + c * 8 + j - 3)
                        for k in range(2):
                            last = m.matmul(bank[j % 4][:, :m_], w1_sb[:, k, j * P:(j + 1) * P], xt[:, k, ds(c * 512, m_)],
                                            start=(k == 0), stop=(k == 1))
                        last.then_inc(S("up_done"), 1)

                def down(c, h, m_):
                    pe.wait_ge(S("hid_ready"), n * 56 + c * 8 + 8)
                    for q in range(m_ // P):
                        if due(c * 4 + q - 3):
                            pe.wait_ge(S("tok_added"), n * NT + c * 4 + q - 3)
                        for j in range(8):
                            last = m.matmul(bank[4 + q][:, :D], hid_sb[:, h, j, q * P:(q + 1) * P], w2_sb[:, j, :],
                                            start=(j == 0), stop=(j == 7))
                        last.then_inc(S("tok_done"), 1)
                pe.wait_ge(S("xt_copied"), n * NT + NT)
                up(0, 512)
                up(1, 512)
                down(0, 0, 512)
                with pe.Fori(1, 3) as i:
                    up(2 * i, 512)
                    down(2 * i - 1, 1, 512)
                    up(2 * i + 1, 512)
                    down(2 * i, 0, 512)
                up(6, NP_ - 6 * 512)
                down(5, 1, 512)
                down(6, 0, NP_ - 6 * 512)

            turn_all(0, "xn2_ready")
            pe.wait_ge(S("router_ready"), 1)
            m.transpose(bank[7][:NT, :P], tok_w, ident).then_inc(S("router_pe"), 1)
            pe.wait_ge(S("mod_w_loaded"), 48)
            pe.wait_ge(S("router_turned"), 1)
            two_products(0)
            for l in range(LAYERS):
                if l == 0:
                    pe.wait_ge(S("edge_w_ready"), 1)
                    pe.wait_ge(S("tok_added"), NT)
                else:
                    pe.wait_ge(S("updated"), (l - 1) * NT + NT)

                def edges(i):
                    def turn(Q, h, n):
                        if due(Q - 1):
                            pe.wait_ge(S("attr_ready"), l * QB + Q - 1)
                        pe.wait_ge(S(f"rec_loaded{h}"), l * TB * 2 + n * 16 + 16)
                        for k in range(4):
                            last = m.transpose(bank[h][:KA, 0:256].bitcast(BF16)[:, k * P:(k + 1) * P],
                                               recb[:, h, k, 0:KA], ident_b)
                        last.then_inc(S("rec_turned"), 1)

                    def sums(Q, h):
                        pe.wait_ge(S("seg_ready"), l * QB + Q + 1)
                        for k in range(4):
                            pe.wait_ge(S("msg_ready"), l * 2 * QB + 2 * Q + k // 2 + 1)
                            if due(Q * 4 + k - 3):
                                pe.wait_ge(S("flushed_b"), l * TB + Q * 4 + k - 3)
                            m.matmul(bank[4 + k][:, :AC], oneh[:, h, k, :], msg[:, h, k, :], start=True, stop=True)\
                                .then_inc(S("summed"), 1)
                    for h in range(2):
                        Q = 2 * i + h
                        if isinstance(i, int) and Q == 0:
                            turn(0, 0, 0)
                        if not (isinstance(i, int) and Q == TB // 4 - 1):
                            turn(Q + 1, 1 - h, i + h)
                        pe.wait_ge(S("attr_ready"), l * QB + Q + 1)
                        for j in range(2):
                            if due(2 * Q + j - 1):
                                pe.wait_ge(S("multiplied"), l * 2 * QB + 2 * Q + j - 1)
                            for k in (2 * j, 2 * j + 1):
                                o_ = bank[2 + j][:, (k % 2) * D:(k % 2 + 1) * D]
                                m.matmul(o_, at[:KA, h, k * P:(k + 1) * P], we[:KA, 0, :], start=True, stop=False)
                                m.matmul(o_, at[:64, h, k * P:(k + 1) * P], we[:64, 1, :], start=False, stop=False)
                                last = m.matmul(o_, at[:32, h, k * P:(k + 1) * P], we[:32, 2, :], start=False, stop=True)
                            last.then_inc(S("projected"), 1)
                        if not (isinstance(i, int) and Q == 0):
                            sums(Q - 1, 1 - h)
                    if isinstance(i, int) and i == TB // 8 - 1:
                        sums(TB // 4 - 1, 1)
                looped(pe, TB // 8, edges)

                pe.wait_ge(S("layer_w_loaded"), 16 * 13)
                pe.wait_ge(S("flushed_b"), l * TB + TB)

                def turn_flat(tt, h):
                    pe.wait_ge(S("flat_ready"), l * NT + tt + 1)
                    if due(2 * tt - 2):
                        pe.wait_ge(S("turn_copied"), l * 2 * NT + 2 * tt - 2)
                    for b in range(2):
                        for r in range(4):
                            last = m.transpose(bank[2 * h + b][:, r * P:(r + 1) * P],
                                               flat[:, h, 2 * b + r // 2, (r % 2) * P:(r % 2 + 1) * P], ident)
                        last.then_inc(S("flat_turned"), 1)

                def apply(tt, h):
                    pe.wait_ge(S("turn_copied"), l * 2 * NT + 2 * tt + 2)
                    if due(tt - 1):
                        pe.wait_ge(S("updated"), l * NT + tt - 1)
                    o_ = bank[4 + h][:, :D]
                    for r in range(8):
                        m.matmul(o_, turned[:, h, r * P:(r + 1) * P], lw[:, l, r, :], start=(r == 0), stop=False)
                    m.matmul(o_, ones[0:1, :], vecs[0:1, l, :], start=False, stop=True).then_inc(S("applied"), 1)
                turn_flat(0, 0)
                turn_flat(1, 1)
                apply(0, 0)
                with pe.Fori(1, NT // 2) as i:
                    turn_flat(2 * i, 0)
                    apply(2 * i - 1, 1)
                    turn_flat(2 * i + 1, 1)
                    apply(2 * i, 0)
                turn_flat(NT - 1, 0)
                apply(NT - 2, 1)
                apply(NT - 1, 0)
            pe.wait_ge(S("xn4_ready"), 1)
            pe.wait_ge(S("gate_w_loaded"), 32)
            for k in range(2):
                for tt in range(NT):
                    last = m.matmul(bank[7][:, k:k + 1], xn[:, tt, k * P:(k + 1) * P], ones[:, 0:1],
                                    start=(tt == 0), stop=(tt == NT - 1))
            last.then_inc(S("mean_summed"), 1)
            pe.wait_ge(S("mean_ready"), 1)
            for k in range(2):
                last = m.matmul(bank[6][0:1, 0:NE], small[:, 490 + k:491 + k], wr_sb[:, k, :], start=(k == 0), stop=(k == 1))
            last.then_inc(S("logits_made"), 1)
            turn_all(1, "xn4_ready")
            pe.wait_ge(S("top_ready"), 1)
            m.matmul(bank[5][:, 0:2], ones[0:1, :], gate[0:1, 56:58], start=True, stop=True).then_inc(S("top_spread"), 1)
            pe.wait_ge(S("moe_w_loaded"), 128)
            pe.wait_ge(S("moe_w_scaled"), 1)
            two_products(1)

        @block.vector
        def _(dve):
            v = nc.vector
            st = Steps(dve, "dve_step")
            dve.wait_ge(S("p_const"), 11)
            v.tensor_scalar(ident, iota, iota_col, None, ALU.is_equal).then_inc(S("d_const"), 1)
            v.tensor_scalar(ident_b, iota, iota_col, None, ALU.is_equal).then_inc(S("d_const"), 1)
            v.tensor_scalar(tri, iota, iota_col, None, ALU.is_gt).then_inc(S("d_const"), 1)
            v.tensor_scalar(tri_b, iota, iota_col, None, ALU.is_gt).then_inc(S("const_ready"), 1)
            dve.wait_ge(S("ids_loaded"), 48)
            v.tensor_single_scalar(hi_i, src_i, 7, ALU.logical_shift_right).then_inc(S("dve_step"), 1); st.n += 1
            v.tensor_single_scalar(lo_i, src_i, 127, ALU.bitwise_and).then_inc(S("dve_step"), 1); st.n += 1
            st.did(v.tensor_copy(itemB[:, :, 0].bitcast(INT32), src_i))
            st.did(v.tensor_copy(itemA[:, :, 0], dst_i))
            st.settle()
            st.did(v.tensor_copy(keyA, hi_i))
            st.did(v.tensor_copy(itemA[:, :, 1], lo_i))
            st.settle()
            st.did(v.tensor_single_scalar(hi_i, dst_i, 7, ALU.logical_shift_right))
            st.did(v.tensor_single_scalar(lo_i, dst_i, 127, ALU.bitwise_and))
            st.settle()
            st.did(v.scalar_tensor_tensor(keyB, rel_i, float(NT), hi_i, ALU.mult, ALU.add))
            st.did(v.tensor_copy(itemB[:, :, 1], lo_i))
            st.settle()

            def rank(s):
                nb, cols, n_, T = s["nb"], s["cols"], s["n"], s["T"]

                def onehot(k, q):
                    kr = kring[k][:, :cols * nb].rearrange("p (c b) -> p c b", b=nb)
                    io = iota_b[:EP, 0:nb].rearrange("p (a b) -> p a b", a=1).broadcast_to([EP, cols, nb])
                    ky = s["key"][:, ds(q * cols, cols)].rearrange("p (c a) -> p c a", a=1).broadcast_to([EP, cols, nb])
                    return v.tensor_tensor(kr, io, ky, ALU.is_equal)

                def count_body(i):
                    for k in range(4):
                        q = i * 4 + k
                        if due(q - 3):
                            dve.wait_ge(S("counted"), n_ * 80 + q - 3)
                        onehot(k, q).then_inc(S("onehot"), 1)
                looped(dve, s["bodies"], count_body)
                half = EC // 2
                dve.wait_ge(S("counted"), n_ * 80 + s['bodies'] * 4)
                st.did(v.tensor_copy(cnt[:nb, :half], bank[0][:nb, :half]))
                st.run(v.tensor_copy(cnt[:nb, half:], bank[1][:nb, :half]))
                v.tensor_tensor_scan(cum[:nb], cnt[:nb], zeros[:nb], 0.0, ALU.add, ALU.add).then_inc(S("counts_read"), 1)
                dve.wait_ge(S("counts_read"), n_ * 1 + 1)
                ti = small[:nb, 2:3].bitcast(INT32)
                st.run(v.tensor_scalar(ti, cum[:nb, EC - 1:EC], 127.0, None, ALU.add))
                st.run(v.tensor_single_scalar(small[:nb, 3:4].bitcast(INT32), ti, 7, ALU.logical_shift_right))
                v.tensor_copy(small[:nb, 1:2], small[:nb, 3:4].bitcast(INT32)).then_inc(S("tiles_ready"), 1)
                dve.wait_ge(S("tilesum"), n_ * 1 + 1)
                dve.wait_ge(S("tiles_ready"), n_ * 1 + 1)
                st.did(v.tensor_scalar(small[:nb, 4:5], bank[2][:nb, 0:1], 128.0, None, ALU.mult))
                st.run(v.tensor_tensor(small[:nb, 5:6], bank[2][:nb, 0:1], small[:nb, 1:2], ALU.add))
                v.scalar_tensor_tensor(cum[:nb], cum[:nb], small[:nb, 4:5], cnt[:nb], ALU.add, ALU.subtract)\
                    .then_inc(S("basecol_ready"), 1)
                v.tensor_scalar(winge[:nb, :T], iotaT[:nb, :T], small[:nb, 5:6], None, ALU.is_ge).then_inc(S("winge_ready"), 1)
                dve.wait_ge(S("base_turned"), n_ * 1 + 1)
                n1 = min(8, 512 // nb) * nb
                if n1 < 8 * nb:
                    st.did(v.tensor_copy(base_sb[:100, n1:8 * nb], bank[4][:100, n1 - 450:8 * nb - 450]))
                st.run(v.tensor_copy(base_sb[:100, :n1], bank[3][:100, :n1]))
                dve.sem_inc(S("base_ready"), 1)
                dve.wait_ge(S("win_summed"), n_ * 1 + 1)
                w = winbc
                st.did(v.tensor_scalar(w[:, :512], bank[5][:, :], float(nb), None, ALU.min))
                st.run(v.tensor_scalar(w[:, 512:T], bank[6][:, :T - 512], float(nb), None, ALU.min))
                pair = w[0:1, :T].rearrange("p (a b) -> p a b", b=2)
                st.run(v.scalar_tensor_tensor(s["winp"], pair[:, :, 1], nb + 1.0, pair[:, :, 0], ALU.mult, ALU.add))

                def rank_body(i):
                    for k in range(4):
                        q = i * 4 + k
                        onehot(k, q).then_inc(S("onehot2"), 1)
                    for k in range(4):
                        q = i * 4 + k
                        dve.wait_ge(S("ranked"), n_ * 80 + q + 1)
                        v.tensor_tensor(prod[k % 2][:, :cols * nb], bank[k % 2][:EP, :cols * nb],
                                        kring[k][:, :cols * nb], ALU.mult).then_inc(S("rank_masked"), 1)
                        dve.wait_ge(S("rank_masked"), n_ * 80 + q + 1)
                        v.tensor_reduce(slotg[:, k * cols:(k + 1) * cols],
                                        prod[k % 2][:, :cols * nb].rearrange("p (c b) -> p c b", b=nb),
                                        X_AXIS, ALU.add).then_inc(S("rank_summed"), 1)
                    dve.wait_ge(S("rank_summed"), n_ * 80 + i * 4 + 4)
                    v.tensor_scalar(slotf[:, ds(i * 4 * cols, 4 * cols)], slotg[:, :4 * cols], 0.0, None, ALU.add)\
                        .then_inc(S("slots_kept"), 1)
                    dve.wait_ge(S("slots_kept"), n_ * 20 + i + 1)
                looped(dve, s["bodies"], rank_body)
                st.run(v.tensor_copy(hi_i, slotf))
                st.run(v.tensor_single_scalar(lo_i, hi_i, 127, ALU.bitwise_and))
                st.run(v.tensor_single_scalar(hi_i, hi_i, 7, ALU.logical_shift_right))
                v.scalar_tensor_tensor(s["addr"], lo_i, float(T), hi_i, ALU.mult, ALU.add).then_inc(S("addr_ready"), 1)
                dve.wait_ge(S("addr_ready"), n_ * 1 + 1)
            def layer_norm(n, dst, done, src=x_sb):
                for tt in range(NT):
                    st.did(v.bn_stats(stats[:, tt, :], src[:, tt, :]))
                st.settle()
                for tt in range(NT):
                    st.did(v.bn_aggr(mv[:, tt, :], stats[:, tt, :]))
                st.settle()
                v.tensor_scalar(sd, mv[:, :, 1], EPS, None, ALU.add).then_inc(S("var_ready"), 1)
                if due(n):
                    dve.wait_ge(S("std_ready"), n)
                st.run(v.reciprocal(rs, sd))
                for tt in range(NT):
                    st.did(v.tensor_scalar(dst[:, tt, :], src[:, tt, :], mv[:, tt, 0:1], rs[:, tt:tt + 1],
                                           ALU.subtract, ALU.mult))
                st.settle()
                dve.sem_inc(S(done), 1)

            dve.wait_ge(S("x_loaded"), 32)
            dve.wait_ge(S("filled0"), 16)
            layer_norm(1, xn, "xn_ready")
            rank(SORT[0])
            dve.wait_ge(S("att_w_loaded"), 96)
            st.did(v.memset(htab[:, :, D:D + 1], 1.0))
            for tt in range(NT):
                dve.wait_ge(S("h_made"), tt + 1)
                v.tensor_tensor(htab[:, tt, :D], bank[2 + tt % 2][:, :D], vecs[:, 0, :], ALU.add).then_inc(S("h_read"), 1)
            dve.wait_ge(S("h_read"), NT)
            for c, dst in ((1, a1), (2, a2)):
                for t0 in range(0, NT, 5):
                    vb = vecs[:, c:c + 1, :].broadcast_to([P, 5, D])
                    st.run(v.tensor_tensor(dots, htab[:, t0:t0 + 5, :D], vb, ALU.mult))
                    st.run(v.tensor_reduce(dst[:, t0:t0 + 5], dots, X_AXIS, ALU.add))
            dve.sem_inc(S("dots_done"), 1)
            st.did(v.tensor_scalar(a1, a1, small[:, 320:321], None, ALU.add))
            st.run(v.tensor_scalar(a2, a2, small[:, 321:322], None, ALU.add))
            st.run(v.tensor_reduce(gmin[:, 0:1], a2, X_AXIS, ALU.min, negate=True))
            dve.sem_inc(S("gmin_part"), 1)
            st.did(v.tensor_scalar(winA, winbc[:, :TA], float(BKT_A - 1), None, ALU.min))
            rank(SORT[1])
            dve.wait_ge(S("gmin_all"), 1)
            st.did(v.tensor_scalar(a1, a1, gmin[:, 1:2], None, ALU.subtract))
            st.run(v.tensor_scalar(htab[:, :, D + 1], a2, gmin[:, 1:2], None, ALU.add))
            dve.sem_inc(S("htab_ready"), 1)
            dve.sem_inc(S("xn_mem_free"), 1)

            def select(i):
                def maxima(Q, h):
                    dve.wait_ge(S("v_turned"), Q + 1)
                    if not isinstance(Q, int):
                        dve.sem_inc(S("passed"), 1)
                    v.tensor_reduce(vmax[:, ds(Q * 4, 4)], bank[h].rearrange("p (k e) -> p k e", k=4), X_AXIS, ALU.max)\
                        .then_inc(S("v_maxed"), 1)
                for h in range(2):
                    Q = 2 * i + h
                    dve.wait_ge(S(f"gathered{h}"), i * 64 + 64)
                    dve.wait_ge(S("gidx_staged"), Q + 1)
                    if due(Q - 1):
                        dve.wait_ge(S("v_turned"), Q - 1)
                    for k in range(4):
                        last = v.tensor_scalar(vsel[:, h, k, :], iota, gseg[:, h, k:k + 1], hrow[:, h, k, HC - 1:HC],
                                               ALU.is_equal, ALU.mult)
                    last.then_inc(S("v_ready"), 1)
                    if not (isinstance(i, int) and Q == 0):
                        maxima(Q - 1, 1 - h)
                if isinstance(i, int) and i == TA // 8 - 1:
                    maxima(TA // 4 - 1, 1)
            looped(dve, TA // 8, select)
            dve.wait_ge(S("v_maxed"), TA // 4)
            st.run(v.memset(ta1, 0.0))
            for w in range(NT):
                st.run(v.tensor_scalar(tx, winA, float(w), a1[:, w:w + 1], ALU.is_equal, ALU.mult))
                st.did(v.tensor_tensor(ta1, ta1, tx, ALU.add))
                st.run(v.scalar_tensor_tensor(ty, winA, float(w), vmax, ALU.is_equal, ALU.mult))
                st.did(v.tensor_reduce(mx[:, w:w + 1], ty, X_AXIS, ALU.max))
            st.settle()
            st.run(v.tensor_tensor(mx, mx, a1, ALU.add))
            st.run(v.scalar_tensor_tensor(mrow, mx, 0.01, mx, ALU.mult, ALU.max))
            st.run(v.memset(tm, 0.0))
            for w in range(NT):
                st.run(v.tensor_scalar(tx, winA, float(w), mrow[:, w:w + 1], ALU.is_equal, ALU.mult))
                st.run(v.tensor_tensor(tm, tm, tx, ALU.add))
            for c, src in enumerate((ta1, tm)):
                st.run(v.tensor_copy(tbl[:, :, c, 0], src))
                st.run(v.tensor_tensor(src, src, tbl[:, :, c, 0], ALU.subtract))
                st.run(v.tensor_copy(tbl[:, :, c, 1], src))
                st.run(v.tensor_tensor(tbl[:, :, c, 2], src, tbl[:, :, c, 1], ALU.subtract))
            st.did(v.memset(acc_mem[:, :(BKT_A + 1) * AC], 0.0))
            st.run(v.memset(stB, 0.0))
            st.run(v.memset(stBb[:, :, :, 96:99], 1.0))
            dve.sem_inc(S("tbl_ready"), 1)
            dve.sem_inc(S("stB_ready"), 1)

            def flush(Q, winp, base, banks, summed, flushed, off):
                for j in range(2):
                    r = dve.value_load(winp[0:1, ds(Q * 2 + j, 1)], min_val=0, max_val=base * base - 1)
                    for w, k in ((r % base, 2 * j), (r // base, 2 * j + 1)):
                        dve.wait_ge(summed, off + Q * 4 + k + 1)
                        if due(Q * 4 + k):
                            dve.wait_ge(flushed, off + Q * 4 + k)
                        a_ = acc_mem[:, ds(w * AC, AC)]
                        v.tensor_tensor(a_, a_, bank[banks + k][:, :AC], ALU.add).then_inc(flushed, 1)

            def attend(i):
                def onehot(Q, h):
                    if due(Q - 1):
                        dve.wait_ge(S("oneh_turned"), Q - 1)
                    v.tensor_tensor(oneb[:, h, :, :], iota.rearrange("p (a s) -> p a s", a=1).broadcast_to([P, 4, P]),
                                    recA[:, ds(Q * 4, 4), 1:2].broadcast_to([P, 4, P]), ALU.is_equal)\
                        .then_inc(S("oneh_ready"), 1)
                for h in range(2):
                    Q = 2 * i + h
                    if isinstance(i, int) and i == 0 and h == 0:
                        onehot(0, 0)
                    if not (isinstance(i, int) and Q == TA // 4 - 1):
                        onehot(Q + 1, 1 - h)
                    if not (isinstance(i, int) and i == TA // 8 - 1):
                        dve.wait_ge(S("attr_hi"), Q + 1)
                        if due(Q * 4):
                            dve.wait_ge(S("act_stepB"), Q * 4)
                        v.tensor_tensor(attr_r, attr_in[:, h, :, :], stBb[:, h, :, 0:32], ALU.subtract)\
                            .then_inc(S("attr_rest"), 1)
                    dve.wait_ge(S("am_ready"), Q + 1)
                    v.tensor_reduce(amv[:, h, 0:8], bank[2][:, h * 32:h * 32 + 24].rearrange("p (n s) -> p n s", s=3),
                                    X_AXIS, ALU.add).then_inc(S("am_read"), 1)
                    am = amv[:, h, 0:8].rearrange("p (k c) -> p k c", c=2)
                    dve.wait_ge(S(f"pay_loaded{h}"), i * 16 + 16)
                    dve.wait_ge(S("am_read"), Q + 1)
                    v.tensor_tensor(amv[:, h, 8:12], am[:, :, 0], hrow[:, h, :, HC - 1], ALU.add).then_inc(S("lin_step"), 1)
                    dve.wait_ge(S("lin_step"), Q * 2 + 1)
                    v.scalar_tensor_tensor(amv[:, h, 8:12], amv[:, h, 8:12], 0.01, amv[:, h, 8:12], ALU.mult, ALU.max)\
                        .then_inc(S("lin_step"), 1)
                    dve.wait_ge(S("lin_step"), Q * 2 + 2)
                    v.tensor_tensor(amv[:, h, 12:16], amv[:, h, 8:12], am[:, :, 1], ALU.subtract).then_inc(S("logit_ready"), 1)
                    if not (isinstance(i, int) and Q == 0):
                        flush(Q - 1, winpA, BKT_A + 1, 3, S("att_summed"), S("flushed"), 0)
                    if not (isinstance(i, int) and i == TA // 8 - 1):
                        dve.wait_ge(S("act_stepB"), Q * 4 + 4)
                        v.tensor_tensor(stBb[:, h, :, 64:96], attr_r, stBb[:, h, :, 32:64], ALU.subtract)\
                            .then_inc(S("attr_split"), 1)
                    dve.wait_ge(S("weight_ready"), Q + 1)
                    if due(Q * 4 - 4):
                        dve.wait_ge(S("att_summed"), Q * 4 - 4)
                    for k in range(4):
                        v.tensor_scalar(vsel[:, h, k, :], iota, recA[:, ds(Q * 4 + k, 1), 1:2].rearrange("p t c -> p (t c)"),
                                        amv[:, h, 16 + k:17 + k], ALU.is_equal, ALU.mult).then_inc(S("ov_ready"), 1)
                if isinstance(i, int) and i == TA // 8 - 1:
                    flush(TA // 4 - 1, winpA, BKT_A + 1, 3, S("att_summed"), S("flushed"), 0)
            looped(dve, TA // 8, attend)
            dve.wait_ge(S("flushed"), TA)
            st.run(v.tensor_scalar(rs, acc[:, 0:NT, D], 0.0, None, ALU.is_equal))
            st.run(v.tensor_tensor(rs, rs, acc[:, 0:NT, D], ALU.add))
            st.run(v.reciprocal(rs, rs))
            for tt in range(NT):
                st.did(v.scalar_tensor_tensor(x_sb[:, tt, :], acc[:, tt, :D], rs[:, tt:tt + 1], x_sb[:, tt, :],
                                              ALU.mult, ALU.add))
            st.settle()
            dve.sem_inc(S("x1_ready"), 1)

            def tokens(n, last_):
                def tile(tt, q):
                    dve.wait_ge(S("tok_done"), n * NT + tt + 1)
                    y = ycol[:, q % 2, :]
                    v.tensor_tensor(y, bank[4 + q][:, :D], vecs[:, 1, :], ALU.add).then_inc(S("tok_added"), 1)
                    dve.wait_ge(S("tok_added"), n * NT + tt + 1)
                    last_(tt, y)
                for q in range(4):
                    tile(q, q)
                with dve.Fori(1, NT // 4) as i:
                    for q in range(4):
                        tile(i * 4 + q, q)
                tile(NT - 1, 0)

            layer_norm(2, xn, "xn2_ready")
            dve.wait_ge(S("mod_v_loaded"), 48)
            for t0 in range(0, NT, 5):
                st.run(v.tensor_tensor(dots, xn[:, t0:t0 + 5, :], vecs[:, 0:1, :].broadcast_to([P, 5, D]), ALU.mult))
                st.run(v.tensor_reduce(tok_w[:, t0:t0 + 5], dots, X_AXIS, ALU.add))
            st.did(v.tensor_scalar(real, iota_col, float(LAST), None, ALU.is_lt))
            st.did(v.tensor_scalar(low, iota, iota_col, None, ALU.is_lt))
            st.run(v.tensor_scalar(tok_w, tok_w, br_sb, None, ALU.add))
            st.run(v.tensor_scalar(tok_w[:, NT - 1:], tok_w[:, NT - 1:], real, None, ALU.mult))
            st.run(v.tensor_scalar(coef[:, 0:1], real, -1.0, 3.0e38, ALU.add, ALU.mult))
            st.run(v.tensor_tensor(tok_w[:, NT - 1:], tok_w[:, NT - 1:], coef[:, 0:1], ALU.add))
            dve.sem_inc(S("router_ready"), 1)
            dve.wait_ge(S("router_pe"), 1)
            st.run(v.tensor_copy(w_turn[:NT, :], bank[7][:NT, :P]))
            dve.sem_inc(S("router_turned"), 1)
            dve.wait_ge(S("router_row"), 16)
            st.run(v.memset(n_gt, 0.0))
            for tt in range(NT):
                w_ = tok_w[:, tt:tt + 1]
                for c, (lo_, n_, op) in enumerate(((0, tt * P, ALU.is_ge), (tt * P, NP_ - tt * P, ALU.is_gt))):
                    if n_:
                        st.run(v.scalar_tensor_tensor(seen[:, :n_], w_row[:, lo_:lo_ + n_], w_, ones[:, 0:1].broadcast_to([P, n_]),
                                                      op, ALU.mult, accum_out=n_gt[:, c, tt:tt + 1]))
                st.run(v.scalar_tensor_tensor(seen[:, :P], w_row[:, tt * P:(tt + 1) * P], w_, low, ALU.is_equal, ALU.mult,
                                              accum_out=n_gt[:, 2, tt:tt + 1]))
            st.run(v.tensor_tensor(coef, n_gt[:, 0, :], n_gt[:, 1, :], ALU.add))
            st.run(v.tensor_tensor(coef, coef, n_gt[:, 2, :], ALU.add))
            st.run(v.scalar_tensor_tensor(coef, coef, float(TOPK), tok_w, ALU.is_lt, ALU.mult))

            def gated(tt, y):
                v.scalar_tensor_tensor(y, y, coef[:, ds(tt, 1)], xn_mem[:, ds(tt * D, D)], ALU.mult, ALU.add)\
                    .then_inc(S("gated"), 1)
                dve.wait_ge(S("gated"), tt + 1)
                xx = x_sb[:, ds(tt, 1), :].rearrange("p t d -> p (t d)")
                v.tensor_tensor(xx, xx, y, ALU.add).then_inc(S("x2_added"), 1)
            tokens(0, gated)
            dve.wait_ge(S("x2_added"), NT)
            dve.sem_inc(S("x2_ready"), 1)
            dve.wait_ge(S("edge_w_loaded"), 64)
            st.run(v.tensor_copy(we[:KA, 0, :], we_f[:KA, :]))
            st.run(v.tensor_tensor(we_r[:KA, :], we_f[:KA, :], we[:KA, 0, :], ALU.subtract))
            st.run(v.tensor_copy(we[:KA, 1, :], we_r[:KA, :]))
            st.run(v.tensor_tensor(we[:KA, 2, :], we_r[:KA, :], we[:KA, 1, :], ALU.subtract))
            for c in range(2):
                msk = small[:, 0:1]
                st.run(v.tensor_scalar(msk, iota_col, float(97 + c), None, ALU.is_equal))
                st.run(v.tensor_scalar(we_r[:KA, :], we[:KA, 1 + c, :], msk[:KA], None, ALU.mult))
                st.run(v.tensor_scalar(msk, iota_col, float(97 + c), None, ALU.not_equal))
                st.run(v.scalar_tensor_tensor(we[:KA, 0, :], we[:KA, 0, :], msk[:KA], we_r[:KA, :], ALU.mult, ALU.add))
            st.did(v.memset(msg[:, :, :, D:AC], 1.0))
            st.did(v.memset(acc_mem, 0.0))
            st.settle()
            dve.sem_inc(S("edge_w_ready"), 1)
            layer_norm(3, xn, "state_ready")
            for l in range(LAYERS):
                if l:
                    dve.wait_ge(S("flat_ready"), (l - 1) * NT + NT)
                    st.did(v.memset(acc_mem[:, 38 * AC:], 0.0))
                    dve.wait_ge(S("acc_half"), l - 1 + 1)
                    st.settle()

                def edges(i):
                    def products(Q, h):
                        if due(4 * Q - 4):
                            dve.wait_ge(S("summed"), l * TB + 4 * Q - 4)
                        dve.wait_ge(S(f"rec_loaded{h}"), l * TB * 2 + i * 16 + 16)
                        v.tensor_tensor(oneh[:, h, :, :], iota.rearrange("p (a s) -> p a s", a=1).broadcast_to([P, 4, P]),
                                        rec[:, h, :, W_SEG:W_SEG + 1].broadcast_to([P, 4, P]), ALU.is_equal)\
                            .then_inc(S("seg_ready"), 1)
                        for j in range(2):
                            dve.wait_ge(S(f"sources{h}"), l * TB * 8 + i * 64 + 64)
                            dve.wait_ge(S("projected"), l * 2 * QB + 2 * Q + j + 1)
                            v.tensor_tensor(msg[:, h, 2 * j:2 * j + 2, :D], bank[2 + j].rearrange("p (k d) -> p k d", k=2),
                                            xg[:, h, 2 * j:2 * j + 2, :], ALU.mult).then_inc(S("multiplied"), 1)
                    for h in range(2):
                        Q = 2 * i + h
                        products(Q, h)
                        if not (isinstance(i, int) and Q == 0):
                            flush(Q - 1, winpB, BKT_B + 1, 4, S("summed"), S("flushed_b"), l * TB)
                    if isinstance(i, int) and i == TB // 8 - 1:
                        flush(TB // 4 - 1, winpB, BKT_B + 1, 4, S("summed"), S("flushed_b"), l * TB)
                looped(dve, TB // 8, edges)
                dve.wait_ge(S("flushed_b"), l * TB + TB)
                if l == 0:
                    st.run(v.tensor_scalar(inv, acc[:, 0:BKT_B, D], 1.0, None, ALU.max))
                    st.run(v.reciprocal(inv, inv))
                dve.sem_inc(S("inv_ready"), 1)

                def copy_turned(tt, h):
                    if due(tt - 1):
                        dve.wait_ge(S("applied"), l * NT + tt - 1)
                    for b in range(2):
                        dve.wait_ge(S("flat_turned"), l * 2 * NT + 2 * tt + b + 1)
                        v.tensor_copy(turned[:, h, b * 512:(b + 1) * 512], bank[2 * h + b]).then_inc(S("turn_copied"), 1)

                def update(tt, h):
                    dve.wait_ge(S("applied"), l * NT + tt + 1)
                    xx = xn_mem[:, ds(tt * D, D)]
                    v.scalar_tensor_tensor(xx, bank[4 + h][:, :D], 0.0, xx, ALU.max, ALU.add).then_inc(S("updated"), 1)
                copy_turned(0, 0)
                copy_turned(1, 1)
                update(0, 0)
                with dve.Fori(1, NT // 2) as i:
                    copy_turned(2 * i, 0)
                    update(2 * i - 1, 1)
                    copy_turned(2 * i + 1, 1)
                    update(2 * i, 0)
                copy_turned(NT - 1, 0)
                update(NT - 2, 1)
                update(NT - 1, 0)
                dve.wait_ge(S("updated"), l * NT + NT)
                if l < LAYERS - 1:
                    dve.sem_inc(S("state_ready"), 1)
            st.run(v.tensor_scalar(xn[:, NT - 1, :], xn[:, NT - 1, :], real, None, ALU.mult))
            for t0 in range(0, NT, 5):
                st.did(v.tensor_tensor(x_sb[:, t0:t0 + 5, :], x_sb[:, t0:t0 + 5, :], xn[:, t0:t0 + 5, :], ALU.add))
            st.settle()
            dve.sem_inc(S("x3_ready"), 1)
            layer_norm(4, xn, "xn4_ready")
            dve.wait_ge(S("gate_w_loaded"), 32)
            dve.wait_ge(S("mean_summed"), 1)
            st.run(v.tensor_scalar(small[:, 490:492], bank[7][:, 0:2], 1.0 / N, None, ALU.mult))
            dve.sem_inc(S("mean_ready"), 1)
            dve.wait_ge(S("logits_made"), 1)
            G = lambda a_, b_: gate[0:1, a_:b_]
            row8 = iota[0:1, 0:8]

            def softmax(dst, n):
                st.run(v.tensor_reduce(G(60, 61), dst, X_AXIS, ALU.max))
                st.run(v.tensor_scalar(dst, dst, G(60, 61), None, ALU.subtract))
                dve.sem_inc(S("gate_exp"), 1)
                if due(n):
                    dve.wait_ge(S("gate_exp_done"), n)
                st.run(v.tensor_reduce(G(60, 61), dst, X_AXIS, ALU.add))
                st.run(v.reciprocal(G(60, 61), G(60, 61)))
                st.run(v.tensor_scalar(dst, dst, G(60, 61), None, ALU.mult))
            st.run(v.tensor_tensor(G(8, 16), bank[6][0:1, 0:8], G(0, 8), ALU.add))
            softmax(G(8, 16), 1)
            capacity = float(math.ceil(N * 1.25 / NE))
            st.run(v.tensor_scalar(G(16, 24), G(8, 16), float(N), 1e-30, ALU.mult, ALU.max))
            st.run(v.reciprocal(G(16, 24), G(16, 24)))
            st.run(v.tensor_scalar(G(16, 24), G(16, 24), capacity, 1.0, ALU.mult, ALU.min))
            st.run(v.tensor_tensor(G(24, 32), G(8, 16), G(16, 24), ALU.mult))
            softmax(G(24, 32), 2)
            for c in range(2):
                st.run(v.tensor_reduce(G(48 + c, 49 + c), G(24, 32), X_AXIS, ALU.max))
                st.run(v.tensor_scalar(G(32, 40), G(24, 32), G(48 + c, 49 + c), -100.0, ALU.is_equal, ALU.mult))
                st.run(v.tensor_tensor(G(32, 40), G(32, 40), row8, ALU.add))
                st.run(v.tensor_reduce(G(50 + c, 51 + c), G(32, 40), X_AXIS, ALU.min))
                st.run(v.tensor_scalar(G(50 + c, 51 + c), G(50 + c, 51 + c), 100.0, None, ALU.add))
                st.run(v.tensor_scalar(G(32, 40), row8, G(50 + c, 51 + c), -10.0, ALU.is_equal, ALU.mult))
                st.run(v.tensor_tensor(G(24, 32), G(24, 32), G(32, 40), ALU.add))
            st.run(v.tensor_copy(G(62, 64).bitcast(INT32), G(50, 52)))
            dve.sem_inc(S("chosen"), 1)
            st.run(v.tensor_tensor(G(40, 41), G(49, 50), G(48, 49), ALU.subtract))
            dve.sem_inc(S("gate_exp"), 1)
            dve.wait_ge(S("gate_exp_done"), 3)
            st.run(v.tensor_scalar(G(41, 42), G(40, 41), 1.0, None, ALU.add))
            st.run(v.reciprocal(G(56, 57), G(41, 42)))
            st.run(v.tensor_tensor(G(57, 58), G(40, 41), G(56, 57), ALU.mult))
            dve.sem_inc(S("top_ready"), 1)
            dve.wait_ge(S("top_spread"), 1)
            st.run(v.tensor_copy(small[:, 494:496], bank[5][:, 0:2]))
            dve.wait_ge(S("moe_w_loaded"), 128)
            for c in range(2):
                st.did(v.tensor_scalar(w2_sb[:, 4 * c:4 * c + 4, :], w2_sb[:, 4 * c:4 * c + 4, :], small[:, 494 + c:495 + c],
                                       None, ALU.mult))
            st.run(v.tensor_scalar(vecs[:, 0, :], vecs[:, 0, :], small[:, 494:495], None, ALU.mult))
            st.run(v.scalar_tensor_tensor(vecs[:, 1, :], vecs[:, 1, :], small[:, 495:496], vecs[:, 0, :], ALU.mult, ALU.add))
            dve.sem_inc(S("moe_w_scaled"), 1)

            def mixed(tt, y):
                xx = xn_mem[:, ds(tt * D, D)]
                v.tensor_tensor(xx, xx, y, ALU.add).then_inc(S("mixed"), 1)
            tokens(1, mixed)
            dve.wait_ge(S("mixed"), NT)
            layer_norm(5, xn, "norm_done", src=xn)
            dve.wait_ge(S("norm_w_loaded"), 32)
            for t0 in range(0, NT, 5):
                xx = xn[:, t0:t0 + 5, :]
                st.run(v.tensor_tensor(xx, xx, vecs[:, 2:3, :].broadcast_to([P, 5, D]), ALU.mult))
                st.run(v.tensor_tensor(xx, xx, vecs[:, 3:4, :].broadcast_to([P, 5, D]), ALU.add))
                st.run(v.tensor_tensor(x_sb[:, t0:t0 + 5, :], x_sb[:, t0:t0 + 5, :], xx, ALU.add))
            dve.sem_inc(S("out_ready"), 1)


INPUTS = ["x", "src", "dst", "edge_attr_32", "edge_type_3", "L0_gnn_b_layer", "L0_gnn_w_a1", "L0_gnn_b_a1",
          "L0_gnn_w_a2", "L0_gnn_b_a2", "L0_ffn_br", "L0_ffn_w1", "L0_ffn_w2", "L0_ffn_b2", "L1_gnn_weights",
          "L1_gnn_roots", "L1_gnn_biases", "L1_gnn_edge_w", "L1_gnn_edge_b", "L1_ffn_Wr", "L1_ffn_br", "L1_ffn_W1",
          "L1_ffn_W2", "L1_ffn_b2", "L1_ffn_gamma", "L1_ffn_beta"]


def laid_out(inputs):
    import numpy as np
    a = {name: np.ascontiguousarray(inputs[name]) for name in INPUTS}
    for name in ("L0_gnn_w_a1", "L0_gnn_w_a2"):
        a[name] = a[name].reshape(D)
    a["W_layer_t"] = np.ascontiguousarray(np.asarray(inputs["L0_gnn_W_layer"]).T)
    a["wr_mod"] = np.asarray(inputs["L0_ffn_wr"]).reshape(D)
    a["b1_mod"] = np.ascontiguousarray(np.asarray(inputs["L0_ffn_b1"]).reshape(HID // P, P).T)
    a["b1_moe"] = np.ascontiguousarray(np.asarray(inputs["L1_ffn_b1"]).reshape(NE, FE // P, P).transpose(0, 2, 1))
    return a


def kernel(**inputs):
    import concourse.bacc as bacc
    from concourse.bass_utils import run_bass_kernel_spmd

    nc = bacc.Bacc("TRN2", target_bir_lowering=False, num_devices=1)
    arrays = {f"in_{name}": a for name, a in laid_out(inputs).items()}
    t = {name[3:]: nc.dram_tensor(name, a.shape, mybir.dt.from_np(a.dtype), kind="ExternalInput").ap()
         for name, a in arrays.items()}
    out = nc.dram_tensor("out_0", (N, D), FP32, kind="ExternalOutput").ap()
    build(nc, t, out)
    r = run_bass_kernel_spmd(nc, [arrays], core_ids=[0])
    return r.results[0]["out_0"]
```

```python
import math
from contextlib import ExitStack

import concourse.bass as bass
from concourse import mybir

FP32 = mybir.dt.float32
BF16 = mybir.dt.bfloat16
INT32 = mybir.dt.int32
ALU = mybir.AluOpType
ACT = mybir.ActivationFunctionType
X_AXIS = mybir.AxisListType.X
ds = bass.ds

P = 128
N = 3125
D = 256
NT = -(-N // P)
NP_ = NT * P
LAST = N - (NT - 1) * P
E = 100000
EP, EC = 125, 800
R = 3
F_ATTR = 32
LAYERS = 3
EPS = 1e-5
TOPK = max(1, int(0.5 * N)) - 1
NE, FE = 8, 512
HID = 1024
BKT_A, BKT_B = NT, R * NT


def slots_tiles(buckets):
    return -(-((E + buckets * (P - 1)) // P) // 8) * 8


TA, TB = slots_tiles(BKT_A), slots_tiles(BKT_B)
QB = TB // 4
assert TB // 4 % 4 == 2
assert TA // 4 == EC // 4 + 2
RW = 64
W_SRC, W_SEG = 50, 51
KA = 3 * F_ATTR + 3
HC = D + 2
AC = D + 1


def build(nc, t, out):
    ctx = ExitStack()
    with ctx:
        def sb(name, shape, dt=FP32):
            return ctx.enter_context(nc.sbuf_tensor(name, shape, dt))[:]

        sems = {}

        def S(name):
            if name not in sems:
                sems[name] = ctx.enter_context(nc.semaphore(name))
            return sems[name]

        def turns(h):
            return (TB // 4 - h + 3) // 4

        def dram(name, shape, dt=FP32):
            return nc.dram_tensor(name, shape, dt, kind="Internal").ap()

        def due(value):
            return not isinstance(value, int) or value > 0

        class Steps:

            def __init__(self, eng, name):
                self.eng, self.name, self.n = eng, name, 0

            def did(self, ins):
                ins.then_inc(S(self.name), 1)
                self.n += 1

            def settle(self):
                self.eng.wait_ge(S(self.name), self.n)

            def run(self, ins):
                self.did(ins)
                self.settle()

        def looped(eng, n, body):
            body(0)
            with eng.Fori(1, n - 1) as i:
                body(i)
            body(n - 1)

        x_sb = sb("x_sb", [P, NT, D])
        xn_mem = sb("xn_mem", [P, NT * D])
        xn = xn_mem.rearrange("p (t d) -> p t d", d=D)
        xt_mem = sb("xt_mem", [P, NT * HC])
        acc_mem = sb("acc_mem", [P, (BKT_B + 1) * AC])
        acc = acc_mem.rearrange("p (w c) -> p w c", c=AC)
        sort_mem = sb("sort_mem", [P, 7 * EC])
        keyA, keyB = (sort_mem[:EP, k * EC // 2:(k + 1) * EC // 2].bitcast(BF16) for k in range(2))
        itemA, itemB = (sort_mem[:EP, (1 + 2 * k) * EC:(3 + 2 * k) * EC].rearrange("p (e c) -> p e c", c=2) for k in range(2))
        addrA, addrB = (sort_mem[:EP, (5 + k) * EC:(6 + k) * EC].bitcast(INT32) for k in range(2))
        winpA, winpB = sb("winpA", [1, TA // 2], INT32), sb("winpB", [1, TB // 2], INT32)
        z_mem = sb("z_mem", [P, 5500])

        def z(lo, n, dt=FP32):
            assert lo + n <= 5500
            v = z_mem[:, lo:lo + n]
            return v if dt == FP32 else v.bitcast(dt)

        iota = sb("iota", [P, P])
        iota_col = sb("iota_col", [P, 1])
        iota_b = sb("iota_b", [P, P], BF16)
        ident = sb("ident", [P, P])
        ident_b = sb("ident_b", [P, P], BF16)
        tri_b = sb("tri_b", [P, P], BF16)
        tri = sb("tri", [P, P])
        ones = sb("ones", [P, P])
        ones_b = sb("ones_b", [P, 1], BF16)
        vecs = sb("vecs", [P, 4, D])
        small = sb("small", [P, 512])

        raw = [acc_mem[:EP, k * EC:(k + 1) * EC].bitcast(INT32) for k in range(5)]
        src_i, dst_i, rel_i, hi_i, lo_i = raw
        o = 5 * EC
        cnt = acc_mem[:, o:o + EC]; o += EC
        cum = acc_mem[:, o:o + EC]; o += EC
        zeros = acc_mem[:, o:o + EC]; o += EC
        base_sb = acc_mem[:, o:o + 8 * BKT_B]; o += 8 * BKT_B
        slotf = acc_mem[:EP, o:o + EC]; o += EC
        iotaT = acc_mem[:, o:o + TB]; o += TB
        winge = acc_mem[:, o:o + TB]; o += TB
        winbc = acc_mem[:, o:o + TB]; o += TB
        fill = acc_mem[:, o:o + 512]; o += 512
        GC = {0: 10, 1: 5}
        kring = [acc_mem[:EP, o + k * 192:o + (k + 1) * 192].bitcast(BF16) for k in range(4)]; o += 4 * 192
        baser = [acc_mem[0:1, o + k * 768:o + k * 768 + 768] for k in range(2)]; o += 2 * 768
        prod = [acc_mem[:EP, o + k * 384:o + (k + 1) * 384] for k in range(2)]; o += 2 * 384
        slotg = acc_mem[:EP, o:o + 40]; o += 40
        assert o <= (BKT_B + 1) * AC, o

        bank = [ctx.enter_context(nc.psum_tensor(f"bank{k}", [P, 512], FP32))[:] for k in range(8)]

        o = 0
        recA = xn_mem[:, o:o + 2 * TA].rearrange("p (t c) -> p t c", c=2); o += 2 * TA
        vmax = xn_mem[:, o:o + TA]; o += TA
        winA = xn_mem[:, o:o + TA]; o += TA
        tbl = xn_mem[:, o:o + 3 * TA].bitcast(BF16).rearrange("p (t c s) -> p t c s", c=2, s=3); o += 3 * TA
        assert o <= NT * D
        htab = xt_mem[:, 0:NT * HC].rearrange("p (t c) -> p t c", c=HC)

        stA_i = z(0, 8, INT32)[:EP].rearrange("p (h k) -> p h k", h=2)
        stA = z(8, 16)[:EP].rearrange("p (h k c) -> p h k c", h=2, c=2)

        wl = z(32, 2 * D).rearrange("p (k d) -> p k d", k=2)
        xtr = z(544, 2 * D).rearrange("p (h c) -> p h c", h=2)
        dots = z(1056, 5 * D).rearrange("p (t d) -> p t d", d=D)
        hrow = z(32, 8 * HC).rearrange("p (h k c) -> p h k c", h=2, k=4)
        vsel = z(2112, 1024).rearrange("p (h k s) -> p h k s", h=2, k=4)
        seg1 = z(32, 2048).rearrange("p (h k s) -> p h k s", h=4, k=4)
        onet = z(3648, 512, BF16).rearrange("p (h k s) -> p h k s", h=2, k=4)
        gidx = z(4160, 8, INT32).rearrange("p (h k) -> p h k", h=2)
        gseg = z(4168, 8).rearrange("p (h k) -> p h k", h=2)
        amv = z(4176, 64).rearrange("p (h n) -> p h n", h=2)
        attr_in = z(4240, 256)[:EP].rearrange("p (h k f) -> p h k f", h=2, k=4)
        attr_r = z(4496, 128)[:EP].rearrange("p (k f) -> p k f", k=4)
        o = (BKT_A + 1) * AC
        ta1 = acc_mem[:, o:o + TA]; o += TA
        tm = acc_mem[:, o:o + TA]; o += TA
        tx = acc_mem[:, o:o + TA]; o += TA
        ty = acc_mem[:, o:o + TA]; o += TA
        pay = acc_mem[:, o:o + 16 * HC].rearrange("p (h k c) -> p h k c", h=4, k=4); o += 16 * HC
        assert o <= (BKT_B + 1) * AC - 16 * RW - 16
        o = (BKT_B + 1) * AC - 16 * RW - 16
        stB_mem = acc_mem[:EP, o:o + 16 * RW]; o += 16 * RW
        stB, stBb, stBi = (m_.rearrange("p (h k w) -> p h k w", h=4, k=4)
                           for m_ in (stB_mem, stB_mem.bitcast(BF16), stB_mem.bitcast(INT32)))
        stB_i = acc_mem[:EP, o:o + 16].bitcast(INT32).rearrange("p (h k) -> p h k", h=4); o += 16
        assert o <= (BKT_B + 1) * AC
        a1 = small[:, 330:355]
        a2 = small[:, 355:380]
        mx = small[:, 380:405]
        mrow = small[:, 405:430]
        gmin = small[:, 430:432]
        ssum = small[:, 432:457]
        stats = small[:, 64:214].rearrange("p (t c) -> p t c", c=6)
        mv = small[:, 214:264].rearrange("p (t c) -> p t c", c=2)
        sd = small[:, 264:289]
        rs = small[:, 289:314]

        w_row = acc_mem[:, 0:NP_]
        o = NP_
        w1_sb = acc_mem[:, o:o + 2 * HID].rearrange("p (k f) -> p k f", k=2); o += 2 * HID
        w2_sb = acc_mem[:, o:o + 8 * D].rearrange("p (j d) -> p j d", d=D); o += 8 * D
        hid_sb = acc_mem[:, o:o + 2 * 8 * 512].rearrange("p (h j n) -> p h j n", h=2, j=8); o += 2 * 8 * 512
        seen = acc_mem[:, o:o + NP_ // 2].bitcast(BF16); o += NP_ // 2
        ycol = acc_mem[:, o:o + 2 * D].rearrange("p (h d) -> p h d", h=2); o += 2 * D
        assert o <= (BKT_B + 1) * AC - 16 * RW - 16
        xt = xt_mem[:, 0:2 * NP_].rearrange("p (k n) -> p k n", k=2)
        tok_w = small[:, 330:355]
        n_gt = small[:, 355:430].rearrange("p (c t) -> p c t", c=3)
        coef = small[:, 432:457]
        real = small[:, 457:458]
        b1_sb = small[:, 460:468]
        br_sb = small[:, 468:469]
        low = z(0, P)
        w_turn = z(P, P)
        lw = xt_mem[:, 0:LAYERS * 8 * D].rearrange("p (l m d) -> p l m d", l=LAYERS, m=8)
        rec_mem = sort_mem[:, 16 * D:16 * D + 16 * RW]
        rec, recb, reci = (m_.rearrange("p (h k w) -> p h k w", h=4, k=4)
                           for m_ in (rec_mem, rec_mem.bitcast(BF16), rec_mem.bitcast(INT32)))
        at = z(512, 512, BF16).rearrange("p (h n) -> p h n", h=2)
        oneh = z(1024, 1024).rearrange("p (h k s) -> p h k s", h=2, k=4)
        msg = z(2048, 8 * AC).rearrange("p (h k c) -> p h k c", h=2, k=4)
        we = z(4104, 3 * 128, BF16).rearrange("p (m d) -> p m d", m=3)
        we_f = z(4488, D)
        we_r = z(4744, D)
        xg = sort_mem[:, 0:16 * D].rearrange("p (h k d) -> p h k d", h=4, k=4)
        turned = sort_mem[:, 0:8 * D].rearrange("p (h n) -> p h n", h=2)
        flat = sort_mem[:, 8 * D:16 * D].rearrange("p (h m d) -> p h m d", h=2, m=4)
        inv = small[:, 320:395]
        gate = small[:, 0:64]
        wr_sb = small[:, 470:486].rearrange("p (k e) -> p k e", k=2)

        recA_d = dram("recA_d", [P * TA, 2])
        recB_d = dram("recB_d", [P * TB, RW])
        h_d = dram("h_d", [NP_, HC])
        pay_d = dram("pay_d", [P, TA * HC])
        x_d = dram("x_d", [NP_, D])
        tok_d = dram("tok_d", [1, NP_])
        baseA_d, baseB_d = dram("baseA_d", [EC, BKT_A]), dram("baseB_d", [EC, BKT_B])
        SORT = [dict(nb=BKT_A, T=TA, key=keyA, base_d=baseA_d, addr=addrA, winp=winpA, n=0),
                dict(nb=BKT_B, T=TB, key=keyB, base_d=baseB_d, addr=addrB, winp=winpB, n=1)]
        for s, cols in zip(SORT, (10, 5)):
            s["cols"] = cols
            s["bodies"] = EC // (4 * cols)

        block = ctx.enter_context(nc.Block())

        @block.sync
        def _(sp):
            for dst, name in ((src_i, "src"), (dst_i, "dst"), (rel_i, "edge_type_3")):
                sp.dma_start(dst, t[name].rearrange("(p c) -> p c", c=EC)).then_inc(S("ids_loaded"), 16)
            x_rows = t["x"][0:(NT - 1) * P, :].rearrange("(t p) d -> p t d", p=P)
            sp.wait_ge(S("x_zeroed"), 1)
            sp.dma_start(x_sb[:, 0:NT - 1, :], x_rows).then_inc(S("x_loaded"), 16)
            sp.dma_start(x_sb[0:LAST, NT - 1, :], t["x"][(NT - 1) * P:N, :]).then_inc(S("x_loaded"), 16)
            sp.dma_start(wl, t["W_layer_t"].rearrange("(k p) d -> p k d", p=P)).then_inc(S("att_w_loaded"), 16)
            for k, name in enumerate(("L0_gnn_b_layer", "L0_gnn_w_a1", "L0_gnn_w_a2")):
                sp.dma_start(vecs[:, k, :], t[name].rearrange("(a d) -> a d", a=1).broadcast_to([P, D]))\
                    .then_inc(S("att_w_loaded"), 16)
            for k, name in enumerate(("L0_gnn_b_a1", "L0_gnn_b_a2")):
                sp.dma_start(small[:, 320 + k:321 + k], t[name].rearrange("(a d) -> a d", a=1).broadcast_to([P, 1]))\
                    .then_inc(S("att_w_loaded"), 16)
            sp.wait_ge(S("fill_ready"), 1)
            sp.dma_start(recA_d.rearrange("(p t) c -> p t c", p=P),
                         xn_mem[:, 0:2 * TA].rearrange("p (t c) -> p t c", c=2)).then_inc(S("filled0"), 16)
            fb = fill.rearrange("p (a c) -> p a c", a=1).broadcast_to([P, TB // 8, 512])
            sp.dma_start(recB_d.rearrange("(p q t) c -> p q (t c)", p=P, t=8), fb).then_inc(S("filled1"), 16)

            def rank_io(s):
                nb, cols, n_ = s["nb"], s["cols"], s["n"]
                sp.wait_ge(S("base_ready"), n_ * 1 + 1)
                sp.dma_start(s["base_d"].rearrange("(k j) b -> j k b", j=100),
                             base_sb[:100, :8 * nb].rearrange("j (k b) -> j k b", b=nb)).then_inc(S("base_stored"), 16)
                sp.wait_ge(S("base_stored"), n_ * 16 + 16)
                rows = s["base_d"].rearrange("(a j) b -> a (j b)", j=2 * cols)

                def body(i):
                    for h in range(2):
                        if due(i * 4 + 2 * h - 2):
                            sp.wait_ge(S("rank_summed"), n_ * 80 + i * 4 + 2 * h - 2)
                        sp.dma_start(baser[h][:, :2 * cols * nb], rows[ds(2 * i + h, 1), :]).then_inc(S(f"row{h}"), 16)
                looped(sp, s["bodies"], body)
            rank_io(SORT[0])
            rank_io(SORT[1])
            sp.wait_ge(S("htab_ready"), 1)
            sp.dma_start(h_d.rearrange("(t p) c -> p t c", p=P), htab).then_inc(S("h_stored"), 16)
            for h in range(2):
                sp.wait_ge(S(f"scattered{h}"), EC // 8 * 64)
            sp.dma_start(recA, recA_d.rearrange("(p t) c -> p t c", p=P)).then_inc(S("recA_loaded"), 16)

            def keep(i):
                for h in range(2):
                    sp.wait_ge(S(f"gathered{h}"), i * 64 + 64)
                    sp.dma_start(pay_d[:, ds((2 * i + h) * 4 * HC, 4 * HC)],
                                 hrow[:, h, :, :].rearrange("p k c -> p (k c)")).then_inc(S(f"kept{h}"), 16)
            looped(sp, TA // 8, keep)
            for h in range(2):
                sp.wait_ge(S(f"kept{h}"), TA // 8 * 16)
            attr = t["edge_attr_32"].rearrange("(p e) f -> p (e f)", e=EC)

            def load_pay(Q, h):
                if due(4 * Q - 12):
                    sp.wait_ge(S("att_summed"), 4 * Q - 12)
                sp.dma_start(pay[:, h, :, :].rearrange("p k c -> p (k c)"),
                             pay_d[:, ds(Q * 4 * HC, 4 * HC)]).then_inc(S(f"pay_loaded{h}"), 16)

            def feed(i):
                for h in range(4):
                    Q = 4 * i + h
                    load_pay(Q + 2, (h + 2) % 4)
                    if due(Q - 1):
                        sp.wait_ge(S("attr_rest"), Q - 1)
                    sp.dma_start(attr_in[:, h % 2, :, :].rearrange("p k f -> p (k f)"),
                                 attr[:, ds(Q * 4 * F_ATTR, 4 * F_ATTR)]).then_inc(S(f"attr_loaded{h % 2}"), 16)
            load_pay(0, 0)
            load_pay(1, 1)
            looped(sp, EC // 16, feed)
            sp.wait_ge(S("x1_ready"), 1)
            sp.dma_start(w1_sb, t["L0_ffn_w1"].rearrange("(k p) f -> p k f", p=P)).then_inc(S("mod_w_loaded"), 16)
            sp.dma_start(w2_sb, t["L0_ffn_w2"].rearrange("(j p) d -> p j d", p=P)).then_inc(S("mod_w_loaded"), 16)
            sp.dma_start(b1_sb, t["b1_mod"]).then_inc(S("mod_w_loaded"), 16)
            sp.dma_start(vecs[:, 0, :], t["wr_mod"].rearrange("(a d) -> a d", a=1).broadcast_to([P, D]))\
                .then_inc(S("mod_v_loaded"), 16)
            sp.dma_start(vecs[:, 1, :], t["L0_ffn_b2"].rearrange("(a d) -> a d", a=1).broadcast_to([P, D]))\
                .then_inc(S("mod_v_loaded"), 16)
            sp.dma_start(br_sb, t["L0_ffn_br"].rearrange("(a d) -> a d", a=1).broadcast_to([P, 1]))\
                .then_inc(S("mod_v_loaded"), 16)
            sp.wait_ge(S("router_turned"), 1)
            sp.dma_start(tok_d.rearrange("a (t p) -> (a t) p", p=P), w_turn[:NT, :]).then_inc(S("router_stored"), 16)
            sp.wait_ge(S("router_stored"), 16)
            sp.dma_start(w_row, tok_d.broadcast_to([P, NP_])).then_inc(S("router_row"), 16)
            sp.wait_ge(S("x2_ready"), 1)
            for h in range(4):
                sp.wait_ge(S(f"edges_put{h}"), EC // 16 * 64)
            for l in range(LAYERS):
                for r in range(R):
                    sp.dma_start(lw[:, l, 2 * r:2 * r + 2, :], t["L1_gnn_weights"][l, r].rearrange("(k p) d -> p k d", p=P))\
                        .then_inc(S("layer_w_loaded"), 16)
                sp.dma_start(lw[:, l, 6:8, :], t["L1_gnn_roots"][l].rearrange("(k p) d -> p k d", p=P))\
                    .then_inc(S("layer_w_loaded"), 16)
            sp.dma_start(vecs[0:1, 0:LAYERS, :], t["L1_gnn_biases"].rearrange("(a l) d -> a l d", a=1))\
                .then_inc(S("layer_w_loaded"), 16)
            for k in range(3):
                sp.dma_start(we_f[32 * k:32 * k + 32, :], t["L1_gnn_edge_w"]).then_inc(S("edge_w_loaded"), 16)
            sp.dma_start(we_f[96:99, :], t["L1_gnn_edge_b"].rearrange("(a d) -> a d", a=1).broadcast_to([3, D]))\
                .then_inc(S("edge_w_loaded"), 16)
            recs = recB_d.rearrange("(p t) w -> p (t w)", p=P)
            for l in range(LAYERS):
                sp.wait_ge(S("state_ready"), l + 1)
                sp.dma_start(x_d.rearrange("(t p) d -> p t d", p=P), xn).then_inc(S("state_stored"), 16)
                if l == 0:
                    sp.wait_ge(S("edge_w_ready"), 1)

                def feed(i, quads=4):
                    for h in range(quads):
                        Q = 4 * i + h
                        if due(Q - 3):
                            sp.wait_ge(S("rec_turned"), l * QB + Q - 3)
                        sp.sem_inc(S("passed"), 1)
                        if due(i * 64):
                            sp.wait_ge(S(f"sources{h}"), l * 64 * turns(h) + i * 64)
                        if due(Q - 3):
                            sp.wait_ge(S("seg_ready"), l * QB + Q - 3)
                        sp.dma_start(rec[:, h, :, :].rearrange("p k w -> p (k w)"),
                                     recs[:, ds(Q * 4 * RW, 4 * RW)]).then_inc(S(f"rec_loaded{h}"), 16)
                looped(sp, TB // 16, feed)
                feed(TB // 16, TB // 4 % 4)
            sp.wait_ge(S("x3_ready"), 1)
            sp.dma_start(wr_sb, t["L1_ffn_Wr"].rearrange("(k p) e -> p k e", p=P)).then_inc(S("gate_w_loaded"), 16)
            sp.dma_start(gate[0:1, 0:8], t["L1_ffn_br"].rearrange("(a e) -> a e", a=1)).then_inc(S("gate_w_loaded"), 16)
            for k, name in ((2, "L1_ffn_gamma"), (3, "L1_ffn_beta")):
                sp.dma_start(vecs[:, k, :], t[name].rearrange("(a d) -> a d", a=1).broadcast_to([P, D]))\
                    .then_inc(S("norm_w_loaded"), 16)
            sp.wait_ge(S("chosen"), 1)
            for c in range(2):
                e = sp.value_load(gate[0:1, 62 + c:63 + c].bitcast(INT32), min_val=0, max_val=NE - 1)
                sp.dma_start(w1_sb[:, :, c * FE:(c + 1) * FE],
                             t["L1_ffn_W1"][ds(e, 1), :, :].rearrange("e (k p) f -> p (e k) f", p=P)).then_inc(S("moe_w_loaded"), 16)
                sp.dma_start(w2_sb[:, 4 * c:4 * c + 4, :],
                             t["L1_ffn_W2"][ds(e, 1), :, :].rearrange("e (j p) d -> p (e j) d", p=P)).then_inc(S("moe_w_loaded"), 16)
                sp.dma_start(b1_sb[:, 4 * c:4 * c + 4],
                             t["b1_moe"][ds(e, 1), :, :].rearrange("e p j -> p (e j)")).then_inc(S("moe_w_loaded"), 16)
                sp.dma_start(vecs[:, c, :], t["L1_ffn_b2"][ds(e, 1), :].broadcast_to([P, D])).then_inc(S("moe_w_loaded"), 16)
            sp.wait_ge(S("out_ready"), 1)
            sp.dma_start(out[0:(NT - 1) * P, :].rearrange("(t p) d -> p t d", p=P), x_sb[:, 0:NT - 1, :]).then_inc(S("out_stored"), 16)
            sp.dma_start(out[(NT - 1) * P:N, :], x_sb[0:LAST, NT - 1, :]).then_inc(S("out_stored"), 16)
            sp.wait_ge(S("out_stored"), 32)
            sp.wait_ge(S("x_loaded"), 32)
            sp.wait_ge(S("layer_w_loaded"), 16 * 13)

        @block.gpsimd
        def _(pool):
            g = nc.gpsimd
            g.memset(x_sb[:, NT - 1, :], 0.0).then_inc(S("x_zeroed"), 1)
            g.memset(fill, 0.0).then_inc(S("p_const"), 1)
            g.memset(xn_mem[:, 0:2 * TA], 0.0).then_inc(S("p_const"), 1)
            g.iota(iota, pattern=[[1, P]], base=0, channel_multiplier=0,
                   allow_small_or_imprecise_dtypes=True).then_inc(S("p_const"), 1)
            g.iota(iota_b, pattern=[[1, P]], base=0, channel_multiplier=0,
                   allow_small_or_imprecise_dtypes=True).then_inc(S("p_const"), 1)
            g.iota(iota_col, pattern=[[1, 1]], base=0, channel_multiplier=1,
                   allow_small_or_imprecise_dtypes=True).then_inc(S("p_const"), 1)
            g.iota(iotaT, pattern=[[1, TB]], base=0, channel_multiplier=0,
                   allow_small_or_imprecise_dtypes=True).then_inc(S("p_const"), 1)
            g.memset(ones, 1.0).then_inc(S("p_const"), 1)
            g.memset(ones_b, 1.0).then_inc(S("p_const"), 1)
            g.memset(zeros, 0.0).then_inc(S("p_const"), 1)
            pool.wait_ge(S("p_const"), 9)
            g.memset(fill.rearrange("p (t c) -> p t c", c=RW)[:, :, W_SEG:W_SEG + 1], -1.0).then_inc(S("p_const"), 1)
            g.memset(xn_mem[:, 0:2 * TA].rearrange("p (t c) -> p t c", c=2)[:, :, 1:2], -1.0).then_inc(S("p_const"), 1)
            pool.wait_ge(S("p_const"), 11)
            pool.sem_inc(S("fill_ready"), 1)

            def scatter_ids(i):
                for h in range(2):
                    pool.wait_ge(S("staged"), 2 * i + h + 1)
                    pool.sem_inc(S("passed_pool"), 1)
                    for k in range(4):
                        pool.indirect_dma_start(
                            out=recA_d, out_offset=bass.IndirectOffsetOnAxis(ap=stA_i[:, h, k:k + 1], axis=0),
                            in_=stA[:, h, k, :], in_offset=None).then_inc(S(f"scattered{h}"), 16)

            def scatter_edges(i):
                for h in range(4):
                    pool.wait_ge(S("act_stepB"), 4 * (4 * i + h) + 4)
                    pool.wait_ge(S("attr_split"), 4 * i + h + 1)
                    pool.sem_inc(S("passed_pool"), 1)
                    for k in range(4):
                        pool.indirect_dma_start(
                            out=recB_d, out_offset=bass.IndirectOffsetOnAxis(ap=stB_i[:, h, k:k + 1], axis=0),
                            in_=stB[:, h, k, :], in_offset=None).then_inc(S(f"edges_put{h}"), 16)
            pool.wait_ge(S("filled0"), 16)
            looped(pool, EC // 8, scatter_ids)
            pool.wait_ge(S("gmin_part"), 1)
            g.partition_all_reduce(gmin[:, 1:2], gmin[:, 0:1], P, bass.bass_isa.ReduceOp.max).then_inc(S("gmin_all"), 1)

            def gather_h(i):
                for h in range(2):
                    if due(i * 16):
                        pool.wait_ge(S(f"kept{h}"), i * 16)
                    if due(2 * i + h - 1):
                        pool.wait_ge(S("a2_kept"), 2 * i + h - 1)
                    pool.wait_ge(S("gidx_staged"), 2 * i + h + 1)
                    pool.sem_inc(S("passed_pool"), 1)
                    for k in range(4):
                        pool.indirect_dma_start(
                            out=hrow[:, h, k, :], out_offset=None, in_=h_d,
                            in_offset=bass.IndirectOffsetOnAxis(ap=gidx[:, h, k:k + 1], axis=0))\
                            .then_inc(S(f"gathered{h}"), 16)
            pool.wait_ge(S("h_stored"), 16)
            pool.wait_ge(S("dots_done"), 1)
            looped(pool, TA // 8, gather_h)
            pool.wait_ge(S("filled1"), 16)
            looped(pool, EC // 16, scatter_edges)
            for l in range(LAYERS):
                pool.wait_ge(S("state_stored"), l * 16 + 16)
                if l:
                    pool.wait_ge(S("flat_ready"), (l - 1) * NT + NT)
                    g.memset(acc_mem[:, 0:38 * AC], 0.0).then_inc(S("acc_half"), 1)

                def gather_x(i, quads=4):
                    for h in range(quads):
                        Q = 4 * i + h
                        pool.wait_ge(S(f"rec_loaded{h}"), l * 16 * turns(h) + i * 16 + 16)
                        if due(2 * Q - 6):
                            pool.wait_ge(S("multiplied"), l * 2 * QB + 2 * Q - 6)
                        pool.sem_inc(S("passed_pool"), 1)
                        for k in range(4):
                            pool.indirect_dma_start(
                                out=xg[:, h, k, :], out_offset=None, in_=x_d,
                                in_offset=bass.IndirectOffsetOnAxis(ap=reci[:, h, k, W_SRC:W_SRC + 1], axis=0))\
                                .then_inc(S(f"sources{h}"), 16)
                looped(pool, TB // 16, gather_x)
                gather_x(TB // 16, TB // 4 % 4)

        @block.scalar
        def _(act):
            a = nc.scalar

            def stage_A(i, h):
                Q = 2 * i + h
                if due(i * 64):
                    act.wait_ge(S(f"scattered{h}"), i * 64)
                act.sem_inc(S("passed"), 1)
                act.wait_ge(S("addr_ready"), 1)
                a.activation(stA_i[:, h, :], addrA[:, ds(Q * 4, 4)], ACT.Copy).then_inc(S("act_stepA"), 1)
                a.activation(stA[:, h, :, :], itemA[:, ds(Q * 4, 4), :], ACT.Copy).then_inc(S("act_stepA"), 1)
                act.wait_ge(S("act_stepA"), Q * 2 + 2)
                act.sem_inc(S("passed"), 1)
                act.sem_inc(S("staged"), 1)

            def sqrt_of_var(n):
                if due(n):
                    act.wait_ge(S("var_ready"), n)
                a.activation(sd, sd, ACT.Sqrt).then_inc(S("std_ready"), 1)

            sqrt_of_var(1)

            for tt in range(NT):
                if due(tt - 1):
                    act.wait_ge(S("h_made"), tt - 1)
                act.wait_ge(S("xn_turned"), tt + 1)
                a.activation(xtr[:, tt % 2, :], bank[4 + 3 * (tt % 2)][:, :D], ACT.Copy).then_inc(S("xn_turn_copied"), 1)
            looped(act, EC // 8, lambda i: [stage_A(i, h) for h in range(2)])

            def stage_gather(i):
                for h in range(2):
                    Q = 2 * i + h
                    if due(Q - 1):
                        act.wait_ge(S("v_ready"), Q - 1)
                    if due(i * 64):
                        act.wait_ge(S(f"gathered{h}"), i * 64)
                    act.sem_inc(S("passed"), 1)
                    a.activation(gidx[:, h, :], recA[:, ds(Q * 4, 4), 0], ACT.Copy).then_inc(S("act_stepG"), 1)
                    a.activation(gseg[:, h, :], recA[:, ds(Q * 4, 4), 1], ACT.Copy).then_inc(S("act_stepG"), 1)
                    act.wait_ge(S("act_stepG"), Q * 2 + 2)
                    act.sem_inc(S("passed"), 1)
                    act.sem_inc(S("gidx_staged"), 1)
            act.wait_ge(S("recA_loaded"), 16)
            looped(act, TA // 8, stage_gather)

            def turned_onehot(Q, h):
                act.wait_ge(S("oneh_turned"), Q + 1)
                if due(Q - 1):
                    act.wait_ge(S("am_ready"), Q - 1)
                a.activation(onet[:, h, :, :].rearrange("p k s -> p (k s)"), bank[h], ACT.Copy)\
                    .then_inc(S("onet_ready"), 1)

            def weigh(Q, h, n):
                act.wait_ge(S("logit_ready"), Q + 1)
                a.activation(amv[:, h % 2, 16:20], amv[:, h % 2, 12:16], ACT.Exp).then_inc(S("weight_ready"), 1)
                act.wait_ge(S("weight_ready"), Q + 1)
                act.wait_ge(S(f"pay_loaded{h}"), n * 16 + 16)
                for k in range(4):
                    a.activation(pay[:, h, k, :AC], pay[:, h, k, :AC], ACT.Copy, scale=amv[:, h % 2, 16 + k:17 + k])\
                        .then_inc(S("weighted"), 1)

            def attr_middle(Q, h):
                act.wait_ge(S("attr_rest"), Q + 1)
                a.activation(stBb[:, h, :, 32:64], attr_r, ACT.Copy).then_inc(S("act_stepB"), 1)

            def attend(i):
                for h in range(4):
                    Q = 4 * i + h
                    if not (isinstance(i, int) and Q == 0):
                        attr_middle(Q - 1, (h - 1) % 4)
                    if due(i * 64):
                        act.wait_ge(S(f"edges_put{h}"), i * 64)
                    act.wait_ge(S(f"attr_loaded{h % 2}"), i * 32 + h // 2 * 16 + 16)
                    a.activation(stBb[:, h, :, 0:32], attr_in[:, h % 2, :, :], ACT.Copy).then_inc(S("attr_hi"), 1)
                    a.activation(stB_i[:, h, :], addrB[:, ds(Q * 4, 4)], ACT.Copy).then_inc(S("act_stepB"), 1)
                    a.activation(stBi[:, h, :, W_SRC], itemB[:, ds(Q * 4, 4), 0].bitcast(INT32), ACT.Copy)\
                        .then_inc(S("act_stepB"), 1)
                    a.activation(stB[:, h, :, W_SEG], itemB[:, ds(Q * 4, 4), 1], ACT.Copy).then_inc(S("act_stepB"), 1)
                    turned_onehot(Q + 2, h % 2)
                    weigh(Q + 1, (h + 1) % 4, i + (h + 1) // 4)
            act.wait_ge(S("stB_ready"), 1)
            act.wait_ge(S("addr_ready"), 1 + 1)
            turned_onehot(0, 0)
            turned_onehot(1, 1)
            weigh(0, 0, 0)
            looped(act, EC // 16, attend)
            attr_middle(EC // 4 - 1, 3)
            weigh(TA // 4 - 1, 1, EC // 16)

            def turn_all(n):
                for tt in range(NT):
                    act.wait_ge(S("xn_all"), n * NT + tt + 1)
                    a.activation(xt[:, :, tt * P:(tt + 1) * P], bank[tt % 2][:, :D].rearrange("p (k n) -> p k n", k=2), ACT.Copy)\
                        .then_inc(S("xt_copied"), 1)

            def hidden(n, func):
                def chunk(c, h, m):
                    for j in range(8):
                        if due((c - 1) * 4):
                            act.wait_ge(S("tok_done"), n * NT + (c - 1) * 4)
                        act.wait_ge(S("up_done"), n * 56 + c * 8 + j + 1)
                        a.activation(hid_sb[:, h, j, :m], bank[j % 4][:, :m], func, bias=b1_sb[:, j:j + 1])\
                            .then_inc(S("hid_ready"), 1)
                for h in range(2):
                    chunk(h, h, 512)
                with act.Fori(1, 3) as i:
                    for h in range(2):
                        chunk(2 * i + h, h, 512)
                chunk(6, 0, NP_ - 6 * 512)
            sqrt_of_var(2)
            turn_all(0)
            act.wait_ge(S("mod_w_loaded"), 48)
            hidden(0, ACT.Gelu_apprx_tanh)
            sqrt_of_var(3)
            for l in range(LAYERS):
                def copy_attr(Q, h):
                    act.wait_ge(S("rec_turned"), l * QB + Q + 1)
                    if due(2 * Q - 2):
                        act.wait_ge(S("projected"), l * 2 * QB + 2 * Q - 2)
                    a.activation(at[:KA, h, :], bank[h][:KA, 0:256].bitcast(BF16), ACT.Copy).then_inc(S("attr_ready"), 1)

                def relu_msg(i, quads=4):
                    for h in range(quads):
                        Q = 4 * i + h
                        if quads == 4:
                            copy_attr(Q + 2, h % 2)
                        for j in range(2):
                            act.wait_ge(S("multiplied"), l * 2 * QB + 2 * Q + j + 1)
                            mm = msg[:, h % 2, 2 * j:2 * j + 2, :D]
                            a.activation(mm, mm, ACT.Relu).then_inc(S("msg_ready"), 1)
                copy_attr(0, 0)
                copy_attr(1, 1)
                looped(act, TB // 16, relu_msg)
                relu_msg(TB // 16, TB // 4 % 4)

                act.wait_ge(S("inv_ready"), l + 1)
                act.wait_ge(S("flushed_b"), l * TB + TB)
                a_flat = lambda tt, h: [
                    a.activation(flat[:, h, r, :], acc_mem[:, ds((tt + r * NT) * AC, D)], ACT.Copy,
                                 scale=inv[:, ds(tt + r * NT, 1)]) for r in range(R)
                ] + [a.activation(flat[:, h, 3, :], xn_mem[:, ds(tt * D, D)], ACT.Copy)]

                def flatten(tt, h):
                    if due(2 * tt - 2):
                        act.wait_ge(S("flat_turned"), l * 2 * NT + 2 * tt - 2)
                    act.sem_inc(S("passed"), 1)
                    if due(tt - 1):
                        act.wait_ge(S("updated"), l * NT + tt - 1)
                    act.sem_inc(S("passed"), 1)
                    a_flat(tt, h)[-1].then_inc(S("flat_ready"), 1)
                for h in range(2):
                    flatten(h, h)
                with act.Fori(1, NT // 2) as i:
                    for h in range(2):
                        flatten(2 * i + h, h)
                flatten(NT - 1, 0)
            sqrt_of_var(4)
            for n in range(3):
                act.wait_ge(S("gate_exp"), n + 1)
                gx = gate[0:1, (8, 24, 40)[n]:(16, 32, 41)[n]]
                a.activation(gx, gx, ACT.Exp).then_inc(S("gate_exp_done"), 1)
            turn_all(1)
            act.wait_ge(S("moe_w_loaded"), 128)
            hidden(1, ACT.Gelu)
            sqrt_of_var(5)

        @block.tensor
        def _(pe):
            m = nc.tensor
            pe.wait_ge(S("const_ready"), 1)

            def rank(s):
                nb, cols, n_ = s["nb"], s["cols"], s["n"]
                for half in range(2):
                    n = s["bodies"] // 2

                    def body(i):
                        for k in range(4):
                            q = (i + half * n) * 4 + k
                            pe.wait_ge(S("onehot"), n_ * 80 + q + 1)
                            if half == 0 and isinstance(i, int) and i == 0 and k == 0 and n_ == 1:
                                pe.wait_ge(S("counts_read"), 1)
                            for c in range(cols):
                                last = m.matmul(bank[half][:nb, ds((i * 4 + k) * cols + c, 1)],
                                                kring[k][:, c * nb:(c + 1) * nb], ones_b[:EP], start=True, stop=True)
                            last.then_inc(S("counted"), 1)
                    looped(pe, n, body)
                pe.wait_ge(S("tiles_ready"), n_ * 1 + 1)
                m.matmul(bank[2][:nb, 0:1], tri[:nb, :nb], small[:nb, 1:2], start=True, stop=True).then_inc(S("tilesum"), 1)
                pe.wait_ge(S("basecol_ready"), n_ * 1 + 1)
                for k in range(8):
                    last = m.transpose(bank[3][:100, k * nb:(k + 1) * nb] if k * nb + nb <= 512 else
                                       bank[4][:100, (k * nb - 450):(k * nb - 450) + nb],
                                       cum[:nb, k * 100:(k + 1) * 100], ident[:nb, :nb])
                last.then_inc(S("base_turned"), 1)
                pe.wait_ge(S("winge_ready"), n_ * 1 + 1)
                for lo in (0, 512):
                    n = min(512, s["T"] - lo)
                    last = m.matmul(bank[5 + lo // 512][:, :n], ones[:nb, :], winge[:nb, lo:lo + n], start=True, stop=True)
                last.then_inc(S("win_summed"), 1)

                def body(i):
                    for k in range(4):
                        q = i * 4 + k
                        h = k // 2
                        pe.wait_ge(S(f"row{h}"), n_ * 320 + i * 16 + 16)
                        pe.wait_ge(S("onehot2"), n_ * 80 + q + 1)
                        if due(q - 1):
                            pe.wait_ge(S("rank_summed"), n_ * 80 + q - 1)
                        ps = bank[k % 2][:EP, :cols * nb]
                        m.matmul(ps, tri_b[:EP, :EP], kring[k][:, :cols * nb], start=True, stop=False)
                        m.matmul(ps, ones[0:1, :EP], baser[h][:, (k % 2) * cols * nb:(k % 2 + 1) * cols * nb],
                                 start=False, stop=True).then_inc(S("ranked"), 1)
                looped(pe, s["bodies"], body)
            rank(SORT[0])

            pe.wait_ge(S("xn_ready"), 1)
            pe.wait_ge(S("att_w_loaded"), 96)

            for tt in range(NT):
                if due(tt - 1):
                    pe.wait_ge(S("h_read"), tt - 1)
                if due(tt - 1):
                    pe.wait_ge(S("xn_turn_copied"), tt - 1)
                for k in range(2):
                    last = m.transpose(bank[4 + 3 * (tt % 2)][:, k * P:(k + 1) * P], xn[:, tt, k * P:(k + 1) * P], ident)
                last.then_inc(S("xn_turned"), 1)
                pe.wait_ge(S("xn_turn_copied"), tt + 1)
                for k in range(2):
                    last = m.matmul(bank[2 + tt % 2][:, :D], xtr[:, tt % 2, k * P:(k + 1) * P], wl[:, k, :],
                                    start=(k == 0), stop=(k == 1))
                last.then_inc(S("h_made"), 1)
            rank(SORT[1])

            def turn_v(i):
                for h in range(2):
                    pe.wait_ge(S("v_ready"), 2 * i + h + 1)
                    if due(2 * i + h - 1):
                        pe.wait_ge(S("v_maxed"), 2 * i + h - 1)
                    for k in range(4):
                        last = m.transpose(bank[h][:, k * P:(k + 1) * P], vsel[:, h, k, :], ident)
                    last.then_inc(S("v_turned"), 1)
            looped(pe, TA // 8, turn_v)

            def turn_onehot(Q, h):
                if due(Q - 1):
                    pe.wait_ge(S("onet_ready"), Q - 1)
                pe.wait_ge(S("oneh_ready"), Q + 1)
                for k in range(4):
                    last = m.transpose(bank[h % 2][:, k * P:(k + 1) * P], seg1[:, h, k, :], ident)
                last.then_inc(S("oneh_turned"), 1)

            def look_up(Q, h):
                pe.wait_ge(S("onet_ready"), Q + 1)
                if due(Q - 1):
                    pe.wait_ge(S("am_read"), Q - 1)
                for k in range(4):
                    last = m.matmul(bank[2 + 5 * h][:, k * 6:k * 6 + 6], onet[:, h, k, :],
                                    tbl[:, ds(Q * 4 + k, 1), :, :].rearrange("p t c s -> p (t c s)"), start=True, stop=True)
                last.then_inc(S("am_ready"), 1)

            def sum_rows(Q, h):
                for k in range(4):
                    if due(Q * 4 + k - 3):
                        pe.wait_ge(S("flushed"), Q * 4 + k - 3)
                    pe.wait_ge(S("weighted"), Q * 4 + k + 1)
                    m.matmul(bank[3 + k][:, :AC], seg1[:, h, k, :], pay[:, h, k, :AC], start=True, stop=True)\
                        .then_inc(S("att_summed"), 1)

            def attend(i):
                for h in range(4):
                    Q = 4 * i + h
                    look_up(Q + 1, (h + 1) % 2)
                    turn_onehot(Q + 2, (h + 2) % 4)
                    sum_rows(Q, h)
            pe.wait_ge(S("tbl_ready"), 1)
            turn_onehot(0, 0)
            turn_onehot(1, 1)
            look_up(0, 0)
            looped(pe, EC // 16, attend)
            look_up(TA // 4 - 1, 1)
            sum_rows(TA // 4 - 2, 0)
            sum_rows(TA // 4 - 1, 1)

            def turn_all(n, ready):
                pe.wait_ge(S(ready), 1)
                for tt in range(NT):
                    if due(tt - 1):
                        pe.wait_ge(S("xt_copied"), n * NT + tt - 1)
                    for k in range(2):
                        last = m.transpose(bank[tt % 2][:, k * P:(k + 1) * P], xn[:, tt, k * P:(k + 1) * P], ident)
                    last.then_inc(S("xn_all"), 1)

            def two_products(n):
                def up(c, m_):
                    for j in range(8):
                        if due(c * 8 + j - 3):
                            pe.wait_ge(S("hid_ready"), n * 56 + c * 8 + j - 3)
                        for k in range(2):
                            last = m.matmul(bank[j % 4][:, :m_], w1_sb[:, k, j * P:(j + 1) * P], xt[:, k, ds(c * 512, m_)],
                                            start=(k == 0), stop=(k == 1))
                        last.then_inc(S("up_done"), 1)

                def down(c, h, m_):
                    pe.wait_ge(S("hid_ready"), n * 56 + c * 8 + 8)
                    for q in range(m_ // P):
                        if due(c * 4 + q - 3):
                            pe.wait_ge(S("tok_added"), n * NT + c * 4 + q - 3)
                        for j in range(8):
                            last = m.matmul(bank[4 + q][:, :D], hid_sb[:, h, j, q * P:(q + 1) * P], w2_sb[:, j, :],
                                            start=(j == 0), stop=(j == 7))
                        last.then_inc(S("tok_done"), 1)
                pe.wait_ge(S("xt_copied"), n * NT + NT)
                up(0, 512)
                up(1, 512)
                down(0, 0, 512)
                with pe.Fori(1, 3) as i:
                    up(2 * i, 512)
                    down(2 * i - 1, 1, 512)
                    up(2 * i + 1, 512)
                    down(2 * i, 0, 512)
                up(6, NP_ - 6 * 512)
                down(5, 1, 512)
                down(6, 0, NP_ - 6 * 512)

            turn_all(0, "xn2_ready")
            pe.wait_ge(S("router_ready"), 1)
            m.transpose(bank[7][:NT, :P], tok_w, ident).then_inc(S("router_pe"), 1)
            pe.wait_ge(S("mod_w_loaded"), 48)
            pe.wait_ge(S("router_turned"), 1)
            two_products(0)
            for l in range(LAYERS):
                if l == 0:
                    pe.wait_ge(S("edge_w_ready"), 1)
                    pe.wait_ge(S("tok_added"), NT)
                else:
                    pe.wait_ge(S("updated"), (l - 1) * NT + NT)

                def turn(Q, h, n):
                    if due(Q - 1):
                        pe.wait_ge(S("attr_ready"), l * QB + Q - 1)
                    pe.wait_ge(S(f"rec_loaded{h}"), l * 16 * turns(h) + n * 16 + 16)
                    for k in range(4):
                        last = m.transpose(bank[h % 2][:KA, 0:256].bitcast(BF16)[:, k * P:(k + 1) * P],
                                           recb[:, h, k, 0:KA], ident_b)
                    last.then_inc(S("rec_turned"), 1)

                def sums(Q, h):
                    pe.wait_ge(S("seg_ready"), l * QB + Q + 1)
                    for k in range(4):
                        pe.wait_ge(S("msg_ready"), l * 2 * QB + 2 * Q + k // 2 + 1)
                        if due(Q * 4 + k - 3):
                            pe.wait_ge(S("flushed_b"), l * TB + Q * 4 + k - 3)
                        m.matmul(bank[4 + k][:, :AC], oneh[:, h, k, :], msg[:, h, k, :], start=True, stop=True)\
                            .then_inc(S("summed"), 1)

                def edges(i, quads=4):
                    for h in range(quads):
                        Q = 4 * i + h
                        pe.wait_ge(S("attr_ready"), l * QB + Q + 1)
                        for j in range(2):
                            if due(2 * Q + j - 1):
                                pe.wait_ge(S("multiplied"), l * 2 * QB + 2 * Q + j - 1)
                            for k in (2 * j, 2 * j + 1):
                                o_ = bank[2 + j][:, (k % 2) * D:(k % 2 + 1) * D]
                                m.matmul(o_, at[:KA, h % 2, k * P:(k + 1) * P], we[:KA, 0, :], start=True, stop=False)
                                m.matmul(o_, at[:64, h % 2, k * P:(k + 1) * P], we[:64, 1, :], start=False, stop=False)
                                last = m.matmul(o_, at[:32, h % 2, k * P:(k + 1) * P], we[:32, 2, :], start=False, stop=True)
                            last.then_inc(S("projected"), 1)
                        if quads == 4:
                            turn(Q + 2, (h + 2) % 4, i + (h + 2) // 4)
                        if not (isinstance(i, int) and Q == 0):
                            sums(Q - 1, (h - 1) % 2)
                turn(0, 0, 0)
                turn(1, 1, 0)
                looped(pe, TB // 16, edges)
                edges(TB // 16, TB // 4 % 4)
                sums(TB // 4 - 1, 1)

                pe.wait_ge(S("layer_w_loaded"), 16 * 13)
                pe.wait_ge(S("flushed_b"), l * TB + TB)

                def turn_flat(tt, h):
                    pe.wait_ge(S("flat_ready"), l * NT + tt + 1)
                    if due(2 * tt - 2):
                        pe.wait_ge(S("turn_copied"), l * 2 * NT + 2 * tt - 2)
                    for b in range(2):
                        for r in range(4):
                            last = m.transpose(bank[2 * h + b][:, r * P:(r + 1) * P],
                                               flat[:, h, 2 * b + r // 2, (r % 2) * P:(r % 2 + 1) * P], ident)
                        last.then_inc(S("flat_turned"), 1)

                def apply(tt, h):
                    pe.wait_ge(S("turn_copied"), l * 2 * NT + 2 * tt + 2)
                    if due(tt - 1):
                        pe.wait_ge(S("updated"), l * NT + tt - 1)
                    o_ = bank[4 + h][:, :D]
                    for r in range(8):
                        m.matmul(o_, turned[:, h, r * P:(r + 1) * P], lw[:, l, r, :], start=(r == 0), stop=False)
                    m.matmul(o_, ones[0:1, :], vecs[0:1, l, :], start=False, stop=True).then_inc(S("applied"), 1)
                turn_flat(0, 0)
                turn_flat(1, 1)
                apply(0, 0)
                with pe.Fori(1, NT // 2) as i:
                    turn_flat(2 * i, 0)
                    apply(2 * i - 1, 1)
                    turn_flat(2 * i + 1, 1)
                    apply(2 * i, 0)
                turn_flat(NT - 1, 0)
                apply(NT - 2, 1)
                apply(NT - 1, 0)
            pe.wait_ge(S("xn4_ready"), 1)
            pe.wait_ge(S("gate_w_loaded"), 32)
            for k in range(2):
                for tt in range(NT):
                    last = m.matmul(bank[7][:, k:k + 1], xn[:, tt, k * P:(k + 1) * P], ones[:, 0:1],
                                    start=(tt == 0), stop=(tt == NT - 1))
            last.then_inc(S("mean_summed"), 1)
            pe.wait_ge(S("mean_ready"), 1)
            for k in range(2):
                last = m.matmul(bank[6][0:1, 0:NE], small[:, 490 + k:491 + k], wr_sb[:, k, :], start=(k == 0), stop=(k == 1))
            last.then_inc(S("logits_made"), 1)
            turn_all(1, "xn4_ready")
            pe.wait_ge(S("top_ready"), 1)
            m.matmul(bank[5][:, 0:2], ones[0:1, :], gate[0:1, 56:58], start=True, stop=True).then_inc(S("top_spread"), 1)
            pe.wait_ge(S("moe_w_loaded"), 128)
            pe.wait_ge(S("moe_w_scaled"), 1)
            two_products(1)

        @block.vector
        def _(dve):
            v = nc.vector
            st = Steps(dve, "dve_step")
            dve.wait_ge(S("p_const"), 11)
            v.tensor_scalar(ident, iota, iota_col, None, ALU.is_equal).then_inc(S("d_const"), 1)
            v.tensor_scalar(ident_b, iota, iota_col, None, ALU.is_equal).then_inc(S("d_const"), 1)
            v.tensor_scalar(tri, iota, iota_col, None, ALU.is_gt).then_inc(S("d_const"), 1)
            v.tensor_scalar(tri_b, iota, iota_col, None, ALU.is_gt).then_inc(S("const_ready"), 1)
            dve.wait_ge(S("ids_loaded"), 48)
            v.tensor_single_scalar(hi_i, src_i, 7, ALU.logical_shift_right).then_inc(S("dve_step"), 1); st.n += 1
            v.tensor_single_scalar(lo_i, src_i, 127, ALU.bitwise_and).then_inc(S("dve_step"), 1); st.n += 1
            st.did(v.tensor_copy(itemB[:, :, 0].bitcast(INT32), src_i))
            st.did(v.tensor_copy(itemA[:, :, 0], dst_i))
            st.settle()
            st.did(v.tensor_copy(keyA, hi_i))
            st.did(v.tensor_copy(itemA[:, :, 1], lo_i))
            st.settle()
            st.did(v.tensor_single_scalar(hi_i, dst_i, 7, ALU.logical_shift_right))
            st.did(v.tensor_single_scalar(lo_i, dst_i, 127, ALU.bitwise_and))
            st.settle()
            st.did(v.scalar_tensor_tensor(keyB, rel_i, float(NT), hi_i, ALU.mult, ALU.add))
            st.did(v.tensor_copy(itemB[:, :, 1], lo_i))
            st.settle()

            def rank(s):
                nb, cols, n_, T = s["nb"], s["cols"], s["n"], s["T"]

                def onehot(k, q):
                    kr = kring[k][:, :cols * nb].rearrange("p (c b) -> p c b", b=nb)
                    io = iota_b[:EP, 0:nb].rearrange("p (a b) -> p a b", a=1).broadcast_to([EP, cols, nb])
                    ky = s["key"][:, ds(q * cols, cols)].rearrange("p (c a) -> p c a", a=1).broadcast_to([EP, cols, nb])
                    return v.tensor_tensor(kr, io, ky, ALU.is_equal)

                def count_body(i):
                    for k in range(4):
                        q = i * 4 + k
                        if due(q - 3):
                            dve.wait_ge(S("counted"), n_ * 80 + q - 3)
                        onehot(k, q).then_inc(S("onehot"), 1)
                looped(dve, s["bodies"], count_body)
                half = EC // 2
                dve.wait_ge(S("counted"), n_ * 80 + s['bodies'] * 4)
                st.did(v.tensor_copy(cnt[:nb, :half], bank[0][:nb, :half]))
                st.run(v.tensor_copy(cnt[:nb, half:], bank[1][:nb, :half]))
                v.tensor_tensor_scan(cum[:nb], cnt[:nb], zeros[:nb], 0.0, ALU.add, ALU.add).then_inc(S("counts_read"), 1)
                dve.wait_ge(S("counts_read"), n_ * 1 + 1)
                ti = small[:nb, 2:3].bitcast(INT32)
                st.run(v.tensor_scalar(ti, cum[:nb, EC - 1:EC], 127.0, None, ALU.add))
                st.run(v.tensor_single_scalar(small[:nb, 3:4].bitcast(INT32), ti, 7, ALU.logical_shift_right))
                v.tensor_copy(small[:nb, 1:2], small[:nb, 3:4].bitcast(INT32)).then_inc(S("tiles_ready"), 1)
                dve.wait_ge(S("tilesum"), n_ * 1 + 1)
                dve.wait_ge(S("tiles_ready"), n_ * 1 + 1)
                st.did(v.tensor_scalar(small[:nb, 4:5], bank[2][:nb, 0:1], 128.0, None, ALU.mult))
                st.run(v.tensor_tensor(small[:nb, 5:6], bank[2][:nb, 0:1], small[:nb, 1:2], ALU.add))
                v.scalar_tensor_tensor(cum[:nb], cum[:nb], small[:nb, 4:5], cnt[:nb], ALU.add, ALU.subtract)\
                    .then_inc(S("basecol_ready"), 1)
                v.tensor_scalar(winge[:nb, :T], iotaT[:nb, :T], small[:nb, 5:6], None, ALU.is_ge).then_inc(S("winge_ready"), 1)
                dve.wait_ge(S("base_turned"), n_ * 1 + 1)
                n1 = min(8, 512 // nb) * nb
                if n1 < 8 * nb:
                    st.did(v.tensor_copy(base_sb[:100, n1:8 * nb], bank[4][:100, n1 - 450:8 * nb - 450]))
                st.run(v.tensor_copy(base_sb[:100, :n1], bank[3][:100, :n1]))
                dve.sem_inc(S("base_ready"), 1)
                dve.wait_ge(S("win_summed"), n_ * 1 + 1)
                w = winbc
                st.did(v.tensor_scalar(w[:, :512], bank[5][:, :], float(nb), None, ALU.min))
                st.run(v.tensor_scalar(w[:, 512:T], bank[6][:, :T - 512], float(nb), None, ALU.min))
                pair = w[0:1, :T].rearrange("p (a b) -> p a b", b=2)
                st.run(v.scalar_tensor_tensor(s["winp"], pair[:, :, 1], nb + 1.0, pair[:, :, 0], ALU.mult, ALU.add))

                def rank_body(i):
                    for k in range(4):
                        q = i * 4 + k
                        onehot(k, q).then_inc(S("onehot2"), 1)
                    for k in range(4):
                        q = i * 4 + k
                        dve.wait_ge(S("ranked"), n_ * 80 + q + 1)
                        v.tensor_tensor(prod[k % 2][:, :cols * nb], bank[k % 2][:EP, :cols * nb],
                                        kring[k][:, :cols * nb], ALU.mult).then_inc(S("rank_masked"), 1)
                        dve.wait_ge(S("rank_masked"), n_ * 80 + q + 1)
                        v.tensor_reduce(slotg[:, k * cols:(k + 1) * cols],
                                        prod[k % 2][:, :cols * nb].rearrange("p (c b) -> p c b", b=nb),
                                        X_AXIS, ALU.add).then_inc(S("rank_summed"), 1)
                    dve.wait_ge(S("rank_summed"), n_ * 80 + i * 4 + 4)
                    v.tensor_scalar(slotf[:, ds(i * 4 * cols, 4 * cols)], slotg[:, :4 * cols], 0.0, None, ALU.add)\
                        .then_inc(S("slots_kept"), 1)
                    dve.wait_ge(S("slots_kept"), n_ * 20 + i + 1)
                looped(dve, s["bodies"], rank_body)
                st.run(v.tensor_copy(hi_i, slotf))
                st.run(v.tensor_single_scalar(lo_i, hi_i, 127, ALU.bitwise_and))
                st.run(v.tensor_single_scalar(hi_i, hi_i, 7, ALU.logical_shift_right))
                v.scalar_tensor_tensor(s["addr"], lo_i, float(T), hi_i, ALU.mult, ALU.add).then_inc(S("addr_ready"), 1)
                dve.wait_ge(S("addr_ready"), n_ * 1 + 1)
            def layer_norm(n, dst, done, src=x_sb):
                for tt in range(NT):
                    st.did(v.bn_stats(stats[:, tt, :], src[:, tt, :]))
                st.settle()
                for tt in range(NT):
                    st.did(v.bn_aggr(mv[:, tt, :], stats[:, tt, :]))
                st.settle()
                v.tensor_scalar(sd, mv[:, :, 1], EPS, None, ALU.add).then_inc(S("var_ready"), 1)
                if due(n):
                    dve.wait_ge(S("std_ready"), n)
                st.run(v.reciprocal(rs, sd))
                for tt in range(NT):
                    st.did(v.tensor_scalar(dst[:, tt, :], src[:, tt, :], mv[:, tt, 0:1], rs[:, tt:tt + 1],
                                           ALU.subtract, ALU.mult))
                st.settle()
                dve.sem_inc(S(done), 1)

            dve.wait_ge(S("x_loaded"), 32)
            dve.wait_ge(S("filled0"), 16)
            layer_norm(1, xn, "xn_ready")
            rank(SORT[0])
            dve.wait_ge(S("att_w_loaded"), 96)
            st.did(v.memset(htab[:, :, D:D + 1], 1.0))
            for tt in range(NT):
                dve.wait_ge(S("h_made"), tt + 1)
                v.tensor_tensor(htab[:, tt, :D], bank[2 + tt % 2][:, :D], vecs[:, 0, :], ALU.add).then_inc(S("h_read"), 1)
            dve.wait_ge(S("h_read"), NT)
            for c, dst in ((1, a1), (2, a2)):
                for t0 in range(0, NT, 5):
                    vb = vecs[:, c:c + 1, :].broadcast_to([P, 5, D])
                    st.run(v.tensor_tensor(dots, htab[:, t0:t0 + 5, :D], vb, ALU.mult))
                    st.run(v.tensor_reduce(dst[:, t0:t0 + 5], dots, X_AXIS, ALU.add))
            dve.sem_inc(S("dots_done"), 1)
            st.did(v.tensor_scalar(a1, a1, small[:, 320:321], None, ALU.add))
            st.run(v.tensor_scalar(a2, a2, small[:, 321:322], None, ALU.add))
            st.run(v.tensor_reduce(gmin[:, 0:1], a2, X_AXIS, ALU.min, negate=True))
            dve.sem_inc(S("gmin_part"), 1)
            st.did(v.tensor_scalar(winA, winbc[:, :TA], float(BKT_A - 1), None, ALU.min))
            rank(SORT[1])
            dve.wait_ge(S("gmin_all"), 1)
            st.did(v.tensor_scalar(a1, a1, gmin[:, 1:2], None, ALU.subtract))
            st.run(v.tensor_scalar(htab[:, :, D + 1], a2, gmin[:, 1:2], None, ALU.add))
            dve.sem_inc(S("htab_ready"), 1)
            st.run(v.memset(ta1, 0.0))
            for w in range(NT):
                st.run(v.tensor_scalar(tx, winA, float(w), a1[:, w:w + 1], ALU.is_equal, ALU.mult))
                st.run(v.tensor_tensor(ta1, ta1, tx, ALU.add))
            st.did(v.memset(tx[:, 0:1], 0.0))
            st.did(v.memset(ty[:, TA - 1:], 0.0))
            st.did(v.tensor_tensor(tx[:, 1:], winA[:, 1:], winA[:, :TA - 1], ALU.is_equal))
            st.did(v.tensor_tensor(ty[:, :TA - 1], winA[:, 1:], winA[:, :TA - 1], ALU.is_equal))
            st.did(v.memset(acc_mem[:, :(BKT_A + 1) * AC], 0.0))
            st.run(v.memset(stB_mem, 0.0))
            st.run(v.memset(stBb[:, :, :, 96:99], 1.0))

            def select(i):
                def maxima(Q, h):
                    dve.wait_ge(S("v_turned"), Q + 1)
                    if not isinstance(Q, int):
                        dve.sem_inc(S("passed"), 1)
                    v.tensor_reduce(vmax[:, ds(Q * 4, 4)], bank[h].rearrange("p (k e) -> p k e", k=4), X_AXIS, ALU.max)\
                        .then_inc(S("v_maxed"), 1)
                for h in range(2):
                    Q = 2 * i + h
                    dve.wait_ge(S(f"gathered{h}"), i * 64 + 64)
                    dve.wait_ge(S("gidx_staged"), Q + 1)
                    if due(Q - 1):
                        dve.wait_ge(S("v_turned"), Q - 1)
                    for k in range(4):
                        last = v.tensor_scalar(vsel[:, h, k, :], iota, gseg[:, h, k:k + 1], hrow[:, h, k, HC - 1:HC],
                                               ALU.is_equal, ALU.mult)
                    last.then_inc(S("v_ready"), 1)
                    v.tensor_scalar(recA[:, ds(Q * 4, 4), 0], hrow[:, h, :, HC - 1], 0.0, None, ALU.add).then_inc(S("a2_kept"), 1)
                    if not (isinstance(i, int) and Q == 0):
                        maxima(Q - 1, 1 - h)
                if isinstance(i, int) and i == TA // 8 - 1:
                    maxima(TA // 4 - 1, 1)
            looped(dve, TA // 8, select)
            dve.wait_ge(S("v_maxed"), TA // 4)
            dve.wait_ge(S("a2_kept"), TA // 4)
            st.run(v.tensor_tensor_scan(tm, tx, vmax, 0.0, ALU.mult, ALU.max))
            st.run(v.tensor_tensor_scan(vmax[:, ::-1], ty[:, ::-1], tm[:, ::-1], 0.0, ALU.mult, ALU.max))
            st.run(v.tensor_tensor(tx, vmax, ta1, ALU.add))
            st.run(v.scalar_tensor_tensor(tm, tx, 0.01, tx, ALU.mult, ALU.max))
            for c, src in enumerate((ta1, tm)):
                st.run(v.tensor_copy(tbl[:, :, c, 0], src))
                st.run(v.tensor_tensor(src, src, tbl[:, :, c, 0], ALU.subtract))
                st.run(v.tensor_copy(tbl[:, :, c, 1], src))
                st.run(v.tensor_tensor(tbl[:, :, c, 2], src, tbl[:, :, c, 1], ALU.subtract))
            dve.sem_inc(S("tbl_ready"), 1)
            dve.sem_inc(S("stB_ready"), 1)

            def window_pair(Q, j, winp):
                return dve.value_load(winp[0:1, ds(Q * 2 + j, 1)])

            def flush(Q, k, pair, base, banks, summed, flushed, off):
                w = pair % base if k % 2 == 0 else pair // base
                if due(Q * 4 + k):
                    dve.wait_ge(flushed, off + Q * 4 + k)
                dve.wait_ge(summed, off + Q * 4 + k + 1)
                a_ = acc_mem[:, ds(w * AC, AC)]
                v.tensor_tensor(a_, a_, bank[banks + k][:, :AC], ALU.add).then_inc(flushed, 1)

            def flush_A(Q, k, pair):
                flush(Q, k, pair, BKT_A + 1, 3, S("att_summed"), S("flushed"), 0)

            def onehot(Q, h):
                if due(4 * Q - 12):
                    dve.wait_ge(S("att_summed"), 4 * Q - 12)
                v.tensor_tensor(seg1[:, h, :, :], iota.rearrange("p (a s) -> p a s", a=1).broadcast_to([P, 4, P]),
                                recA[:, ds(Q * 4, 4), 1:2].broadcast_to([P, 4, P]), ALU.is_equal)\
                    .then_inc(S("oneh_ready"), 1)

            def logit(Q, h):
                dve.wait_ge(S("am_ready"), Q + 1)
                v.tensor_reduce(amv[:, h, 0:8], bank[2 + 5 * h][:, :24].rearrange("p (n s) -> p n s", s=3),
                                X_AXIS, ALU.add).then_inc(S("am_read"), 1)
                am = amv[:, h, 0:8].rearrange("p (k c) -> p k c", c=2)
                dve.wait_ge(S("am_read"), Q + 1)
                v.tensor_tensor(amv[:, h, 8:12], am[:, :, 0], recA[:, ds(Q * 4, 4), 0], ALU.add).then_inc(S("lin_step"), 1)
                dve.wait_ge(S("lin_step"), Q * 2 + 1)
                v.scalar_tensor_tensor(amv[:, h, 8:12], amv[:, h, 8:12], 0.01, amv[:, h, 8:12], ALU.mult, ALU.max)\
                    .then_inc(S("lin_step"), 1)
                dve.wait_ge(S("lin_step"), Q * 2 + 2)
                v.tensor_tensor(amv[:, h, 12:16], amv[:, h, 8:12], am[:, :, 1], ALU.subtract).then_inc(S("logit_ready"), 1)

            def attr_low(Q, h):
                dve.wait_ge(S("act_stepB"), Q * 4 + 4)
                v.tensor_tensor(stBb[:, h, :, 64:96], attr_r, stBb[:, h, :, 32:64], ALU.subtract)\
                    .then_inc(S("attr_split"), 1)

            def attend(i):
                for h in range(4):
                    Q = 4 * i + h
                    first = isinstance(i, int) and Q == 0
                    if not first:
                        pair = window_pair(Q - 1, 0, winpA)
                        flush_A(Q - 1, 0, pair)
                    logit(Q + 1, (h + 1) % 2)
                    if not first:
                        flush_A(Q - 1, 1, pair)
                    if not (isinstance(i, int) and Q == EC // 4 - 1):
                        onehot(Q + 3, (h + 3) % 4)
                    if not first:
                        pair = window_pair(Q - 1, 1, winpA)
                        flush_A(Q - 1, 2, pair)
                        attr_low(Q - 1, (h - 1) % 4)
                        flush_A(Q - 1, 3, pair)
                    if due(Q):
                        dve.wait_ge(S("attr_split"), Q)
                    dve.wait_ge(S("attr_hi"), Q + 1)
                    v.tensor_tensor(attr_r, attr_in[:, h % 2, :, :], stBb[:, h, :, 0:32], ALU.subtract)\
                        .then_inc(S("attr_rest"), 1)
            for h in range(2):
                dve.wait_ge(S(f"kept{h}"), TA // 8 * 16)
            for q in range(3):
                onehot(q, q)
            logit(0, 0)
            looped(dve, EC // 16, attend)
            attr_low(EC // 4 - 1, 3)
            for q in (TA // 4 - 3, TA // 4 - 2, TA // 4 - 1):
                for k in range(4):
                    flush_A(q, k, window_pair(q, k // 2, winpA))
                if q == TA // 4 - 3:
                    logit(TA // 4 - 1, 1)
            dve.wait_ge(S("flushed"), TA)
            st.run(v.tensor_scalar(rs, acc[:, 0:NT, D], 0.0, None, ALU.is_equal))
            st.run(v.tensor_tensor(rs, rs, acc[:, 0:NT, D], ALU.add))
            st.run(v.reciprocal(rs, rs))
            for tt in range(NT):
                st.did(v.scalar_tensor_tensor(x_sb[:, tt, :], acc[:, tt, :D], rs[:, tt:tt + 1], x_sb[:, tt, :],
                                              ALU.mult, ALU.add))
            st.settle()
            dve.sem_inc(S("x1_ready"), 1)

            def tokens(n, last_):
                def tile(tt, q):
                    dve.wait_ge(S("tok_done"), n * NT + tt + 1)
                    y = ycol[:, q % 2, :]
                    v.tensor_tensor(y, bank[4 + q][:, :D], vecs[:, 1, :], ALU.add).then_inc(S("tok_added"), 1)
                    dve.wait_ge(S("tok_added"), n * NT + tt + 1)
                    last_(tt, y)
                for q in range(4):
                    tile(q, q)
                with dve.Fori(1, NT // 4) as i:
                    for q in range(4):
                        tile(i * 4 + q, q)
                tile(NT - 1, 0)

            layer_norm(2, xn, "xn2_ready")
            dve.wait_ge(S("mod_v_loaded"), 48)
            for t0 in range(0, NT, 5):
                st.run(v.tensor_tensor(dots, xn[:, t0:t0 + 5, :], vecs[:, 0:1, :].broadcast_to([P, 5, D]), ALU.mult))
                st.run(v.tensor_reduce(tok_w[:, t0:t0 + 5], dots, X_AXIS, ALU.add))
            st.did(v.tensor_scalar(real, iota_col, float(LAST), None, ALU.is_lt))
            st.did(v.tensor_scalar(low, iota, iota_col, None, ALU.is_lt))
            st.run(v.tensor_scalar(tok_w, tok_w, br_sb, None, ALU.add))
            st.run(v.tensor_scalar(tok_w[:, NT - 1:], tok_w[:, NT - 1:], real, None, ALU.mult))
            st.run(v.tensor_scalar(coef[:, 0:1], real, -1.0, 3.0e38, ALU.add, ALU.mult))
            st.run(v.tensor_tensor(tok_w[:, NT - 1:], tok_w[:, NT - 1:], coef[:, 0:1], ALU.add))
            dve.sem_inc(S("router_ready"), 1)
            dve.wait_ge(S("router_pe"), 1)
            st.run(v.tensor_copy(w_turn[:NT, :], bank[7][:NT, :P]))
            dve.sem_inc(S("router_turned"), 1)
            dve.wait_ge(S("router_row"), 16)
            st.run(v.memset(n_gt, 0.0))
            for tt in range(NT):
                w_ = tok_w[:, tt:tt + 1]
                for c, (lo_, n_, op) in enumerate(((0, tt * P, ALU.is_ge), (tt * P, NP_ - tt * P, ALU.is_gt))):
                    if n_:
                        st.run(v.scalar_tensor_tensor(seen[:, :n_], w_row[:, lo_:lo_ + n_], w_, ones[:, 0:1].broadcast_to([P, n_]),
                                                      op, ALU.mult, accum_out=n_gt[:, c, tt:tt + 1]))
                st.run(v.scalar_tensor_tensor(seen[:, :P], w_row[:, tt * P:(tt + 1) * P], w_, low, ALU.is_equal, ALU.mult,
                                              accum_out=n_gt[:, 2, tt:tt + 1]))
            st.run(v.tensor_tensor(coef, n_gt[:, 0, :], n_gt[:, 1, :], ALU.add))
            st.run(v.tensor_tensor(coef, coef, n_gt[:, 2, :], ALU.add))
            st.run(v.scalar_tensor_tensor(coef, coef, float(TOPK), tok_w, ALU.is_lt, ALU.mult))

            def gated(tt, y):
                v.scalar_tensor_tensor(y, y, coef[:, ds(tt, 1)], xn_mem[:, ds(tt * D, D)], ALU.mult, ALU.add)\
                    .then_inc(S("gated"), 1)
                dve.wait_ge(S("gated"), tt + 1)
                xx = x_sb[:, ds(tt, 1), :].rearrange("p t d -> p (t d)")
                v.tensor_tensor(xx, xx, y, ALU.add).then_inc(S("x2_added"), 1)
            tokens(0, gated)
            dve.wait_ge(S("x2_added"), NT)
            dve.sem_inc(S("x2_ready"), 1)
            dve.wait_ge(S("edge_w_loaded"), 64)
            st.run(v.tensor_copy(we[:KA, 0, :], we_f[:KA, :]))
            st.run(v.tensor_tensor(we_r[:KA, :], we_f[:KA, :], we[:KA, 0, :], ALU.subtract))
            st.run(v.tensor_copy(we[:KA, 1, :], we_r[:KA, :]))
            st.run(v.tensor_tensor(we[:KA, 2, :], we_r[:KA, :], we[:KA, 1, :], ALU.subtract))
            for c in range(2):
                msk = small[:, 0:1]
                st.run(v.tensor_scalar(msk, iota_col, float(97 + c), None, ALU.is_equal))
                st.run(v.tensor_scalar(we_r[:KA, :], we[:KA, 1 + c, :], msk[:KA], None, ALU.mult))
                st.run(v.tensor_scalar(msk, iota_col, float(97 + c), None, ALU.not_equal))
                st.run(v.scalar_tensor_tensor(we[:KA, 0, :], we[:KA, 0, :], msk[:KA], we_r[:KA, :], ALU.mult, ALU.add))
            st.did(v.memset(msg[:, :, :, D:AC], 1.0))
            st.did(v.memset(acc_mem, 0.0))
            st.settle()
            dve.sem_inc(S("edge_w_ready"), 1)
            layer_norm(3, xn, "state_ready")
            for l in range(LAYERS):
                if l:
                    dve.wait_ge(S("flat_ready"), (l - 1) * NT + NT)
                    st.did(v.memset(acc_mem[:, 38 * AC:], 0.0))
                    dve.wait_ge(S("acc_half"), l - 1 + 1)
                    st.settle()

                def flush_B(Q, k, pair):
                    flush(Q, k, pair, BKT_B + 1, 4, S("summed"), S("flushed_b"), l * TB)

                def compare(Q, h, n):
                    if due(4 * Q - 4):
                        dve.wait_ge(S("summed"), l * TB + 4 * Q - 4)
                    dve.wait_ge(S(f"rec_loaded{h}"), l * 16 * turns(h) + n * 16 + 16)
                    v.tensor_tensor(oneh[:, h % 2, :, :], iota.rearrange("p (a s) -> p a s", a=1).broadcast_to([P, 4, P]),
                                    rec[:, h, :, W_SEG:W_SEG + 1].broadcast_to([P, 4, P]), ALU.is_equal)\
                        .then_inc(S("seg_ready"), 1)

                def multiply(Q, h, j, i):
                    dve.wait_ge(S(f"sources{h}"), l * 64 * turns(h) + i * 64 + 64)
                    dve.wait_ge(S("projected"), l * 2 * QB + 2 * Q + j + 1)
                    if due(4 * Q - 4):
                        dve.wait_ge(S("summed"), l * TB + 4 * Q - 4)
                    v.tensor_tensor(msg[:, h % 2, 2 * j:2 * j + 2, :D], bank[2 + j].rearrange("p (k d) -> p k d", k=2),
                                    xg[:, h, 2 * j:2 * j + 2, :], ALU.mult).then_inc(S("multiplied"), 1)

                def edges(i, quads=4):
                    for h in range(quads):
                        Q = 4 * i + h
                        first = isinstance(i, int) and Q == 0
                        multiply(Q, h, 0, i)
                        if not first:
                            pair = window_pair(Q - 1, 0, winpB)
                            flush_B(Q - 1, 0, pair)
                        multiply(Q, h, 1, i)
                        if not first:
                            flush_B(Q - 1, 1, pair)
                        compare(Q, h, i)
                        if not first:
                            pair = window_pair(Q - 1, 1, winpB)
                            flush_B(Q - 1, 2, pair)
                            flush_B(Q - 1, 3, pair)
                looped(dve, TB // 16, edges)
                edges(TB // 16, TB // 4 % 4)
                for k in range(4):
                    flush_B(TB // 4 - 1, k, window_pair(TB // 4 - 1, k // 2, winpB))
                dve.wait_ge(S("flushed_b"), l * TB + TB)
                if l == 0:
                    st.run(v.tensor_scalar(inv, acc[:, 0:BKT_B, D], 1.0, None, ALU.max))
                    st.run(v.reciprocal(inv, inv))
                dve.sem_inc(S("inv_ready"), 1)

                def copy_turned(tt, h):
                    if due(tt - 1):
                        dve.wait_ge(S("applied"), l * NT + tt - 1)
                    for b in range(2):
                        dve.wait_ge(S("flat_turned"), l * 2 * NT + 2 * tt + b + 1)
                        v.tensor_copy(turned[:, h, b * 512:(b + 1) * 512], bank[2 * h + b]).then_inc(S("turn_copied"), 1)

                def update(tt, h):
                    dve.wait_ge(S("applied"), l * NT + tt + 1)
                    xx = xn_mem[:, ds(tt * D, D)]
                    v.scalar_tensor_tensor(xx, bank[4 + h][:, :D], 0.0, xx, ALU.max, ALU.add).then_inc(S("updated"), 1)
                copy_turned(0, 0)
                copy_turned(1, 1)
                update(0, 0)
                with dve.Fori(1, NT // 2) as i:
                    copy_turned(2 * i, 0)
                    update(2 * i - 1, 1)
                    copy_turned(2 * i + 1, 1)
                    update(2 * i, 0)
                copy_turned(NT - 1, 0)
                update(NT - 2, 1)
                update(NT - 1, 0)
                dve.wait_ge(S("updated"), l * NT + NT)
                if l < LAYERS - 1:
                    dve.sem_inc(S("state_ready"), 1)
            st.run(v.tensor_scalar(xn[:, NT - 1, :], xn[:, NT - 1, :], real, None, ALU.mult))
            for t0 in range(0, NT, 5):
                st.did(v.tensor_tensor(x_sb[:, t0:t0 + 5, :], x_sb[:, t0:t0 + 5, :], xn[:, t0:t0 + 5, :], ALU.add))
            st.settle()
            dve.sem_inc(S("x3_ready"), 1)
            layer_norm(4, xn, "xn4_ready")
            dve.wait_ge(S("gate_w_loaded"), 32)
            dve.wait_ge(S("mean_summed"), 1)
            st.run(v.tensor_scalar(small[:, 490:492], bank[7][:, 0:2], 1.0 / N, None, ALU.mult))
            dve.sem_inc(S("mean_ready"), 1)
            dve.wait_ge(S("logits_made"), 1)
            G = lambda a_, b_: gate[0:1, a_:b_]
            row8 = iota[0:1, 0:8]

            def softmax(dst, n):
                st.run(v.tensor_reduce(G(60, 61), dst, X_AXIS, ALU.max))
                st.run(v.tensor_scalar(dst, dst, G(60, 61), None, ALU.subtract))
                dve.sem_inc(S("gate_exp"), 1)
                if due(n):
                    dve.wait_ge(S("gate_exp_done"), n)
                st.run(v.tensor_reduce(G(60, 61), dst, X_AXIS, ALU.add))
                st.run(v.reciprocal(G(60, 61), G(60, 61)))
                st.run(v.tensor_scalar(dst, dst, G(60, 61), None, ALU.mult))
            st.run(v.tensor_tensor(G(8, 16), bank[6][0:1, 0:8], G(0, 8), ALU.add))
            softmax(G(8, 16), 1)
            capacity = float(math.ceil(N * 1.25 / NE))
            st.run(v.tensor_scalar(G(16, 24), G(8, 16), float(N), 1e-30, ALU.mult, ALU.max))
            st.run(v.reciprocal(G(16, 24), G(16, 24)))
            st.run(v.tensor_scalar(G(16, 24), G(16, 24), capacity, 1.0, ALU.mult, ALU.min))
            st.run(v.tensor_tensor(G(24, 32), G(8, 16), G(16, 24), ALU.mult))
            softmax(G(24, 32), 2)
            for c in range(2):
                st.run(v.tensor_reduce(G(48 + c, 49 + c), G(24, 32), X_AXIS, ALU.max))
                st.run(v.tensor_scalar(G(32, 40), G(24, 32), G(48 + c, 49 + c), -100.0, ALU.is_equal, ALU.mult))
                st.run(v.tensor_tensor(G(32, 40), G(32, 40), row8, ALU.add))
                st.run(v.tensor_reduce(G(50 + c, 51 + c), G(32, 40), X_AXIS, ALU.min))
                st.run(v.tensor_scalar(G(50 + c, 51 + c), G(50 + c, 51 + c), 100.0, None, ALU.add))
                st.run(v.tensor_scalar(G(32, 40), row8, G(50 + c, 51 + c), -10.0, ALU.is_equal, ALU.mult))
                st.run(v.tensor_tensor(G(24, 32), G(24, 32), G(32, 40), ALU.add))
            st.run(v.tensor_copy(G(62, 64).bitcast(INT32), G(50, 52)))
            dve.sem_inc(S("chosen"), 1)
            st.run(v.tensor_tensor(G(40, 41), G(49, 50), G(48, 49), ALU.subtract))
            dve.sem_inc(S("gate_exp"), 1)
            dve.wait_ge(S("gate_exp_done"), 3)
            st.run(v.tensor_scalar(G(41, 42), G(40, 41), 1.0, None, ALU.add))
            st.run(v.reciprocal(G(56, 57), G(41, 42)))
            st.run(v.tensor_tensor(G(57, 58), G(40, 41), G(56, 57), ALU.mult))
            dve.sem_inc(S("top_ready"), 1)
            dve.wait_ge(S("top_spread"), 1)
            st.run(v.tensor_copy(small[:, 494:496], bank[5][:, 0:2]))
            dve.wait_ge(S("moe_w_loaded"), 128)
            for c in range(2):
                st.did(v.tensor_scalar(w2_sb[:, 4 * c:4 * c + 4, :], w2_sb[:, 4 * c:4 * c + 4, :], small[:, 494 + c:495 + c],
                                       None, ALU.mult))
            st.run(v.tensor_scalar(vecs[:, 0, :], vecs[:, 0, :], small[:, 494:495], None, ALU.mult))
            st.run(v.scalar_tensor_tensor(vecs[:, 1, :], vecs[:, 1, :], small[:, 495:496], vecs[:, 0, :], ALU.mult, ALU.add))
            dve.sem_inc(S("moe_w_scaled"), 1)

            def mixed(tt, y):
                xx = xn_mem[:, ds(tt * D, D)]
                v.tensor_tensor(xx, xx, y, ALU.add).then_inc(S("mixed"), 1)
            tokens(1, mixed)
            dve.wait_ge(S("mixed"), NT)
            layer_norm(5, xn, "norm_done", src=xn)
            dve.wait_ge(S("norm_w_loaded"), 32)
            for t0 in range(0, NT, 5):
                xx = xn[:, t0:t0 + 5, :]
                st.run(v.tensor_tensor(xx, xx, vecs[:, 2:3, :].broadcast_to([P, 5, D]), ALU.mult))
                st.run(v.tensor_tensor(xx, xx, vecs[:, 3:4, :].broadcast_to([P, 5, D]), ALU.add))
                st.run(v.tensor_tensor(x_sb[:, t0:t0 + 5, :], x_sb[:, t0:t0 + 5, :], xx, ALU.add))
            dve.sem_inc(S("out_ready"), 1)


INPUTS = ["x", "src", "dst", "edge_attr_32", "edge_type_3", "L0_gnn_b_layer", "L0_gnn_w_a1", "L0_gnn_b_a1",
          "L0_gnn_w_a2", "L0_gnn_b_a2", "L0_ffn_br", "L0_ffn_w1", "L0_ffn_w2", "L0_ffn_b2", "L1_gnn_weights",
          "L1_gnn_roots", "L1_gnn_biases", "L1_gnn_edge_w", "L1_gnn_edge_b", "L1_ffn_Wr", "L1_ffn_br", "L1_ffn_W1",
          "L1_ffn_W2", "L1_ffn_b2", "L1_ffn_gamma", "L1_ffn_beta"]


def laid_out(inputs):
    import numpy as np
    a = {name: np.ascontiguousarray(inputs[name]) for name in INPUTS}
    for name in ("L0_gnn_w_a1", "L0_gnn_w_a2"):
        a[name] = a[name].reshape(D)
    a["W_layer_t"] = np.ascontiguousarray(np.asarray(inputs["L0_gnn_W_layer"]).T)
    a["wr_mod"] = np.asarray(inputs["L0_ffn_wr"]).reshape(D)
    a["b1_mod"] = np.ascontiguousarray(np.asarray(inputs["L0_ffn_b1"]).reshape(HID // P, P).T)
    a["b1_moe"] = np.ascontiguousarray(np.asarray(inputs["L1_ffn_b1"]).reshape(NE, FE // P, P).transpose(0, 2, 1))
    return a


def kernel(**inputs):
    import concourse.bacc as bacc
    from concourse.bass_utils import run_bass_kernel_spmd

    nc = bacc.Bacc("TRN2", target_bir_lowering=False, num_devices=1)
    arrays = {f"in_{name}": a for name, a in laid_out(inputs).items()}
    t = {name[3:]: nc.dram_tensor(name, a.shape, mybir.dt.from_np(a.dtype), kind="ExternalInput").ap()
         for name, a in arrays.items()}
    out = nc.dram_tensor("out_0", (N, D), FP32, kind="ExternalOutput").ap()
    build(nc, t, out)
    r = run_bass_kernel_spmd(nc, [arrays], core_ids=[0])
    return r.results[0]["out_0"]
```

```python
import math
from contextlib import ExitStack

import concourse.bass as bass
from concourse import mybir

FP32 = mybir.dt.float32
BF16 = mybir.dt.bfloat16
INT32 = mybir.dt.int32
ALU = mybir.AluOpType
ACT = mybir.ActivationFunctionType
X_AXIS = mybir.AxisListType.X
ds = bass.ds

P = 128
N = 3125
D = 256
NT = -(-N // P)
NP_ = NT * P
LAST = N - (NT - 1) * P
E = 100000
EP, EC = 125, 800
R = 3
F_ATTR = 32
LAYERS = 3
EPS = 1e-5
TOPK = max(1, int(0.5 * N)) - 1
NE, FE = 8, 512
HID = 1024
BKT_A, BKT_B = NT, R * NT


def slots_tiles(buckets):
    return -(-((E + buckets * (P - 1)) // P) // 8) * 8


TA, TB = slots_tiles(BKT_A), slots_tiles(BKT_B)
QB = TB // 4
assert TB // 4 % 4 == 2
assert TA // 4 == EC // 4 + 2
RW = 64
W_SRC, W_SEG = 50, 51
KA = 3 * F_ATTR + 3
HC = D + 2
AC = D + 1


def build(nc, t, out):
    ctx = ExitStack()
    with ctx:
        def sb(name, shape, dt=FP32):
            return ctx.enter_context(nc.sbuf_tensor(name, shape, dt))[:]

        sems = {}

        def S(name):
            if name not in sems:
                sems[name] = ctx.enter_context(nc.semaphore(name))
            return sems[name]

        def turns(h):
            return (TB // 4 - h + 3) // 4

        def turns_A(h):
            return (TA // 4 - h + 3) // 4

        def dram(name, shape, dt=FP32):
            return nc.dram_tensor(name, shape, dt, kind="Internal").ap()

        def due(value):
            return not isinstance(value, int) or value > 0

        class Steps:

            def __init__(self, eng, name):
                self.eng, self.name, self.n = eng, name, 0

            def did(self, ins):
                ins.then_inc(S(self.name), 1)
                self.n += 1

            def settle(self):
                self.eng.wait_ge(S(self.name), self.n)

            def run(self, ins):
                self.did(ins)
                self.settle()

        def looped(eng, n, body):
            body(0)
            with eng.Fori(1, n - 1) as i:
                body(i)
            body(n - 1)

        x_sb = sb("x_sb", [P, NT, D])
        xn_mem = sb("xn_mem", [P, NT * D])
        xn = xn_mem.rearrange("p (t d) -> p t d", d=D)
        xt_mem = sb("xt_mem", [P, NT * HC])
        acc_mem = sb("acc_mem", [P, (BKT_B + 1) * AC])
        acc = acc_mem.rearrange("p (w c) -> p w c", c=AC)
        sort_mem = sb("sort_mem", [P, 7 * EC])
        keyA, keyB = (sort_mem[:EP, k * EC // 2:(k + 1) * EC // 2].bitcast(BF16) for k in range(2))
        itemA, itemB = (sort_mem[:EP, (1 + 2 * k) * EC:(3 + 2 * k) * EC].rearrange("p (e c) -> p e c", c=2) for k in range(2))
        addrA, addrB = (sort_mem[:EP, (5 + k) * EC:(6 + k) * EC].bitcast(INT32) for k in range(2))
        winpA, winpB = sb("winpA", [1, TA // 2], INT32), sb("winpB", [1, TB // 2], INT32)
        z_mem = sb("z_mem", [P, 5500])

        def z(lo, n, dt=FP32):
            assert lo + n <= 5500
            v = z_mem[:, lo:lo + n]
            return v if dt == FP32 else v.bitcast(dt)

        iota = sb("iota", [P, P])
        iota_col = sb("iota_col", [P, 1])
        iota_b = sb("iota_b", [P, P], BF16)
        ident = sb("ident", [P, P])
        ident_b = sb("ident_b", [P, P], BF16)
        tri_b = sb("tri_b", [P, P], BF16)
        tri = sb("tri", [P, P])
        ones = sb("ones", [P, P])
        ones_b = sb("ones_b", [P, 1], BF16)
        vecs = sb("vecs", [P, 4, D])
        small = sb("small", [P, 512])

        raw = [acc_mem[:EP, k * EC:(k + 1) * EC].bitcast(INT32) for k in range(5)]
        src_i, dst_i, rel_i, hi_i, lo_i = raw
        o = 5 * EC
        cnt = acc_mem[:, o:o + EC]; o += EC
        cum = acc_mem[:, o:o + EC]; o += EC
        zeros = acc_mem[:, o:o + EC]; o += EC
        base_sb = acc_mem[:, o:o + 8 * BKT_B]; o += 8 * BKT_B
        slotf = acc_mem[:EP, o:o + EC]; o += EC
        iotaT = acc_mem[:, o:o + TB]; o += TB
        winge = acc_mem[:, o:o + TB]; o += TB
        winbc = acc_mem[:, o:o + TB]; o += TB
        fill = acc_mem[:, o:o + 512]; o += 512
        kring = [acc_mem[:EP, o + k * 192:o + (k + 1) * 192].bitcast(BF16) for k in range(4)]; o += 4 * 192
        baser = [acc_mem[0:1, o + k * 768:o + k * 768 + 768] for k in range(2)]; o += 2 * 768
        prod = [acc_mem[:EP, o + k * 384:o + (k + 1) * 384] for k in range(2)]; o += 2 * 384
        slotg = acc_mem[:EP, o:o + 40]; o += 40
        pick = acc_mem[:EP, o:o + 80].bitcast(BF16); o += 80
        assert o <= (BKT_B + 1) * AC, o

        bank = [ctx.enter_context(nc.psum_tensor(f"bank{k}", [P, 512], FP32))[:] for k in range(8)]

        o = 0
        recA = xn_mem[:, o:o + 2 * TA].rearrange("p (t c) -> p t c", c=2); o += 2 * TA
        vmax = xn_mem[:, o:o + TA]; o += TA
        winA = xn_mem[:, o:o + TA]; o += TA
        tbl = xn_mem[:, o:o + 3 * TA].bitcast(BF16).rearrange("p (t c s) -> p t c s", c=2, s=3); o += 3 * TA
        assert o <= NT * D
        htab = xt_mem[:, 0:NT * HC].rearrange("p (t c) -> p t c", c=HC)

        stA_i = z(0, 8, INT32)[:EP].rearrange("p (h k) -> p h k", h=2)
        stA = z(8, 16)[:EP].rearrange("p (h k c) -> p h k c", h=2, c=2)

        wl = z(32, 2 * D).rearrange("p (k d) -> p k d", k=2)
        xtr = z(544, 2 * D).rearrange("p (h c) -> p h c", h=2)
        dots = z(1056, 5 * D).rearrange("p (t d) -> p t d", d=D)
        vsel = z(2112, 1024).rearrange("p (h k s) -> p h k s", h=2, k=4)
        seg1 = z(32, 2048).rearrange("p (h k s) -> p h k s", h=4, k=4)
        onet = z(3648, 512, BF16).rearrange("p (h k s) -> p h k s", h=2, k=4)
        gidx = z(3136, 16, INT32).rearrange("p (h k) -> p h k", h=4)
        gseg = z(3152, 16).rearrange("p (h k) -> p h k", h=4)
        amv = z(4176, 64).rearrange("p (h n) -> p h n", h=2)
        attr_in = z(4240, 256)[:EP].rearrange("p (h k f) -> p h k f", h=2, k=4)
        attr_r = z(4496, 128)[:EP].rearrange("p (k f) -> p k f", k=4)
        o = (BKT_A + 1) * AC
        ta1 = acc_mem[:, o:o + TA]; o += TA
        tm = acc_mem[:, o:o + TA]; o += TA
        tx = acc_mem[:, o:o + TA]; o += TA
        ty = acc_mem[:, o:o + TA]; o += TA
        pay = acc_mem[:, o:o + 16 * HC].rearrange("p (h k c) -> p h k c", h=4, k=4); o += 16 * HC
        assert o <= (BKT_B + 1) * AC - 16 * RW - 16
        o = (BKT_B + 1) * AC - 16 * RW - 16
        stB_mem = acc_mem[:EP, o:o + 16 * RW]; o += 16 * RW
        stB, stBb, stBi = (m_.rearrange("p (h k w) -> p h k w", h=4, k=4)
                           for m_ in (stB_mem, stB_mem.bitcast(BF16), stB_mem.bitcast(INT32)))
        stB_i = acc_mem[:EP, o:o + 16].bitcast(INT32).rearrange("p (h k) -> p h k", h=4); o += 16
        assert o <= (BKT_B + 1) * AC
        a1 = small[:, 330:355]
        a2 = small[:, 355:380]
        gmin = small[:, 430:432]
        stats = small[:, 64:214].rearrange("p (t c) -> p t c", c=6)
        mv = small[:, 214:264].rearrange("p (t c) -> p t c", c=2)
        sd = small[:, 264:289]
        rs = small[:, 289:314]

        w_row = acc_mem[:, 0:NP_]
        o = NP_
        w1_sb = acc_mem[:, o:o + 2 * HID].rearrange("p (k f) -> p k f", k=2); o += 2 * HID
        w2_sb = acc_mem[:, o:o + 8 * D].rearrange("p (j d) -> p j d", d=D); o += 8 * D
        hid_sb = acc_mem[:, o:o + 2 * 8 * 512].rearrange("p (h j n) -> p h j n", h=2, j=8); o += 2 * 8 * 512
        seen = acc_mem[:, o:o + NP_ // 2].bitcast(BF16); o += NP_ // 2
        ycol = acc_mem[:, o:o + 2 * D].rearrange("p (h d) -> p h d", h=2); o += 2 * D
        assert o <= (BKT_B + 1) * AC - 16 * RW - 16
        xt = xt_mem[:, 0:2 * NP_].rearrange("p (k n) -> p k n", k=2)
        tok_w = small[:, 330:355]
        n_gt = small[:, 355:430].rearrange("p (c t) -> p c t", c=3)
        coef = small[:, 432:457]
        real = small[:, 457:458]
        b1_sb = small[:, 460:468]
        br_sb = small[:, 468:469]
        low = z(0, P)
        w_turn = z(P, P)
        lw = xt_mem[:, 0:LAYERS * 8 * D].rearrange("p (l m d) -> p l m d", l=LAYERS, m=8)
        rec_mem = sort_mem[:, 16 * D:16 * D + 16 * RW]
        rec, recb, reci = (m_.rearrange("p (h k w) -> p h k w", h=4, k=4)
                           for m_ in (rec_mem, rec_mem.bitcast(BF16), rec_mem.bitcast(INT32)))
        at = z(512, 512, BF16).rearrange("p (h n) -> p h n", h=2)
        oneh = z(1024, 1024).rearrange("p (h k s) -> p h k s", h=2, k=4)
        msg = z(2048, 8 * AC).rearrange("p (h k c) -> p h k c", h=2, k=4)
        we = z(4104, 3 * 128, BF16).rearrange("p (m d) -> p m d", m=3)
        we_f = z(4488, D)
        we_r = z(4744, D)
        xg = sort_mem[:, 0:16 * D].rearrange("p (h k d) -> p h k d", h=4, k=4)
        turned = sort_mem[:, 0:8 * D].rearrange("p (h n) -> p h n", h=2)
        flat = sort_mem[:, 8 * D:16 * D].rearrange("p (h m d) -> p h m d", h=2, m=4)
        inv = small[:, 320:395]
        biased = z(5000, D)
        gate = small[:, 0:64]
        wr_sb = small[:, 470:486].rearrange("p (k e) -> p k e", k=2)

        recA_d = dram("recA_d", [P * TA, 2])
        recB_d = dram("recB_d", [P * TB, RW])
        h_d = dram("h_d", [NP_, HC])
        pay_d = dram("pay_d", [P, TA * HC])
        x_d = dram("x_d", [NP_, D])
        tok_d = dram("tok_d", [1, NP_])
        baseA_d, baseB_d = dram("baseA_d", [EC, BKT_A]), dram("baseB_d", [EC, BKT_B])
        SORT = [dict(nb=BKT_A, T=TA, key=keyA, base_d=baseA_d, addr=addrA, winp=winpA, n=0),
                dict(nb=BKT_B, T=TB, key=keyB, base_d=baseB_d, addr=addrB, winp=winpB, n=1)]
        for s, cols in zip(SORT, (10, 5)):
            s["cols"] = cols
            s["bodies"] = EC // (4 * cols)

        block = ctx.enter_context(nc.Block())

        @block.sync
        def _(sp):
            for dst, name in ((src_i, "src"), (dst_i, "dst"), (rel_i, "edge_type_3")):
                sp.dma_start(dst, t[name].rearrange("(p c) -> p c", c=EC)).then_inc(S("ids_loaded"), 16)
            x_rows = t["x"][0:(NT - 1) * P, :].rearrange("(t p) d -> p t d", p=P)
            sp.wait_ge(S("x_zeroed"), 1)
            sp.dma_start(x_sb[:, 0:NT - 1, :], x_rows).then_inc(S("x_loaded"), 16)
            sp.dma_start(x_sb[0:LAST, NT - 1, :], t["x"][(NT - 1) * P:N, :]).then_inc(S("x_loaded"), 16)
            sp.dma_start(wl, t["W_layer_t"].rearrange("(k p) d -> p k d", p=P)).then_inc(S("att_w_loaded"), 16)
            for k, name in enumerate(("L0_gnn_b_layer", "L0_gnn_w_a1", "L0_gnn_w_a2")):
                sp.dma_start(vecs[:, k, :], t[name].rearrange("(a d) -> a d", a=1).broadcast_to([P, D]))\
                    .then_inc(S("att_w_loaded"), 16)
            for k, name in enumerate(("L0_gnn_b_a1", "L0_gnn_b_a2")):
                sp.dma_start(small[:, 320 + k:321 + k], t[name].rearrange("(a d) -> a d", a=1).broadcast_to([P, 1]))\
                    .then_inc(S("att_w_loaded"), 16)
            sp.wait_ge(S("fill_ready"), 1)
            sp.dma_start(recA_d.rearrange("(p t) c -> p t c", p=P),
                         xn_mem[:, 0:2 * TA].rearrange("p (t c) -> p t c", c=2)).then_inc(S("filled0"), 16)
            def fill_B(q, n):
                sp.dma_start(recB_d.rearrange("(p q t) c -> p q (t c)", p=P, t=8)[:, ds(q, n), :],
                             fill.rearrange("p (a c) -> p a c", a=1).broadcast_to([P, n, 512])).then_inc(S("filled1"), 16)

            def rank_io(s):
                nb, cols, n_ = s["nb"], s["cols"], s["n"]
                sp.wait_ge(S("base_ready"), n_ + 1)
                sp.dma_start(s["base_d"].rearrange("(k j) b -> j k b", j=100),
                             base_sb[:100, :8 * nb].rearrange("j (k b) -> j k b", b=nb)).then_inc(S("base_stored"), 16)
                sp.wait_ge(S("base_stored"), n_ * 16 + 16)
                rows = s["base_d"].rearrange("(a j) b -> a (j b)", j=2 * cols)

                def body(i):
                    for h in range(2):
                        if due(i * 4 + 2 * h - 2):
                            sp.wait_ge(S("rank_summed"), n_ * 80 + i * 4 + 2 * h - 2)
                        sp.dma_start(baser[h][:, :2 * cols * nb], rows[ds(2 * i + h, 1), :]).then_inc(S(f"row{h}"), 16)
                    if n_ == 1:
                        fill_B(2 * i, 2)
                looped(sp, s["bodies"], body)
            rank_io(SORT[0])
            rank_io(SORT[1])
            fill_B(2 * SORT[1]["bodies"], TB // 8 - 2 * SORT[1]["bodies"])
            sp.wait_ge(S("htab_ready"), 1)
            sp.dma_start(h_d.rearrange("(t p) c -> p t c", p=P), htab).then_inc(S("h_stored"), 16)
            for h in range(2):
                sp.wait_ge(S(f"scattered{h}"), EC // 8 * 64)
            sp.dma_start(recA, recA_d.rearrange("(p t) c -> p t c", p=P)).then_inc(S("recA_loaded"), 16)

            def keep(i, quads=4):
                for h in range(quads):
                    sp.wait_ge(S(f"gathered{h}"), i * 64 + 64)
                    sp.dma_start(pay_d[:, ds((4 * i + h) * 4 * HC, 4 * HC)],
                                 pay[:, h, :, :].rearrange("p k c -> p (k c)")).then_inc(S(f"kept{h}"), 16)
            looped(sp, TA // 16, keep)
            keep(TA // 16, TA // 4 % 4)
            for h in range(4):
                sp.wait_ge(S(f"kept{h}"), turns_A(h) * 16)
            sp.wait_ge(S("a2_kept"), TA // 4)
            attr = t["edge_attr_32"].rearrange("(p e) f -> p (e f)", e=EC)

            def load_pay(Q, h):
                if due(4 * Q - 12):
                    sp.wait_ge(S("att_summed"), 4 * Q - 12)
                sp.dma_start(pay[:, h, :, :].rearrange("p k c -> p (k c)"),
                             pay_d[:, ds(Q * 4 * HC, 4 * HC)]).then_inc(S(f"pay_loaded{h}"), 16)

            def feed(i):
                for h in range(4):
                    Q = 4 * i + h
                    load_pay(Q + 2, (h + 2) % 4)
                    if due(Q - 1):
                        sp.wait_ge(S("attr_rest"), Q - 1)
                    sp.dma_start(attr_in[:, h % 2, :, :].rearrange("p k f -> p (k f)"),
                                 attr[:, ds(Q * 4 * F_ATTR, 4 * F_ATTR)]).then_inc(S(f"attr_loaded{h % 2}"), 16)
            load_pay(0, 0)
            load_pay(1, 1)
            looped(sp, EC // 16, feed)
            sp.wait_ge(S("x1_ready"), 1)
            sp.dma_start(w1_sb, t["L0_ffn_w1"].rearrange("(k p) f -> p k f", p=P)).then_inc(S("mod_w_loaded"), 16)
            sp.dma_start(w2_sb, t["L0_ffn_w2"].rearrange("(j p) d -> p j d", p=P)).then_inc(S("mod_w_loaded"), 16)
            sp.dma_start(b1_sb, t["b1_mod"]).then_inc(S("mod_w_loaded"), 16)
            sp.dma_start(vecs[:, 0, :], t["wr_mod"].rearrange("(a d) -> a d", a=1).broadcast_to([P, D]))\
                .then_inc(S("mod_v_loaded"), 16)
            sp.dma_start(vecs[:, 1, :], t["L0_ffn_b2"].rearrange("(a d) -> a d", a=1).broadcast_to([P, D]))\
                .then_inc(S("mod_v_loaded"), 16)
            sp.dma_start(br_sb, t["L0_ffn_br"].rearrange("(a d) -> a d", a=1).broadcast_to([P, 1]))\
                .then_inc(S("mod_v_loaded"), 16)
            sp.wait_ge(S("router_turned"), 1)
            sp.dma_start(tok_d.rearrange("a (t p) -> (a t) p", p=P), w_turn[:NT, :]).then_inc(S("router_stored"), 16)
            sp.wait_ge(S("router_stored"), 16)
            sp.dma_start(w_row, tok_d.broadcast_to([P, NP_])).then_inc(S("router_row"), 16)
            for h in range(4):
                sp.wait_ge(S(f"edges_put{h}"), EC // 16 * 64)
            for k in range(3):
                sp.dma_start(we_f[32 * k:32 * k + 32, :], t["L1_gnn_edge_w"]).then_inc(S("edge_w_loaded"), 16)
            sp.dma_start(we_f[96:99, :], t["L1_gnn_edge_b"].rearrange("(a d) -> a d", a=1).broadcast_to([3, D]))\
                .then_inc(S("edge_w_loaded"), 16)
            sp.wait_ge(S("x2_ready"), 1)
            for l in range(LAYERS):
                for r in range(R):
                    sp.dma_start(lw[:, l, 2 * r:2 * r + 2, :], t["L1_gnn_weights"][l, r].rearrange("(k p) d -> p k d", p=P))\
                        .then_inc(S("layer_w_loaded"), 16)
                sp.dma_start(lw[:, l, 6:8, :], t["L1_gnn_roots"][l].rearrange("(k p) d -> p k d", p=P))\
                    .then_inc(S("layer_w_loaded"), 16)
            sp.dma_start(vecs[:, 0:LAYERS, :], t["L1_gnn_biases"].rearrange("(a l) d -> a l d", a=1).broadcast_to([P, LAYERS, D]))\
                .then_inc(S("layer_w_loaded"), 16)
            recs = recB_d.rearrange("(p t) w -> p (t w)", p=P)
            for l in range(LAYERS):
                for t0 in range(0, NT, 5):
                    if l:
                        sp.wait_ge(S("updated"), (l - 1) * NT + t0 + 5)
                    else:
                        sp.wait_ge(S("state_ready"), t0 // 5 + 1)
                    sp.dma_start(x_d[t0 * P:(t0 + 5) * P, :].rearrange("(t p) d -> p t d", p=P), xn[:, t0:t0 + 5, :])\
                        .then_inc(S("state_stored"), 16)
                if l == 0:
                    sp.wait_ge(S("edge_w_ready"), 1)

                def feed(i, quads=4):
                    for h in range(quads):
                        Q = 4 * i + h
                        if due(Q - 3):
                            sp.wait_ge(S("rec_turned"), l * QB + Q - 3)
                        sp.sem_inc(S("passed"), 1)
                        if due(i * 64):
                            sp.wait_ge(S(f"sources{h}"), l * 64 * turns(h) + i * 64)
                        if due(Q - 3):
                            sp.wait_ge(S("seg_ready"), l * QB + Q - 3)
                        sp.dma_start(rec[:, h, :, :].rearrange("p k w -> p (k w)"),
                                     recs[:, ds(Q * 4 * RW, 4 * RW)]).then_inc(S(f"rec_loaded{h}"), 16)
                looped(sp, TB // 16, feed)
                feed(TB // 16, TB // 4 % 4)
            sp.wait_ge(S("x3_ready"), 1)
            sp.dma_start(wr_sb, t["L1_ffn_Wr"].rearrange("(k p) e -> p k e", p=P)).then_inc(S("gate_w_loaded"), 16)
            sp.dma_start(gate[0:1, 0:8], t["L1_ffn_br"].rearrange("(a e) -> a e", a=1)).then_inc(S("gate_w_loaded"), 16)
            for k, name in ((2, "L1_ffn_gamma"), (3, "L1_ffn_beta")):
                sp.dma_start(vecs[:, k, :], t[name].rearrange("(a d) -> a d", a=1).broadcast_to([P, D]))\
                    .then_inc(S("norm_w_loaded"), 16)
            sp.wait_ge(S("chosen"), 1)
            for c in range(2):
                e = sp.value_load(gate[0:1, 62 + c:63 + c].bitcast(INT32), min_val=0, max_val=NE - 1)
                sp.dma_start(w1_sb[:, :, c * FE:(c + 1) * FE],
                             t["L1_ffn_W1"][ds(e, 1), :, :].rearrange("e (k p) f -> p (e k) f", p=P)).then_inc(S("moe_w_loaded"), 16)
                sp.dma_start(w2_sb[:, 4 * c:4 * c + 4, :],
                             t["L1_ffn_W2"][ds(e, 1), :, :].rearrange("e (j p) d -> p (e j) d", p=P)).then_inc(S("moe_w_loaded"), 16)
                sp.dma_start(b1_sb[:, 4 * c:4 * c + 4],
                             t["b1_moe"][ds(e, 1), :, :].rearrange("e p j -> p (e j)")).then_inc(S("moe_w_loaded"), 16)
                sp.dma_start(vecs[:, c, :], t["L1_ffn_b2"][ds(e, 1), :].broadcast_to([P, D])).then_inc(S("moe_w_loaded"), 16)
            for t0 in range(0, NT, 5):
                sp.wait_ge(S("out_ready"), t0 // 5 + 1)
                if t0 + 5 < NT:
                    sp.dma_start(out[t0 * P:(t0 + 5) * P, :].rearrange("(t p) d -> p t d", p=P), x_sb[:, t0:t0 + 5, :])\
                        .then_inc(S("out_stored"), 16)
            sp.dma_start(out[(NT - 5) * P:(NT - 1) * P, :].rearrange("(t p) d -> p t d", p=P), x_sb[:, NT - 5:NT - 1, :])\
                .then_inc(S("out_stored"), 16)
            sp.dma_start(out[(NT - 1) * P:N, :], x_sb[0:LAST, NT - 1, :]).then_inc(S("out_stored"), 16)
            sp.wait_ge(S("out_stored"), 96)
            sp.wait_ge(S("x_loaded"), 32)
            sp.wait_ge(S("layer_w_loaded"), 16 * 13)

        @block.gpsimd
        def _(pool):
            g = nc.gpsimd
            g.memset(x_sb[:, NT - 1, :], 0.0).then_inc(S("x_zeroed"), 1)
            g.memset(fill, 0.0).then_inc(S("p_const"), 1)
            g.memset(xn_mem[:, 0:2 * TA], 0.0).then_inc(S("p_const"), 1)
            g.iota(iota, pattern=[[1, P]], base=0, channel_multiplier=0,
                   allow_small_or_imprecise_dtypes=True).then_inc(S("p_const"), 1)
            g.iota(iota_b, pattern=[[1, P]], base=0, channel_multiplier=0,
                   allow_small_or_imprecise_dtypes=True).then_inc(S("p_const"), 1)
            g.iota(iota_col, pattern=[[1, 1]], base=0, channel_multiplier=1,
                   allow_small_or_imprecise_dtypes=True).then_inc(S("p_const"), 1)
            g.iota(iotaT, pattern=[[1, TB]], base=0, channel_multiplier=0,
                   allow_small_or_imprecise_dtypes=True).then_inc(S("p_const"), 1)
            g.memset(ones, 1.0).then_inc(S("p_const"), 1)
            g.memset(ones_b, 1.0).then_inc(S("p_const"), 1)
            g.memset(zeros, 0.0).then_inc(S("p_const"), 1)
            g.memset(pick, 0.0).then_inc(S("p_const"), 1)
            pool.wait_ge(S("p_const"), 10)
            g.memset(pick[:, 79:80], 1.0).then_inc(S("p_const"), 1)
            g.memset(fill.rearrange("p (t c) -> p t c", c=RW)[:, :, W_SEG:W_SEG + 1], -1.0).then_inc(S("p_const"), 1)
            g.memset(xn_mem[:, 0:2 * TA].rearrange("p (t c) -> p t c", c=2)[:, :, 1:2], -1.0).then_inc(S("p_const"), 1)
            pool.wait_ge(S("p_const"), 13)
            pool.sem_inc(S("fill_ready"), 1)

            def scatter_ids(i):
                for h in range(2):
                    pool.wait_ge(S("staged"), 2 * i + h + 1)
                    pool.sem_inc(S("passed_pool"), 1)
                    for k in range(4):
                        pool.indirect_dma_start(
                            out=recA_d, out_offset=bass.IndirectOffsetOnAxis(ap=stA_i[:, h, k:k + 1], axis=0),
                            in_=stA[:, h, k, :], in_offset=None).then_inc(S(f"scattered{h}"), 16)

            def scatter_edges(i):
                for h in range(4):
                    pool.wait_ge(S("act_stepB"), 4 * (4 * i + h) + 4)
                    pool.wait_ge(S("attr_split"), 4 * i + h + 1)
                    pool.sem_inc(S("passed_pool"), 1)
                    for k in range(4):
                        pool.indirect_dma_start(
                            out=recB_d, out_offset=bass.IndirectOffsetOnAxis(ap=stB_i[:, h, k:k + 1], axis=0),
                            in_=stB[:, h, k, :], in_offset=None).then_inc(S(f"edges_put{h}"), 16)
            pool.wait_ge(S("filled0"), 16)
            looped(pool, EC // 8, scatter_ids)
            pool.wait_ge(S("gmin_part"), 1)
            g.partition_all_reduce(gmin[:, 1:2], gmin[:, 0:1], P, bass.bass_isa.ReduceOp.max).then_inc(S("gmin_all"), 1)

            def gather_h(i, quads=4):
                for h in range(quads):
                    if due(i * 16):
                        pool.wait_ge(S(f"kept{h}"), i * 16)
                    if due(4 * i + h - 3):
                        pool.wait_ge(S("a2_kept"), 4 * i + h - 3)
                    pool.wait_ge(S("gidx_staged"), 4 * i + h + 1)
                    pool.sem_inc(S("passed_pool"), 1)
                    for k in range(4):
                        pool.indirect_dma_start(
                            out=pay[:, h, k, :], out_offset=None, in_=h_d,
                            in_offset=bass.IndirectOffsetOnAxis(ap=gidx[:, h, k:k + 1], axis=0))\
                            .then_inc(S(f"gathered{h}"), 16)
            pool.wait_ge(S("filled1"), 16 * (SORT[1]['bodies'] + 1))
            pool.wait_ge(S("h_stored"), 16)
            pool.wait_ge(S("dots_done"), 1)
            looped(pool, TA // 16, gather_h)
            gather_h(TA // 16, TA // 4 % 4)
            looped(pool, EC // 16, scatter_edges)
            for l in range(LAYERS):
                if l == 0:
                    pool.wait_ge(S("x2_ready"), 1)
                    for h in range(4):
                        pool.wait_ge(S(f"edges_put{h}"), EC // 16 * 64)
                    g.memset(acc_mem, 0.0).then_inc(S("acc_zeroed"), 1)
                if l:
                    pool.wait_ge(S("flat_ready"), (l - 1) * NT + NT)
                    g.memset(acc_mem[:, 0:38 * AC], 0.0).then_inc(S("acc_half"), 1)

                pool.wait_ge(S("state_stored"), l * 80 + 80)

                def gather_x(i, quads=4):
                    for h in range(quads):
                        Q = 4 * i + h
                        pool.wait_ge(S(f"rec_loaded{h}"), l * 16 * turns(h) + i * 16 + 16)
                        if due(2 * Q - 6):
                            pool.wait_ge(S("multiplied"), l * 2 * QB + 2 * Q - 6)
                        pool.sem_inc(S("passed_pool"), 1)
                        for k in range(4):
                            pool.indirect_dma_start(
                                out=xg[:, h, k, :], out_offset=None, in_=x_d,
                                in_offset=bass.IndirectOffsetOnAxis(ap=reci[:, h, k, W_SRC:W_SRC + 1], axis=0))\
                                .then_inc(S(f"sources{h}"), 16)
                looped(pool, TB // 16, gather_x)
                gather_x(TB // 16, TB // 4 % 4)

        @block.scalar
        def _(act):
            a = nc.scalar

            def stage_A(i, h):
                Q = 2 * i + h
                if due(i * 64):
                    act.wait_ge(S(f"scattered{h}"), i * 64)
                act.sem_inc(S("passed"), 1)
                act.wait_ge(S("addr_ready"), 1)
                a.activation(stA_i[:, h, :], addrA[:, ds(Q * 4, 4)], ACT.Copy).then_inc(S("act_stepA"), 1)
                a.activation(stA[:, h, :, :], itemA[:, ds(Q * 4, 4), :], ACT.Copy).then_inc(S("act_stepA"), 1)
                act.wait_ge(S("act_stepA"), Q * 2 + 2)
                act.sem_inc(S("passed"), 1)
                act.sem_inc(S("staged"), 1)

            def sqrt_of_var(n):
                if due(n):
                    act.wait_ge(S("var_ready"), n)
                a.activation(sd, sd, ACT.Sqrt).then_inc(S("std_ready"), 1)

            def stage_ids(i):
                for h in range(2):
                    stage_A(i, h)
            stage_ids(0)
            stage_ids(1)
            sqrt_of_var(1)
            with act.Fori(2, EC // 8 - 1) as i:
                stage_ids(i)
            stage_ids(EC // 8 - 1)

            def stage_gather(i, quads=4):
                for h in range(quads):
                    Q = 4 * i + h
                    if due(Q - 3):
                        act.wait_ge(S("v_ready"), Q - 3)
                    if due(i * 64):
                        act.wait_ge(S(f"gathered{h}"), i * 64)
                    act.sem_inc(S("passed"), 1)
                    a.activation(gidx[:, h, :], recA[:, ds(Q * 4, 4), 0], ACT.Copy).then_inc(S("act_stepG"), 1)
                    a.activation(gseg[:, h, :], recA[:, ds(Q * 4, 4), 1], ACT.Copy).then_inc(S("act_stepG"), 1)
                    act.wait_ge(S("act_stepG"), Q * 2 + 2)
                    act.sem_inc(S("passed"), 1)
                    act.sem_inc(S("gidx_staged"), 1)
            act.wait_ge(S("recA_loaded"), 16)
            looped(act, TA // 16, stage_gather)
            stage_gather(TA // 16, TA // 4 % 4)

            def turned_onehot(Q, h):
                act.wait_ge(S("oneh_turned"), Q + 1)
                if due(Q - 1):
                    act.wait_ge(S("am_ready"), Q - 1)
                a.activation(onet[:, h, :, :].rearrange("p k s -> p (k s)"), bank[h], ACT.Copy)\
                    .then_inc(S("onet_ready"), 1)

            def weigh(Q, h, n):
                act.wait_ge(S("logit_ready"), Q + 1)
                a.activation(amv[:, h % 2, 16:20], amv[:, h % 2, 12:16], ACT.Exp).then_inc(S("weight_ready"), 1)
                act.wait_ge(S("weight_ready"), Q + 1)
                act.wait_ge(S(f"pay_loaded{h}"), n * 16 + 16)
                for k in range(4):
                    a.activation(pay[:, h, k, :AC], pay[:, h, k, :AC], ACT.Copy, scale=amv[:, h % 2, 16 + k:17 + k])\
                        .then_inc(S("weighted"), 1)

            def attr_middle(Q, h):
                act.wait_ge(S("attr_rest"), Q + 1)
                a.activation(stBb[:, h, :, 32:64], attr_r, ACT.Copy).then_inc(S("act_stepB"), 1)

            def attend(i):
                for h in range(4):
                    Q = 4 * i + h
                    if not (isinstance(i, int) and Q == 0):
                        attr_middle(Q - 1, (h - 1) % 4)
                    if due(i * 64):
                        act.wait_ge(S(f"edges_put{h}"), i * 64)
                    act.wait_ge(S(f"attr_loaded{h % 2}"), i * 32 + h // 2 * 16 + 16)
                    a.activation(stBb[:, h, :, 0:32], attr_in[:, h % 2, :, :], ACT.Copy).then_inc(S("attr_hi"), 1)
                    a.activation(stB_i[:, h, :], addrB[:, ds(Q * 4, 4)], ACT.Copy).then_inc(S("act_stepB"), 1)
                    a.activation(stBi[:, h, :, W_SRC], itemB[:, ds(Q * 4, 4), 0].bitcast(INT32), ACT.Copy)\
                        .then_inc(S("act_stepB"), 1)
                    a.activation(stB[:, h, :, W_SEG], itemB[:, ds(Q * 4, 4), 1], ACT.Copy).then_inc(S("act_stepB"), 1)
                    turned_onehot(Q + 2, h % 2)
                    weigh(Q + 1, (h + 1) % 4, i + (h + 1) // 4)
            act.wait_ge(S("stB_ready"), 1)
            act.wait_ge(S("addr_ready"), 1 + 1)
            turned_onehot(0, 0)
            turned_onehot(1, 1)
            weigh(0, 0, 0)
            looped(act, EC // 16, attend)
            attr_middle(EC // 4 - 1, 3)
            weigh(TA // 4 - 1, 1, EC // 16)

            def turn_all(n):
                for tt in range(NT):
                    act.wait_ge(S("xn_all"), n * NT + tt + 1)
                    a.activation(xt[:, :, tt * P:(tt + 1) * P], bank[tt % 2][:, :D].rearrange("p (k n) -> p k n", k=2), ACT.Copy)\
                        .then_inc(S("xt_copied"), 1)

            def hidden(n, func):
                def chunk(c, h, m):
                    for j in range(8):
                        if due((c - 1) * 4):
                            act.wait_ge(S("tok_done"), n * NT + (c - 1) * 4)
                        act.wait_ge(S("up_done"), n * 56 + c * 8 + j + 1)
                        a.activation(hid_sb[:, h, j, :m], bank[j % 4][:, :m], func, bias=b1_sb[:, j:j + 1])\
                            .then_inc(S("hid_ready"), 1)
                for h in range(2):
                    chunk(h, h, 512)
                with act.Fori(1, 3) as i:
                    for h in range(2):
                        chunk(2 * i + h, h, 512)
                chunk(6, 0, NP_ - 6 * 512)
            sqrt_of_var(2)
            turn_all(0)
            act.wait_ge(S("mod_w_loaded"), 48)
            hidden(0, ACT.Gelu_apprx_tanh)
            sqrt_of_var(3)
            for l in range(LAYERS):
                def copy_attr(Q, h):
                    act.wait_ge(S("rec_turned"), l * QB + Q + 1)
                    if due(2 * Q - 2):
                        act.wait_ge(S("projected"), l * 2 * QB + 2 * Q - 2)
                    a.activation(at[:KA, h, :], bank[h][:KA, 0:256].bitcast(BF16), ACT.Copy).then_inc(S("attr_ready"), 1)

                def relu_msg(i, quads=4):
                    for h in range(quads):
                        Q = 4 * i + h
                        if quads == 4:
                            copy_attr(Q + 2, h % 2)
                        for j in range(2):
                            act.wait_ge(S("multiplied"), l * 2 * QB + 2 * Q + j + 1)
                            mm = msg[:, h % 2, 2 * j:2 * j + 2, :D]
                            a.activation(mm, mm, ACT.Relu).then_inc(S("msg_ready"), 1)
                copy_attr(0, 0)
                copy_attr(1, 1)
                looped(act, TB // 16, relu_msg)
                relu_msg(TB // 16, TB // 4 % 4)

                act.wait_ge(S("inv_ready"), l + 1)
                act.wait_ge(S("flushed_b"), l * TB + TB)
                a_flat = lambda tt, h: [
                    a.activation(flat[:, h, r, :], acc_mem[:, ds((tt + r * NT) * AC, D)], ACT.Copy,
                                 scale=inv[:, ds(tt + r * NT, 1)]) for r in range(R)
                ] + [a.activation(flat[:, h, 3, :], xn_mem[:, ds(tt * D, D)], ACT.Copy)]

                def flatten(tt, h):
                    if due(2 * tt - 2):
                        act.wait_ge(S("flat_turned"), l * 2 * NT + 2 * tt - 2)
                    act.sem_inc(S("passed"), 1)
                    a_flat(tt, h)[-1].then_inc(S("flat_ready"), 1)
                for h in range(2):
                    flatten(h, h)
                with act.Fori(1, NT // 2) as i:
                    for h in range(2):
                        flatten(2 * i + h, h)
                flatten(NT - 1, 0)
            sqrt_of_var(4)
            turn_all(1)
            for n in range(3):
                act.wait_ge(S("gate_exp"), n + 1)
                gx = gate[0:1, (8, 24, 40)[n]:(16, 32, 41)[n]]
                a.activation(gx, gx, ACT.Exp).then_inc(S("gate_exp_done"), 1)
            act.wait_ge(S("moe_w_loaded"), 128)
            hidden(1, ACT.Gelu)
            sqrt_of_var(5)

        @block.tensor
        def _(pe):
            m = nc.tensor
            pe.wait_ge(S("const_ready"), 1)

            def rank(s):
                nb, cols, n_ = s["nb"], s["cols"], s["n"]
                for half in range(2):
                    n = s["bodies"] // 2

                    def body(i):
                        for k in range(4):
                            q = (i + half * n) * 4 + k
                            pe.wait_ge(S("onehot"), n_ * 80 + q + 1)
                            if half == 0 and isinstance(i, int) and i == 0 and k == 0 and n_ == 1:
                                pe.wait_ge(S("counts_read"), 1)
                            m.matmul(bank[half][:4 * n, :cols * nb], pick[:, ds((i * 4 + k) * -1 + 79, 4 * n)],
                                     kring[k][:, :cols * nb], start=isinstance(i, int) and i * 4 + k == 0,
                                     stop=isinstance(i, int) and i * 4 + k == 4 * n - 1).then_inc(S("counted"), 1)
                    looped(pe, n, body)
                for half in range(2):
                    pe.wait_ge(S("rows_copied"), n_ * 2 + half + 1)
                    G = s["bodies"] * 2
                    for c in range(cols):
                        last = m.transpose(bank[2 + half][:nb, c * G:(c + 1) * G], prod[half][:G, c * nb:(c + 1) * nb],
                                           ident[:G, :G])
                    last.then_inc(S("counts_turned"), 1)
                pe.wait_ge(S("tiles_ready"), n_ + 1)
                m.matmul(bank[2][:nb, 0:1], tri[:nb, :nb], small[:nb, 1:2], start=True, stop=True).then_inc(S("tilesum"), 1)
                pe.wait_ge(S("basecol_ready"), n_ + 1)
                for k in range(8):
                    last = m.transpose(bank[3][:100, k * nb:(k + 1) * nb] if k * nb + nb <= 512 else
                                       bank[4][:100, (k * nb - 450):(k * nb - 450) + nb],
                                       cum[:nb, k * 100:(k + 1) * 100], ident[:nb, :nb])
                last.then_inc(S("base_turned"), 1)
                pe.wait_ge(S("winge_ready"), n_ + 1)
                for lo in (0, 512):
                    n = min(512, s["T"] - lo)
                    last = m.matmul(bank[5 + lo // 512][:, :n], ones[:nb, :], winge[:nb, lo:lo + n], start=True, stop=True)
                last.then_inc(S("win_summed"), 1)

                def body(i):
                    for k in range(4):
                        q = i * 4 + k
                        h = k // 2
                        pe.wait_ge(S(f"row{h}"), n_ * 320 + i * 16 + 16)
                        pe.wait_ge(S("onehot2"), n_ * 80 + q + 1)
                        if due(q - 1):
                            pe.wait_ge(S("rank_summed"), n_ * 80 + q - 1)
                        ps = bank[k % 2][:EP, :cols * nb]
                        m.matmul(ps, tri_b[:EP, :EP], kring[k][:, :cols * nb], start=True, stop=False)
                        m.matmul(ps, ones[0:1, :EP], baser[h][:, (k % 2) * cols * nb:(k % 2 + 1) * cols * nb],
                                 start=False, stop=True).then_inc(S("ranked"), 1)
                looped(pe, s["bodies"], body)
            rank(SORT[0])

            pe.wait_ge(S("xn_ready"), 1)
            pe.wait_ge(S("att_w_loaded"), 96)

            def turn_xn(tt):
                if due(tt - 1):
                    pe.wait_ge(S("xn_turn_copied"), tt - 1)
                for k in range(2):
                    last = m.transpose(bank[4 + 3 * (tt % 2)][:, k * P:(k + 1) * P], xn[:, tt, k * P:(k + 1) * P], ident)
                last.then_inc(S("xn_turned"), 1)
            turn_xn(0)
            for tt in range(NT):
                if tt + 1 < NT:
                    turn_xn(tt + 1)
                if due(tt - 1):
                    pe.wait_ge(S("h_read"), tt - 1)
                pe.wait_ge(S("xn_turn_copied"), tt + 1)
                for k in range(2):
                    last = m.matmul(bank[2 + tt % 2][:, :D], xtr[:, tt % 2, k * P:(k + 1) * P], wl[:, k, :],
                                    start=(k == 0), stop=(k == 1))
                last.then_inc(S("h_made"), 1)
            rank(SORT[1])

            def turn_v(i):
                for h in range(2):
                    pe.wait_ge(S("v_ready"), 2 * i + h + 1)
                    if due(2 * i + h - 1):
                        pe.wait_ge(S("v_maxed"), 2 * i + h - 1)
                    for k in range(4):
                        last = m.transpose(bank[h][:, k * P:(k + 1) * P], vsel[:, h, k, :], ident)
                    last.then_inc(S("v_turned"), 1)
            looped(pe, TA // 8, turn_v)

            def turn_onehot(Q, h):
                if due(Q - 1):
                    pe.wait_ge(S("onet_ready"), Q - 1)
                pe.wait_ge(S("oneh_ready"), Q + 1)
                for k in range(4):
                    last = m.transpose(bank[h % 2][:, k * P:(k + 1) * P], seg1[:, h, k, :], ident)
                last.then_inc(S("oneh_turned"), 1)

            def look_up(Q, h):
                pe.wait_ge(S("onet_ready"), Q + 1)
                if due(Q - 1):
                    pe.wait_ge(S("am_read"), Q - 1)
                for k in range(4):
                    last = m.matmul(bank[2 + 5 * h][:, k * 6:k * 6 + 6], onet[:, h, k, :],
                                    tbl[:, ds(Q * 4 + k, 1), :, :].rearrange("p t c s -> p (t c s)"), start=True, stop=True)
                last.then_inc(S("am_ready"), 1)

            def sum_rows(Q, h):
                for k in range(4):
                    if due(Q * 4 + k - 3):
                        pe.wait_ge(S("flushed"), Q * 4 + k - 3)
                    pe.wait_ge(S("weighted"), Q * 4 + k + 1)
                    m.matmul(bank[3 + k][:, :AC], seg1[:, h, k, :], pay[:, h, k, :AC], start=True, stop=True)\
                        .then_inc(S("att_summed"), 1)

            def attend(i):
                for h in range(4):
                    Q = 4 * i + h
                    look_up(Q + 1, (h + 1) % 2)
                    turn_onehot(Q + 2, (h + 2) % 4)
                    sum_rows(Q, h)
            pe.wait_ge(S("tbl_ready"), 1)
            turn_onehot(0, 0)
            turn_onehot(1, 1)
            look_up(0, 0)
            looped(pe, EC // 16, attend)
            look_up(TA // 4 - 1, 1)
            sum_rows(TA // 4 - 2, 0)
            sum_rows(TA // 4 - 1, 1)

            def turn_all(n, ready):
                for tt in range(NT):
                    pe.wait_ge(S(ready), tt // 5 + 1)
                    if due(tt - 1):
                        pe.wait_ge(S("xt_copied"), n * NT + tt - 1)
                    for k in range(2):
                        last = m.transpose(bank[tt % 2][:, k * P:(k + 1) * P], xn[:, tt, k * P:(k + 1) * P], ident)
                    last.then_inc(S("xn_all"), 1)

            def two_products(n):
                def up(c, m_):
                    for j in range(8):
                        if due(c * 8 + j - 3):
                            pe.wait_ge(S("hid_ready"), n * 56 + c * 8 + j - 3)
                        for k in range(2):
                            last = m.matmul(bank[j % 4][:, :m_], w1_sb[:, k, j * P:(j + 1) * P], xt[:, k, ds(c * 512, m_)],
                                            start=(k == 0), stop=(k == 1))
                        last.then_inc(S("up_done"), 1)

                def down(c, h, m_):
                    pe.wait_ge(S("hid_ready"), n * 56 + c * 8 + 8)
                    for q in range(m_ // P):
                        if due(c * 4 + q - 3):
                            pe.wait_ge(S("tok_added"), n * NT + c * 4 + q - 3)
                        for j in range(8):
                            last = m.matmul(bank[4 + q][:, :D], hid_sb[:, h, j, q * P:(q + 1) * P], w2_sb[:, j, :],
                                            start=(j == 0), stop=(j == 7))
                        last.then_inc(S("tok_done"), 1)
                pe.wait_ge(S("xt_copied"), n * NT + NT)
                up(0, 512)
                up(1, 512)
                down(0, 0, 512)
                with pe.Fori(1, 3) as i:
                    up(2 * i, 512)
                    down(2 * i - 1, 1, 512)
                    up(2 * i + 1, 512)
                    down(2 * i, 0, 512)
                up(6, NP_ - 6 * 512)
                down(5, 1, 512)
                down(6, 0, NP_ - 6 * 512)

            turn_all(0, "xn2_ready")
            pe.wait_ge(S("router_ready"), 1)
            m.transpose(bank[7][:NT, :P], tok_w, ident).then_inc(S("router_pe"), 1)
            pe.wait_ge(S("mod_w_loaded"), 48)
            pe.wait_ge(S("router_turned"), 1)
            two_products(0)
            for l in range(LAYERS):
                if l == 0:
                    pe.wait_ge(S("edge_w_ready"), 1)
                    pe.wait_ge(S("tok_added"), NT)
                else:
                    pe.wait_ge(S("updated"), (l - 1) * NT + NT)

                def turn(Q, h, n):
                    if due(Q - 1):
                        pe.wait_ge(S("attr_ready"), l * QB + Q - 1)
                    pe.wait_ge(S(f"rec_loaded{h}"), l * 16 * turns(h) + n * 16 + 16)
                    for k in range(4):
                        last = m.transpose(bank[h % 2][:KA, 0:256].bitcast(BF16)[:, k * P:(k + 1) * P],
                                           recb[:, h, k, 0:KA], ident_b)
                    last.then_inc(S("rec_turned"), 1)

                def sums(Q, h):
                    pe.wait_ge(S("seg_ready"), l * QB + Q + 1)
                    for k in range(4):
                        pe.wait_ge(S("msg_ready"), l * 2 * QB + 2 * Q + k // 2 + 1)
                        if due(Q * 4 + k - 3):
                            pe.wait_ge(S("flushed_b"), l * TB + Q * 4 + k - 3)
                        m.matmul(bank[4 + k][:, :AC], oneh[:, h, k, :], msg[:, h, k, :], start=True, stop=True)\
                            .then_inc(S("summed"), 1)

                def edges(i, quads=4):
                    for h in range(quads):
                        Q = 4 * i + h
                        pe.wait_ge(S("attr_ready"), l * QB + Q + 1)
                        for j in range(2):
                            if due(2 * Q + j - 1):
                                pe.wait_ge(S("multiplied"), l * 2 * QB + 2 * Q + j - 1)
                            for k in (2 * j, 2 * j + 1):
                                o_ = bank[2 + j][:, (k % 2) * D:(k % 2 + 1) * D]
                                m.matmul(o_, at[:KA, h % 2, k * P:(k + 1) * P], we[:KA, 0, :], start=True, stop=False)
                                m.matmul(o_, at[:64, h % 2, k * P:(k + 1) * P], we[:64, 1, :], start=False, stop=False)
                                last = m.matmul(o_, at[:32, h % 2, k * P:(k + 1) * P], we[:32, 2, :], start=False, stop=True)
                            last.then_inc(S("projected"), 1)
                        if quads == 4:
                            turn(Q + 2, (h + 2) % 4, i + (h + 2) // 4)
                        if not (isinstance(i, int) and Q == 0):
                            sums(Q - 1, (h - 1) % 2)
                turn(0, 0, 0)
                turn(1, 1, 0)
                looped(pe, TB // 16, edges)
                edges(TB // 16, TB // 4 % 4)
                sums(TB // 4 - 1, 1)

                pe.wait_ge(S("layer_w_loaded"), 16 * 13)
                pe.wait_ge(S("flushed_b"), l * TB + TB)

                def turn_flat(tt, h):
                    pe.wait_ge(S("flat_ready"), l * NT + tt + 1)
                    if due(2 * tt - 2):
                        pe.wait_ge(S("turn_copied"), l * 2 * NT + 2 * tt - 2)
                    for b in range(2):
                        for r in range(4):
                            last = m.transpose(bank[2 * h + b][:, r * P:(r + 1) * P],
                                               flat[:, h, 2 * b + r // 2, (r % 2) * P:(r % 2 + 1) * P], ident)
                        last.then_inc(S("flat_turned"), 1)

                def apply(tt, h):
                    pe.wait_ge(S("turn_copied"), l * 2 * NT + 2 * tt + 2)
                    if due(tt - 1):
                        pe.wait_ge(S("biased"), l * NT + tt - 1)
                    o_ = bank[4 + h][:, :D]
                    for r in range(8):
                        last = m.matmul(o_, turned[:, h, r * P:(r + 1) * P], lw[:, l, r, :], start=(r == 0), stop=(r == 7))
                    last.then_inc(S("applied"), 1)
                turn_flat(0, 0)
                turn_flat(1, 1)
                apply(0, 0)
                with pe.Fori(1, NT // 2) as i:
                    turn_flat(2 * i, 0)
                    apply(2 * i - 1, 1)
                    turn_flat(2 * i + 1, 1)
                    apply(2 * i, 0)
                turn_flat(NT - 1, 0)
                apply(NT - 2, 1)
                apply(NT - 1, 0)
            turn_all(1, "xn4_ready")
            pe.wait_ge(S("gate_w_loaded"), 32)
            pe.wait_ge(S("mean_ready"), 1)
            for k in range(2):
                last = m.matmul(bank[6][0:1, 0:NE], small[:, 490 + k:491 + k], wr_sb[:, k, :], start=(k == 0), stop=(k == 1))
            last.then_inc(S("logits_made"), 1)
            pe.wait_ge(S("top_ready"), 1)
            m.matmul(bank[5][:, 0:2], ones[0:1, :], gate[0:1, 56:58], start=True, stop=True).then_inc(S("top_spread"), 1)
            pe.wait_ge(S("moe_w_loaded"), 128)
            pe.wait_ge(S("moe_w_scaled"), 1)
            two_products(1)

        @block.vector
        def _(dve):
            v = nc.vector
            st = Steps(dve, "dve_step")
            dve.wait_ge(S("p_const"), 13)
            v.tensor_scalar(ident, iota, iota_col, None, ALU.is_equal).then_inc(S("d_const"), 1)
            v.tensor_scalar(ident_b, iota, iota_col, None, ALU.is_equal).then_inc(S("d_const"), 1)
            v.tensor_scalar(tri, iota, iota_col, None, ALU.is_gt).then_inc(S("d_const"), 1)
            v.tensor_scalar(tri_b, iota, iota_col, None, ALU.is_gt).then_inc(S("const_ready"), 1)
            dve.wait_ge(S("ids_loaded"), 48)
            v.tensor_single_scalar(hi_i, src_i, 7, ALU.logical_shift_right).then_inc(S("dve_step"), 1); st.n += 1
            v.tensor_single_scalar(lo_i, src_i, 127, ALU.bitwise_and).then_inc(S("dve_step"), 1); st.n += 1
            st.did(v.tensor_copy(itemB[:, :, 0].bitcast(INT32), src_i))
            st.did(v.tensor_copy(itemA[:, :, 0], dst_i))
            st.settle()
            st.did(v.tensor_copy(keyA, hi_i))
            st.did(v.tensor_copy(itemA[:, :, 1], lo_i))
            st.settle()
            st.did(v.tensor_single_scalar(hi_i, dst_i, 7, ALU.logical_shift_right))
            st.did(v.tensor_single_scalar(lo_i, dst_i, 127, ALU.bitwise_and))
            st.settle()
            st.did(v.scalar_tensor_tensor(keyB, rel_i, float(NT), hi_i, ALU.mult, ALU.add))
            st.did(v.tensor_copy(itemB[:, :, 1], lo_i))
            st.settle()

            def rank(s):
                nb, cols, n_, T = s["nb"], s["cols"], s["n"], s["T"]

                def onehot(k, q):
                    kr = kring[k][:, :cols * nb].rearrange("p (c b) -> p c b", b=nb)
                    io = iota_b[:EP, 0:nb].rearrange("p (a b) -> p a b", a=1).broadcast_to([EP, cols, nb])
                    ky = s["key"][:, ds(q * cols, cols)].rearrange("p (c a) -> p c a", a=1).broadcast_to([EP, cols, nb])
                    return v.tensor_tensor(kr, io, ky, ALU.is_equal)

                def count_body(i):
                    for k in range(4):
                        q = i * 4 + k
                        if due(q - 3):
                            dve.wait_ge(S("counted"), n_ * 80 + q - 3)
                        onehot(k, q).then_inc(S("onehot"), 1)
                looped(dve, s["bodies"], count_body)
                half = EC // 2
                dve.wait_ge(S("counted"), n_ * 80 + s["bodies"] * 4)
                G = s["bodies"] * 2
                for b in range(2):
                    v.tensor_copy(prod[b][:G, :cols * nb], bank[b][:G, :cols * nb]).then_inc(S("rows_copied"), 1)
                for b in range(2):
                    dve.wait_ge(S("counts_turned"), n_ * 2 + b + 1)
                    st.did(v.tensor_copy(cnt[:nb, b * half:(b + 1) * half].rearrange("p (g c) -> p c g", c=cols),
                                         bank[2 + b][:nb, :half].rearrange("p (c g) -> p c g", c=cols)))
                st.settle()
                v.tensor_tensor_scan(cum[:nb], cnt[:nb], zeros[:nb], 0.0, ALU.add, ALU.add).then_inc(S("counts_read"), 1)
                dve.wait_ge(S("counts_read"), n_ + 1)
                ti = small[:nb, 2:3].bitcast(INT32)
                st.run(v.tensor_scalar(ti, cum[:nb, EC - 1:EC], 127.0, None, ALU.add))
                st.run(v.tensor_single_scalar(small[:nb, 3:4].bitcast(INT32), ti, 7, ALU.logical_shift_right))
                v.tensor_copy(small[:nb, 1:2], small[:nb, 3:4].bitcast(INT32)).then_inc(S("tiles_ready"), 1)
                dve.wait_ge(S("tilesum"), n_ + 1)
                dve.wait_ge(S("tiles_ready"), n_ + 1)
                st.did(v.tensor_scalar(small[:nb, 4:5], bank[2][:nb, 0:1], 128.0, None, ALU.mult))
                st.run(v.tensor_tensor(small[:nb, 5:6], bank[2][:nb, 0:1], small[:nb, 1:2], ALU.add))
                v.scalar_tensor_tensor(cum[:nb], cum[:nb], small[:nb, 4:5], cnt[:nb], ALU.add, ALU.subtract)\
                    .then_inc(S("basecol_ready"), 1)
                v.tensor_scalar(winge[:nb, :T], iotaT[:nb, :T], small[:nb, 5:6], None, ALU.is_ge).then_inc(S("winge_ready"), 1)
                dve.wait_ge(S("base_turned"), n_ + 1)
                n1 = min(8, 512 // nb) * nb
                if n1 < 8 * nb:
                    st.did(v.tensor_copy(base_sb[:100, n1:8 * nb], bank[4][:100, n1 - 450:8 * nb - 450]))
                st.run(v.tensor_copy(base_sb[:100, :n1], bank[3][:100, :n1]))
                dve.sem_inc(S("base_ready"), 1)
                dve.wait_ge(S("win_summed"), n_ + 1)
                w = winbc
                st.did(v.tensor_scalar(w[:, :512], bank[5][:, :], float(nb), None, ALU.min))
                st.run(v.tensor_scalar(w[:, 512:T], bank[6][:, :T - 512], float(nb), None, ALU.min))
                pair = w[0:1, :T].rearrange("p (a b) -> p a b", b=2)
                st.run(v.scalar_tensor_tensor(s["winp"], pair[:, :, 1], nb + 1.0, pair[:, :, 0], ALU.mult, ALU.add))

                def rank_body(i):
                    for k in range(4):
                        q = i * 4 + k
                        onehot(k, q).then_inc(S("onehot2"), 1)
                    for k in range(4):
                        q = i * 4 + k
                        dve.wait_ge(S("ranked"), n_ * 80 + q + 1)
                        v.tensor_tensor(prod[k % 2][:, :cols * nb], bank[k % 2][:EP, :cols * nb],
                                        kring[k][:, :cols * nb], ALU.mult).then_inc(S("rank_masked"), 1)
                        dve.wait_ge(S("rank_masked"), n_ * 80 + q + 1)
                        v.tensor_reduce(slotg[:, k * cols:(k + 1) * cols],
                                        prod[k % 2][:, :cols * nb].rearrange("p (c b) -> p c b", b=nb),
                                        X_AXIS, ALU.add).then_inc(S("rank_summed"), 1)
                    dve.wait_ge(S("rank_summed"), n_ * 80 + i * 4 + 4)
                    v.tensor_scalar(slotf[:, ds(i * 4 * cols, 4 * cols)], slotg[:, :4 * cols], 0.0, None, ALU.add)\
                        .then_inc(S("slots_kept"), 1)
                    dve.wait_ge(S("slots_kept"), n_ * 20 + i + 1)
                looped(dve, s["bodies"], rank_body)
                st.run(v.tensor_copy(hi_i, slotf))
                st.run(v.tensor_single_scalar(lo_i, hi_i, 127, ALU.bitwise_and))
                st.run(v.tensor_single_scalar(hi_i, hi_i, 7, ALU.logical_shift_right))
                v.scalar_tensor_tensor(s["addr"], lo_i, float(T), hi_i, ALU.mult, ALU.add).then_inc(S("addr_ready"), 1)
                dve.wait_ge(S("addr_ready"), n_ + 1)
            def norm_stats(src, tt):
                st.run(v.bn_stats(stats[:, tt, :], src[:, tt, :]))
                st.did(v.bn_aggr(mv[:, tt, :], stats[:, tt, :]))

            def layer_norm(n, dst, done, src=x_sb, stats_made=False, group=NT, then=None):
                if not stats_made:
                    for tt in range(NT):
                        st.did(v.bn_stats(stats[:, tt, :], src[:, tt, :]))
                    st.settle()
                    for tt in range(NT):
                        st.did(v.bn_aggr(mv[:, tt, :], stats[:, tt, :]))
                st.settle()
                v.tensor_scalar(sd, mv[:, :, 1], EPS, None, ALU.add).then_inc(S("var_ready"), 1)
                if due(n):
                    dve.wait_ge(S("std_ready"), n)
                st.run(v.reciprocal(rs, sd))
                for t0 in range(0, NT, group):
                    for tt in range(t0, t0 + group):
                        st.did(v.tensor_scalar(dst[:, tt, :], src[:, tt, :], mv[:, tt, 0:1], rs[:, tt:tt + 1],
                                               ALU.subtract, ALU.mult))
                    st.settle()
                    if then:
                        then(t0)
                    dve.sem_inc(S(done), 1)

            rank(SORT[0])
            dve.wait_ge(S("x_loaded"), 32)
            dve.wait_ge(S("filled0"), 16)
            layer_norm(1, xn, "xn_ready")
            dve.wait_ge(S("att_w_loaded"), 96)
            st.did(v.memset(htab[:, :, D:D + 1], 1.0))

            def copy_turned_xn(tt):
                if due(tt - 1):
                    dve.wait_ge(S("h_made"), tt - 1)
                dve.wait_ge(S("xn_turned"), tt + 1)
                v.tensor_copy(xtr[:, tt % 2, :], bank[4 + 3 * (tt % 2)][:, :D]).then_inc(S("xn_turn_copied"), 1)
            copy_turned_xn(0)
            for tt in range(NT):
                if tt + 1 < NT:
                    copy_turned_xn(tt + 1)
                dve.wait_ge(S("h_made"), tt + 1)
                v.tensor_tensor(htab[:, tt, :D], bank[2 + tt % 2][:, :D], vecs[:, 0, :], ALU.add).then_inc(S("h_read"), 1)
            dve.wait_ge(S("h_read"), NT)
            for c, dst in ((1, a1), (2, a2)):
                for t0 in range(0, NT, 5):
                    vb = vecs[:, c:c + 1, :].broadcast_to([P, 5, D])
                    st.run(v.tensor_tensor(dots, htab[:, t0:t0 + 5, :D], vb, ALU.mult))
                    st.run(v.tensor_reduce(dst[:, t0:t0 + 5], dots, X_AXIS, ALU.add))
            dve.sem_inc(S("dots_done"), 1)
            st.did(v.tensor_scalar(a1, a1, small[:, 320:321], None, ALU.add))
            st.run(v.tensor_scalar(a2, a2, small[:, 321:322], None, ALU.add))
            st.run(v.tensor_reduce(gmin[:, 0:1], a2, X_AXIS, ALU.min, negate=True))
            dve.sem_inc(S("gmin_part"), 1)
            st.did(v.tensor_scalar(winA, winbc[:, :TA], float(BKT_A - 1), None, ALU.min))
            rank(SORT[1])
            dve.wait_ge(S("gmin_all"), 1)
            st.did(v.tensor_scalar(a1, a1, gmin[:, 1:2], None, ALU.subtract))
            st.run(v.tensor_scalar(htab[:, :, D + 1], a2, gmin[:, 1:2], None, ALU.add))
            dve.sem_inc(S("htab_ready"), 1)
            st.run(v.memset(ta1, 0.0))
            for w in range(NT):
                st.run(v.tensor_scalar(tx, winA, float(w), a1[:, w:w + 1], ALU.is_equal, ALU.mult))
                st.run(v.tensor_tensor(ta1, ta1, tx, ALU.add))
            st.did(v.memset(tx[:, 0:1], 0.0))
            st.did(v.memset(ty[:, TA - 1:], 0.0))
            st.did(v.tensor_tensor(tx[:, 1:], winA[:, 1:], winA[:, :TA - 1], ALU.is_equal))
            st.did(v.tensor_tensor(ty[:, :TA - 1], winA[:, 1:], winA[:, :TA - 1], ALU.is_equal))
            st.did(v.memset(acc_mem[:, :(BKT_A + 1) * AC], 0.0))
            st.run(v.memset(stB_mem, 0.0))
            st.run(v.memset(stBb[:, :, :, 96:99], 1.0))

            def select(i, quads=4):
                def maxima(Q, h):
                    dve.wait_ge(S("v_turned"), Q + 1)
                    if not isinstance(Q, int):
                        dve.sem_inc(S("passed"), 1)
                    v.tensor_reduce(vmax[:, ds(Q * 4, 4)], bank[h].rearrange("p (k e) -> p k e", k=4), X_AXIS, ALU.max)\
                        .then_inc(S("v_maxed"), 1)
                for h in range(quads):
                    Q = 4 * i + h
                    dve.wait_ge(S(f"gathered{h}"), i * 64 + 64)
                    dve.wait_ge(S("gidx_staged"), Q + 1)
                    if due(Q - 1):
                        dve.wait_ge(S("v_turned"), Q - 1)
                    for k in range(4):
                        last = v.tensor_scalar(vsel[:, h % 2, k, :], iota, gseg[:, h, k:k + 1], pay[:, h, k, HC - 1:HC],
                                               ALU.is_equal, ALU.mult)
                    last.then_inc(S("v_ready"), 1)
                    v.tensor_scalar(recA[:, ds(Q * 4, 4), 0], pay[:, h, :, HC - 1], 0.0, None, ALU.add).then_inc(S("a2_kept"), 1)
                    if not (isinstance(i, int) and Q == 0):
                        maxima(Q - 1, (h - 1) % 2)
                if quads < 4:
                    maxima(TA // 4 - 1, 1)
            looped(dve, TA // 16, select)
            select(TA // 16, TA // 4 % 4)
            dve.wait_ge(S("v_maxed"), TA // 4)
            dve.wait_ge(S("a2_kept"), TA // 4)
            st.run(v.tensor_tensor_scan(tm, tx, vmax, 0.0, ALU.mult, ALU.max))
            st.run(v.tensor_tensor_scan(vmax[:, ::-1], ty[:, ::-1], tm[:, ::-1], 0.0, ALU.mult, ALU.max))
            st.run(v.tensor_tensor(tx, vmax, ta1, ALU.add))
            st.run(v.scalar_tensor_tensor(tm, tx, 0.01, tx, ALU.mult, ALU.max))
            for c, src in enumerate((ta1, tm)):
                st.run(v.tensor_copy(tbl[:, :, c, 0], src))
                st.run(v.tensor_tensor(src, src, tbl[:, :, c, 0], ALU.subtract))
                st.run(v.tensor_copy(tbl[:, :, c, 1], src))
                st.run(v.tensor_tensor(tbl[:, :, c, 2], src, tbl[:, :, c, 1], ALU.subtract))
            dve.sem_inc(S("tbl_ready"), 1)
            dve.sem_inc(S("stB_ready"), 1)

            def window_pair(Q, j, winp):
                return dve.value_load(winp[0:1, ds(Q * 2 + j, 1)])

            def flush(Q, k, pair, base, banks, summed, flushed, off):
                w = pair % base if k % 2 == 0 else pair // base
                if due(Q * 4 + k):
                    dve.wait_ge(flushed, off + Q * 4 + k)
                dve.wait_ge(summed, off + Q * 4 + k + 1)
                a_ = acc_mem[:, ds(w * AC, AC)]
                v.tensor_tensor(a_, a_, bank[banks + k][:, :AC], ALU.add).then_inc(flushed, 1)

            def flush_A(Q, k, pair):
                flush(Q, k, pair, BKT_A + 1, 3, S("att_summed"), S("flushed"), 0)

            def onehot(Q, h):
                if due(4 * Q - 12):
                    dve.wait_ge(S("att_summed"), 4 * Q - 12)
                v.tensor_tensor(seg1[:, h, :, :], iota.rearrange("p (a s) -> p a s", a=1).broadcast_to([P, 4, P]),
                                recA[:, ds(Q * 4, 4), 1:2].broadcast_to([P, 4, P]), ALU.is_equal)\
                    .then_inc(S("oneh_ready"), 1)

            def logit_parts(Q, h):
                dve.wait_ge(S("am_ready"), Q + 1)
                v.tensor_reduce(amv[:, h, 0:8], bank[2 + 5 * h][:, :24].rearrange("p (n s) -> p n s", s=3),
                                X_AXIS, ALU.add).then_inc(S("am_read"), 1)

            def logit_sum(Q, h):
                am = amv[:, h, 0:8].rearrange("p (k c) -> p k c", c=2)
                dve.wait_ge(S("am_read"), Q + 1)
                v.tensor_tensor(amv[:, h, 8:12], am[:, :, 0], recA[:, ds(Q * 4, 4), 0], ALU.add).then_inc(S("lin_step"), 1)

            def logit_leak(Q, h):
                dve.wait_ge(S("lin_step"), Q * 2 + 1)
                v.scalar_tensor_tensor(amv[:, h, 8:12], amv[:, h, 8:12], 0.01, amv[:, h, 8:12], ALU.mult, ALU.max)\
                    .then_inc(S("lin_step"), 1)

            def logit_less(Q, h):
                am = amv[:, h, 0:8].rearrange("p (k c) -> p k c", c=2)
                dve.wait_ge(S("lin_step"), Q * 2 + 2)
                v.tensor_tensor(amv[:, h, 12:16], amv[:, h, 8:12], am[:, :, 1], ALU.subtract).then_inc(S("logit_ready"), 1)

            def logit(Q, h):
                logit_parts(Q, h)
                logit_sum(Q, h)
                logit_leak(Q, h)
                logit_less(Q, h)

            def attr_low(Q, h):
                dve.wait_ge(S("act_stepB"), Q * 4 + 4)
                v.tensor_tensor(stBb[:, h, :, 64:96], attr_r, stBb[:, h, :, 32:64], ALU.subtract)\
                    .then_inc(S("attr_split"), 1)

            def attend(i):
                for h in range(4):
                    Q = 4 * i + h
                    first = isinstance(i, int) and Q == 0
                    if not first:
                        pair = window_pair(Q - 1, 0, winpA)
                        flush_A(Q - 1, 0, pair)
                    logit_parts(Q + 1, (h + 1) % 2)
                    if not (isinstance(i, int) and Q == EC // 4 - 1):
                        onehot(Q + 3, (h + 3) % 4)
                    logit_sum(Q + 1, (h + 1) % 2)
                    if not first:
                        flush_A(Q - 1, 1, pair)
                    logit_leak(Q + 1, (h + 1) % 2)
                    if not first:
                        pair = window_pair(Q - 1, 1, winpA)
                    logit_less(Q + 1, (h + 1) % 2)
                    if not first:
                        flush_A(Q - 1, 2, pair)
                        attr_low(Q - 1, (h - 1) % 4)
                        flush_A(Q - 1, 3, pair)
                    if due(Q):
                        dve.wait_ge(S("attr_split"), Q)
                    dve.wait_ge(S("attr_hi"), Q + 1)
                    v.tensor_tensor(attr_r, attr_in[:, h % 2, :, :], stBb[:, h, :, 0:32], ALU.subtract)\
                        .then_inc(S("attr_rest"), 1)
            for q in range(3):
                onehot(q, q)
            logit(0, 0)
            looped(dve, EC // 16, attend)
            attr_low(EC // 4 - 1, 3)
            for q in (TA // 4 - 3, TA // 4 - 2, TA // 4 - 1):
                for k in range(4):
                    flush_A(q, k, window_pair(q, k // 2, winpA))
                if q == TA // 4 - 3:
                    logit(TA // 4 - 1, 1)
            dve.wait_ge(S("flushed"), TA)
            st.run(v.tensor_scalar(rs, acc[:, 0:NT, D], 0.0, None, ALU.is_equal))
            st.run(v.tensor_tensor(rs, rs, acc[:, 0:NT, D], ALU.add))
            st.run(v.reciprocal(rs, rs))
            for tt in range(NT):
                st.did(v.scalar_tensor_tensor(x_sb[:, tt, :], acc[:, tt, :D], rs[:, tt:tt + 1], x_sb[:, tt, :],
                                              ALU.mult, ALU.add))
            st.settle()
            dve.sem_inc(S("x1_ready"), 1)

            def token_tile(n, tt):
                dve.wait_ge(S("tok_done"), n * NT + tt + 1)
                y = ycol[:, tt % 2, :]
                v.tensor_tensor(y, bank[4 + tt % 4][:, :D], vecs[:, 1, :], ALU.add).then_inc(S("tok_added"), 1)
                dve.wait_ge(S("tok_added"), n * NT + tt + 1)
                return y

            layer_norm(2, xn, "xn2_ready", group=5)
            dve.wait_ge(S("mod_v_loaded"), 48)
            for t0 in range(0, NT, 5):
                st.run(v.tensor_tensor(dots, xn[:, t0:t0 + 5, :], vecs[:, 0:1, :].broadcast_to([P, 5, D]), ALU.mult))
                st.run(v.tensor_reduce(tok_w[:, t0:t0 + 5], dots, X_AXIS, ALU.add))
            st.did(v.tensor_scalar(real, iota_col, float(LAST), None, ALU.is_lt))
            st.did(v.tensor_scalar(low, iota, iota_col, None, ALU.is_lt))
            st.run(v.tensor_scalar(tok_w, tok_w, br_sb, None, ALU.add))
            st.run(v.tensor_scalar(tok_w[:, NT - 1:], tok_w[:, NT - 1:], real, None, ALU.mult))
            st.run(v.tensor_scalar(coef[:, 0:1], real, -1.0, 3.0e38, ALU.add, ALU.mult))
            st.run(v.tensor_tensor(tok_w[:, NT - 1:], tok_w[:, NT - 1:], coef[:, 0:1], ALU.add))
            dve.sem_inc(S("router_ready"), 1)
            dve.wait_ge(S("router_pe"), 1)
            st.run(v.tensor_copy(w_turn[:NT, :], bank[7][:NT, :P]))
            dve.sem_inc(S("router_turned"), 1)
            dve.wait_ge(S("router_row"), 16)
            st.run(v.memset(n_gt, 0.0))
            for tt in range(NT):
                w_ = tok_w[:, tt:tt + 1]
                for c, (lo_, n_, op) in enumerate(((0, tt * P, ALU.is_ge), (tt * P, NP_ - tt * P, ALU.is_gt))):
                    if n_:
                        st.run(v.scalar_tensor_tensor(seen[:, :n_], w_row[:, lo_:lo_ + n_], w_, ones[:, 0:1].broadcast_to([P, n_]),
                                                      op, ALU.mult, accum_out=n_gt[:, c, tt:tt + 1]))
                st.run(v.scalar_tensor_tensor(seen[:, :P], w_row[:, tt * P:(tt + 1) * P], w_, low, ALU.is_equal, ALU.mult,
                                              accum_out=n_gt[:, 2, tt:tt + 1]))
                cf = coef[:, tt:tt + 1]
                st.run(v.tensor_tensor(cf, n_gt[:, 0, tt:tt + 1], n_gt[:, 1, tt:tt + 1], ALU.add))
                st.run(v.tensor_tensor(cf, cf, n_gt[:, 2, tt:tt + 1], ALU.add))
                st.run(v.scalar_tensor_tensor(cf, cf, float(TOPK), w_, ALU.is_lt, ALU.mult))
                y = token_tile(0, tt)
                st.run(v.scalar_tensor_tensor(y, y, cf, xn[:, tt, :], ALU.mult, ALU.add))
                st.run(v.tensor_tensor(x_sb[:, tt, :], x_sb[:, tt, :], y, ALU.add))
                norm_stats(x_sb, tt)
            st.settle()
            dve.sem_inc(S("x2_ready"), 1)
            dve.wait_ge(S("edge_w_loaded"), 64)
            st.run(v.tensor_copy(we[:KA, 0, :], we_f[:KA, :]))
            st.run(v.tensor_tensor(we_r[:KA, :], we_f[:KA, :], we[:KA, 0, :], ALU.subtract))
            st.run(v.tensor_copy(we[:KA, 1, :], we_r[:KA, :]))
            st.run(v.tensor_tensor(we[:KA, 2, :], we_r[:KA, :], we[:KA, 1, :], ALU.subtract))
            for c in range(2):
                msk = small[:, 0:1]
                st.run(v.tensor_scalar(msk, iota_col, float(97 + c), None, ALU.is_equal))
                st.run(v.tensor_scalar(we_r[:KA, :], we[:KA, 1 + c, :], msk[:KA], None, ALU.mult))
                st.run(v.tensor_scalar(msk, iota_col, float(97 + c), None, ALU.not_equal))
                st.run(v.scalar_tensor_tensor(we[:KA, 0, :], we[:KA, 0, :], msk[:KA], we_r[:KA, :], ALU.mult, ALU.add))
            st.did(v.memset(msg[:, :, :, D:AC], 1.0))
            dve.wait_ge(S("acc_zeroed"), 1)
            st.settle()
            dve.sem_inc(S("edge_w_ready"), 1)
            layer_norm(3, xn, "state_ready", stats_made=True, group=5)
            for l in range(LAYERS):
                if l:
                    dve.wait_ge(S("flat_ready"), (l - 1) * NT + NT)
                    st.did(v.memset(acc_mem[:, 38 * AC:], 0.0))
                    dve.wait_ge(S("acc_half"), l - 1 + 1)
                    st.settle()

                def flush_B(Q, k, pair):
                    flush(Q, k, pair, BKT_B + 1, 4, S("summed"), S("flushed_b"), l * TB)

                def compare(Q, h, n):
                    if due(4 * Q - 4):
                        dve.wait_ge(S("summed"), l * TB + 4 * Q - 4)
                    dve.wait_ge(S(f"rec_loaded{h}"), l * 16 * turns(h) + n * 16 + 16)
                    v.tensor_tensor(oneh[:, h % 2, :, :], iota.rearrange("p (a s) -> p a s", a=1).broadcast_to([P, 4, P]),
                                    rec[:, h, :, W_SEG:W_SEG + 1].broadcast_to([P, 4, P]), ALU.is_equal)\
                        .then_inc(S("seg_ready"), 1)

                def multiply(Q, h, j, i):
                    dve.wait_ge(S(f"sources{h}"), l * 64 * turns(h) + i * 64 + 64)
                    dve.wait_ge(S("projected"), l * 2 * QB + 2 * Q + j + 1)
                    if due(4 * Q - 4):
                        dve.wait_ge(S("summed"), l * TB + 4 * Q - 4)
                    v.tensor_tensor(msg[:, h % 2, 2 * j:2 * j + 2, :D], bank[2 + j].rearrange("p (k d) -> p k d", k=2),
                                    xg[:, h, 2 * j:2 * j + 2, :], ALU.mult).then_inc(S("multiplied"), 1)

                def edges(i, quads=4):
                    for h in range(quads):
                        Q = 4 * i + h
                        first = isinstance(i, int) and Q == 0
                        multiply(Q, h, 0, i)
                        if not first:
                            pair = window_pair(Q - 1, 0, winpB)
                            flush_B(Q - 1, 0, pair)
                        multiply(Q, h, 1, i)
                        if not first:
                            flush_B(Q - 1, 1, pair)
                        compare(Q, h, i)
                        if not first:
                            pair = window_pair(Q - 1, 1, winpB)
                            flush_B(Q - 1, 2, pair)
                            flush_B(Q - 1, 3, pair)
                looped(dve, TB // 16, edges)
                edges(TB // 16, TB // 4 % 4)
                for k in range(4):
                    flush_B(TB // 4 - 1, k, window_pair(TB // 4 - 1, k // 2, winpB))
                dve.wait_ge(S("flushed_b"), l * TB + TB)
                if l == 0:
                    st.run(v.tensor_scalar(inv, acc[:, 0:BKT_B, D], 1.0, None, ALU.max))
                    st.run(v.reciprocal(inv, inv))
                dve.sem_inc(S("inv_ready"), 1)

                def copy_turned(tt, h):
                    if due(tt - 1):
                        dve.wait_ge(S("applied"), l * NT + tt - 1)
                    for b in range(2):
                        dve.wait_ge(S("flat_turned"), l * 2 * NT + 2 * tt + b + 1)
                        v.tensor_copy(turned[:, h, b * 512:(b + 1) * 512], bank[2 * h + b]).then_inc(S("turn_copied"), 1)

                def update(tt, h):
                    dve.wait_ge(S("applied"), l * NT + tt + 1)
                    xx = xn_mem[:, ds(tt * D, D)]
                    if due(tt):
                        dve.wait_ge(S("updated"), l * NT + tt)
                    v.tensor_tensor(biased, bank[4 + h][:, :D], vecs[:, l, :], ALU.add).then_inc(S("biased"), 1)
                    dve.wait_ge(S("biased"), l * NT + tt + 1)
                    v.scalar_tensor_tensor(xx, biased, 0.0, xx, ALU.max, ALU.add).then_inc(S("updated"), 1)

                def finish(tt):
                    dve.wait_ge(S("updated"), l * NT + tt + 1)
                    if tt == NT - 1:
                        st.run(v.tensor_scalar(xn[:, tt, :], xn[:, tt, :], real, None, ALU.mult))
                    st.run(v.tensor_tensor(x_sb[:, tt, :], x_sb[:, tt, :], xn[:, tt, :], ALU.add))
                    norm_stats(x_sb, tt)
                if l == LAYERS - 1:
                    copy_turned(0, 0)
                    for tt in range(NT):
                        if tt + 1 < NT:
                            copy_turned(tt + 1, (tt + 1) % 2)
                        update(tt, tt % 2)
                        finish(tt)
                    continue
                copy_turned(0, 0)
                copy_turned(1, 1)
                update(0, 0)
                with dve.Fori(1, NT // 2) as i:
                    copy_turned(2 * i, 0)
                    update(2 * i - 1, 1)
                    copy_turned(2 * i + 1, 1)
                    update(2 * i, 0)
                copy_turned(NT - 1, 0)
                update(NT - 2, 1)
                update(NT - 1, 0)
                dve.wait_ge(S("updated"), l * NT + NT)
            st.settle()
            dve.sem_inc(S("x3_ready"), 1)
            layer_norm(4, xn, "xn4_ready", stats_made=True, group=5)
            dve.wait_ge(S("gate_w_loaded"), 32)
            dve.wait_ge(S("xt_copied"), NT + NT)
            for k in range(2):
                st.run(v.tensor_reduce(small[:, 490 + k:491 + k], xt[:, k, :N], X_AXIS, ALU.add))
            st.run(v.tensor_scalar(small[:, 490:492], small[:, 490:492], 1.0 / N, None, ALU.mult))
            dve.sem_inc(S("mean_ready"), 1)
            dve.wait_ge(S("logits_made"), 1)
            G = lambda a_, b_: gate[0:1, a_:b_]
            row8 = iota[0:1, 0:8]

            def softmax(dst, n):
                st.run(v.tensor_reduce(G(60, 61), dst, X_AXIS, ALU.max))
                st.run(v.tensor_scalar(dst, dst, G(60, 61), None, ALU.subtract))
                dve.sem_inc(S("gate_exp"), 1)
                if due(n):
                    dve.wait_ge(S("gate_exp_done"), n)
                st.run(v.tensor_reduce(G(60, 61), dst, X_AXIS, ALU.add))
                st.run(v.reciprocal(G(60, 61), G(60, 61)))
                st.run(v.tensor_scalar(dst, dst, G(60, 61), None, ALU.mult))
            st.run(v.tensor_tensor(G(8, 16), bank[6][0:1, 0:8], G(0, 8), ALU.add))
            softmax(G(8, 16), 1)
            capacity = float(math.ceil(N * 1.25 / NE))
            st.run(v.tensor_scalar(G(16, 24), G(8, 16), float(N), 1e-30, ALU.mult, ALU.max))
            st.run(v.reciprocal(G(16, 24), G(16, 24)))
            st.run(v.tensor_scalar(G(16, 24), G(16, 24), capacity, 1.0, ALU.mult, ALU.min))
            st.run(v.tensor_tensor(G(24, 32), G(8, 16), G(16, 24), ALU.mult))
            softmax(G(24, 32), 2)
            for c in range(2):
                st.run(v.tensor_reduce(G(48 + c, 49 + c), G(24, 32), X_AXIS, ALU.max))
                st.run(v.tensor_scalar(G(32, 40), G(24, 32), G(48 + c, 49 + c), -100.0, ALU.is_equal, ALU.mult))
                st.run(v.tensor_tensor(G(32, 40), G(32, 40), row8, ALU.add))
                st.run(v.tensor_reduce(G(50 + c, 51 + c), G(32, 40), X_AXIS, ALU.min))
                st.run(v.tensor_scalar(G(50 + c, 51 + c), G(50 + c, 51 + c), 100.0, None, ALU.add))
                st.run(v.tensor_scalar(G(32, 40), row8, G(50 + c, 51 + c), -10.0, ALU.is_equal, ALU.mult))
                st.run(v.tensor_tensor(G(24, 32), G(24, 32), G(32, 40), ALU.add))
            st.run(v.tensor_copy(G(62, 64).bitcast(INT32), G(50, 52)))
            dve.sem_inc(S("chosen"), 1)
            st.run(v.tensor_tensor(G(40, 41), G(49, 50), G(48, 49), ALU.subtract))
            dve.sem_inc(S("gate_exp"), 1)
            dve.wait_ge(S("gate_exp_done"), 3)
            st.run(v.tensor_scalar(G(41, 42), G(40, 41), 1.0, None, ALU.add))
            st.run(v.reciprocal(G(56, 57), G(41, 42)))
            st.run(v.tensor_tensor(G(57, 58), G(40, 41), G(56, 57), ALU.mult))
            dve.sem_inc(S("top_ready"), 1)
            dve.wait_ge(S("top_spread"), 1)
            st.run(v.tensor_copy(small[:, 494:496], bank[5][:, 0:2]))
            dve.wait_ge(S("moe_w_loaded"), 128)
            for c in range(2):
                st.did(v.tensor_scalar(w2_sb[:, 4 * c:4 * c + 4, :], w2_sb[:, 4 * c:4 * c + 4, :], small[:, 494 + c:495 + c],
                                       None, ALU.mult))
            st.run(v.tensor_scalar(vecs[:, 0, :], vecs[:, 0, :], small[:, 494:495], None, ALU.mult))
            st.run(v.scalar_tensor_tensor(vecs[:, 1, :], vecs[:, 1, :], small[:, 495:496], vecs[:, 0, :], ALU.mult, ALU.add))
            dve.sem_inc(S("moe_w_scaled"), 1)

            dve.wait_ge(S("norm_w_loaded"), 32)
            for tt in range(NT):
                st.run(v.tensor_tensor(x_sb[:, tt, :], x_sb[:, tt, :], vecs[:, 3, :], ALU.add))
                y = token_tile(1, tt)
                st.run(v.tensor_tensor(xn[:, tt, :], xn[:, tt, :], y, ALU.add))
                norm_stats(xn, tt)

            def scaled(t0):
                xx = xn[:, t0:t0 + 5, :]
                st.run(v.tensor_tensor(xx, xx, vecs[:, 2:3, :].broadcast_to([P, 5, D]), ALU.mult))
                st.run(v.tensor_tensor(x_sb[:, t0:t0 + 5, :], x_sb[:, t0:t0 + 5, :], xx, ALU.add))
            layer_norm(5, xn, "out_ready", src=xn, stats_made=True, group=5, then=scaled)


INPUTS = ["x", "src", "dst", "edge_attr_32", "edge_type_3", "L0_gnn_b_layer", "L0_gnn_w_a1", "L0_gnn_b_a1",
          "L0_gnn_w_a2", "L0_gnn_b_a2", "L0_ffn_br", "L0_ffn_w1", "L0_ffn_w2", "L0_ffn_b2", "L1_gnn_weights",
          "L1_gnn_roots", "L1_gnn_biases", "L1_gnn_edge_w", "L1_gnn_edge_b", "L1_ffn_Wr", "L1_ffn_br", "L1_ffn_W1",
          "L1_ffn_W2", "L1_ffn_b2", "L1_ffn_gamma", "L1_ffn_beta"]


def laid_out(inputs):
    import numpy as np
    a = {name: np.ascontiguousarray(inputs[name]) for name in INPUTS}
    for name in ("L0_gnn_w_a1", "L0_gnn_w_a2"):
        a[name] = a[name].reshape(D)
    a["W_layer_t"] = np.ascontiguousarray(np.asarray(inputs["L0_gnn_W_layer"]).T)
    a["wr_mod"] = np.asarray(inputs["L0_ffn_wr"]).reshape(D)
    a["b1_mod"] = np.ascontiguousarray(np.asarray(inputs["L0_ffn_b1"]).reshape(HID // P, P).T)
    a["b1_moe"] = np.ascontiguousarray(np.asarray(inputs["L1_ffn_b1"]).reshape(NE, FE // P, P).transpose(0, 2, 1))
    return a


def kernel(**inputs):
    import concourse.bacc as bacc
    from concourse.bass_utils import run_bass_kernel_spmd

    nc = bacc.Bacc("TRN2", target_bir_lowering=False, num_devices=1)
    arrays = {f"in_{name}": a for name, a in laid_out(inputs).items()}
    t = {name[3:]: nc.dram_tensor(name, a.shape, mybir.dt.from_np(a.dtype), kind="ExternalInput").ap()
         for name, a in arrays.items()}
    out = nc.dram_tensor("out_0", (N, D), FP32, kind="ExternalOutput").ap()
    build(nc, t, out)
    r = run_bass_kernel_spmd(nc, [arrays], core_ids=[0])
    return r.results[0]["out_0"]
```
